# Optimizing a Trainium2 kernel written in Bass

```python
import numpy as np
import jax
import jax.numpy as jnp

def _softmax(x, axis=-1):
    return jax.nn.softmax(x, axis=axis)

def _gelu(x):
    return jax.nn.gelu(x, approximate=True)

def _silu(x):
    return jax.nn.silu(x)

def _sigmoid(x):
    return jax.nn.sigmoid(x)

def _layernorm(x, axis=-1, eps=1e-05):
    m = jnp.mean(x, axis=axis, keepdims=True)
    v = jnp.var(x, axis=axis, keepdims=True)
    return (x - m) / jnp.sqrt(v + eps)

def _scatter_add(tgt, idx, src, axis=0):
    return tgt.at[idx].add(src)

def _segment_sum(src, seg, n):
    return jax.ops.segment_sum(src, seg, n)
kernel_name = 'mk_xattn_ffn_d2_seqx_r4_020f58'

def setup_inputs(seed: int=0):
    np.random.seed(seed)
    _w = jnp.asarray

    def _rec_inputs():
        import jax
        import jax.numpy as jnp
        _rk = jax.random.key(seed)
        x = -7.109e-05 + 0.9999 * jax.random.normal(jax.random.fold_in(_rk, 1), (4, 512, 512), jnp.float32)
        _lenS = 512 - jax.random.randint(jax.random.fold_in(_rk, 7), (4,), 0, max(1, 512 // 4) + 1, jnp.int32)
        _lenS2 = 512 - jax.random.randint(jax.random.fold_in(_rk, 8), (4,), 0, max(1, 512 // 4) + 1, jnp.int32)
        _ctx_512P = jax.random.normal(jax.random.fold_in(_rk, 11), (4, 16, 128), jnp.float32)
        _ctx_512c = jax.random.dirichlet(jax.random.fold_in(_rk, 511), 0.3 * jnp.ones((16,), jnp.float32), (4, 512))
        _ctx_512t = jnp.einsum('bsk,bkd->bsd', _ctx_512c, _ctx_512P)
        _ctx_512t = _ctx_512t * jax.lax.rsqrt(jnp.mean(jnp.square(_ctx_512t)) + 1e-12) * 0.953939
        ctx_512 = 2.81802e-05 + 1.00001 * (_ctx_512t + 0.3 * jax.random.normal(jax.random.fold_in(_rk, 611), (4, 512, 128), jnp.float32))
        return (x, ctx_512)
    x, ctx_512 = _rec_inputs()

    def _L0_xattn_setup():
        import jax, jax.numpy as jnp
        import numpy as np
        EPS = 1e-06
        IMAGE_DIMS = 512
        key = jax.random.key(seed)
        k1, k2, k3 = jax.random.split(key, 3)
        B, I, J, D = (16, 512, 512, 128)
        p = jax.random.normal(k1, (B, I, J), dtype=jnp.float32)
        k_v = jax.random.normal(k2, (B, J, D), dtype=jnp.float32)
        W_k = jax.random.normal(k3, (D, D), dtype=jnp.float32) * (1.0 / np.sqrt(D))
        b_k = jnp.zeros((D,), dtype=jnp.float32)
        ln_gamma = jnp.ones((J,), dtype=jnp.float32)
        ln_beta = jnp.zeros((J,), dtype=jnp.float32)
        return {'p': p, 'k_v': k_v, 'W_k': W_k, 'b_k': b_k, 'ln_gamma': ln_gamma, 'ln_beta': ln_beta}
    _L0_xattn_all = _L0_xattn_setup()
    _L0_xattn_in = {k: v for k, v in _L0_xattn_all.items() if k in ('W_k', 'b_k', 'ln_gamma', 'ln_beta')}
    del _L0_xattn_all

    def _L0_ffn_setup():
        import jax, jax.numpy as jnp
        import numpy as np
        H = 512
        I = 2048
        MI = 256
        E = 8
        K = 2
        B, S = (2, 256)
        EPS = 1e-06
        ROOT = H ** (-0.5)

        def _rms(x, w=None, eps=EPS):
            ms = jnp.mean(x * x, axis=-1, keepdims=True) + eps
            y = x * jax.lax.rsqrt(ms)
            return y * w if w is not None else y

        def _gelu_tanh(x):
            return jax.nn.gelu(x, approximate=True)
        key = jax.random.key(seed)
        ks = jax.random.split(key, 10)
        s = 0.02
        return {'hidden_states': jax.random.normal(ks[0], (B, S, H), jnp.float32), 'rn_pre1': jnp.ones((H,), jnp.float32), 'rn_pre2': jnp.ones((H,), jnp.float32), 'rn_post1': jnp.ones((H,), jnp.float32), 'rn_post2': jnp.ones((H,), jnp.float32), 'rn_post': jnp.ones((H,), jnp.float32), 'w_gate': jax.random.normal(ks[1], (H, I), jnp.float32) * s, 'w_up': jax.random.normal(ks[2], (H, I), jnp.float32) * s, 'w_down': jax.random.normal(ks[3], (I, H), jnp.float32) * s, 'router_w': jax.random.normal(ks[4], (H, E), jnp.float32) * s, 'router_scale': jnp.ones((H,), jnp.float32), 'per_expert_scale': jnp.ones((E,), jnp.float32), 'we_gate': jax.random.normal(ks[5], (E, H, MI), jnp.float32) * s, 'we_up': jax.random.normal(ks[6], (E, H, MI), jnp.float32) * s, 'we_down': jax.random.normal(ks[7], (E, MI, H), jnp.float32) * s}
    _L0_ffn_all = _L0_ffn_setup()
    _L0_ffn_in = {k: v for k, v in _L0_ffn_all.items() if k in ('rn_pre1', 'rn_pre2', 'rn_post1', 'rn_post2', 'rn_post', 'w_gate', 'w_up', 'w_down', 'router_w', 'router_scale', 'per_expert_scale', 'we_gate', 'we_up', 'we_down')}
    del _L0_ffn_all

    def _L1_xattn_setup():
        import jax, jax.numpy as jnp
        import numpy as np
        N_HEADS = 16
        N_KV_HEADS = 4
        ROPE_THETA = 10000.0
        EPS = 1e-05

        def _rms_norm(x, w):
            var = jnp.mean(x * x, axis=-1, keepdims=True)
            return x * jax.lax.rsqrt(var + EPS) * w

        def _rope_sin_cos(T, head_dim, dtype):
            inv_freq = 1.0 / ROPE_THETA ** (jnp.arange(0, head_dim, 2, dtype=jnp.float32) / head_dim)
            t = jnp.arange(T, dtype=jnp.float32)
            freqs = jnp.outer(t, inv_freq)
            emb = jnp.concatenate([freqs, freqs], -1)
            return (jnp.sin(emb).astype(dtype)[None, None], jnp.cos(emb).astype(dtype)[None, None])

        def _rotate_half(x):
            h = x.shape[-1] // 2
            x1, x2 = (x[..., :h], x[..., h:])
            return jnp.concatenate([-x2, x1], axis=-1)
        key = jax.random.key(seed)
        ks = jax.random.split(key, 6)
        B, T, C = (2, 512, 512)
        Ckv = C // N_HEADS * N_KV_HEADS
        return {'q': jax.random.normal(ks[0], (B, T, C), jnp.float32), 'k': jax.random.normal(ks[1], (B, T, Ckv), jnp.float32), 'v': jax.random.normal(ks[2], (B, T, Ckv), jnp.float32), 'q_norm_w': jnp.ones((C,), jnp.float32), 'k_norm_w': jnp.ones((Ckv,), jnp.float32), 'w_out': jax.random.normal(ks[3], (C, C), jnp.float32) * C ** (-0.5)}
    _L1_xattn_all = _L1_xattn_setup()
    _L1_xattn_in = {k: v for k, v in _L1_xattn_all.items() if k in ('q_norm_w', 'k_norm_w', 'w_out')}
    del _L1_xattn_all

    def _L1_ffn_setup():
        import jax, jax.numpy as jnp
        import numpy as np
        DIM_IN = 512
        DIM_HIDDEN = 2048
        key = jax.random.key(seed)
        k_x, k_g, k_u, k_d = jax.random.split(key, 4)
        s_in = 1.0 / np.sqrt(DIM_IN)
        s_hid = 1.0 / np.sqrt(DIM_HIDDEN)
        x = jax.random.normal(k_x, (4, 512, DIM_IN), dtype=jnp.float32)
        w_gate = jax.random.uniform(k_g, (DIM_HIDDEN, DIM_IN), jnp.float32, -s_in, s_in)
        w_up = jax.random.uniform(k_u, (DIM_HIDDEN, DIM_IN), jnp.float32, -s_in, s_in)
        w_down = jax.random.uniform(k_d, (DIM_IN, DIM_HIDDEN), jnp.float32, -s_hid, s_hid)
        return {'x': x, 'w_gate': w_gate, 'w_up': w_up, 'w_down': w_down}
    _L1_ffn_all = _L1_ffn_setup()
    _L1_ffn_in = {k: v for k, v in _L1_ffn_all.items() if k in ('w_gate', 'w_up', 'w_down')}
    del _L1_ffn_all
    return {'x': x, 'ctx_512': ctx_512, 'L0_xattn_W_k': _L0_xattn_in['W_k'], 'L0_xattn_b_k': _L0_xattn_in['b_k'], 'L0_xattn_ln_gamma': _L0_xattn_in['ln_gamma'], 'L0_xattn_ln_beta': _L0_xattn_in['ln_beta'], 'L0_ffn_rn_pre1': _L0_ffn_in['rn_pre1'], 'L0_ffn_rn_pre2': _L0_ffn_in['rn_pre2'], 'L0_ffn_rn_post1': _L0_ffn_in['rn_post1'], 'L0_ffn_rn_post2': _L0_ffn_in['rn_post2'], 'L0_ffn_rn_post': _L0_ffn_in['rn_post'], 'L0_ffn_w_gate': _L0_ffn_in['w_gate'], 'L0_ffn_w_up': _L0_ffn_in['w_up'], 'L0_ffn_w_down': _L0_ffn_in['w_down'], 'L0_ffn_router_w': _L0_ffn_in['router_w'], 'L0_ffn_router_scale': _L0_ffn_in['router_scale'], 'L0_ffn_per_expert_scale': _L0_ffn_in['per_expert_scale'], 'L0_ffn_we_gate': _L0_ffn_in['we_gate'], 'L0_ffn_we_up': _L0_ffn_in['we_up'], 'L0_ffn_we_down': _L0_ffn_in['we_down'], 'L1_xattn_q_norm_w': _L1_xattn_in['q_norm_w'], 'L1_xattn_k_norm_w': _L1_xattn_in['k_norm_w'], 'L1_xattn_w_out': _L1_xattn_in['w_out'], 'L1_ffn_w_gate': _L1_ffn_in['w_gate'], 'L1_ffn_w_up': _L1_ffn_in['w_up'], 'L1_ffn_w_down': _L1_ffn_in['w_down']}

def reference(x, ctx_512, L0_xattn_W_k, L0_xattn_b_k, L0_xattn_ln_gamma, L0_xattn_ln_beta, L0_ffn_rn_pre1, L0_ffn_rn_pre2, L0_ffn_rn_post1, L0_ffn_rn_post2, L0_ffn_rn_post, L0_ffn_w_gate, L0_ffn_w_up, L0_ffn_w_down, L0_ffn_router_w, L0_ffn_router_scale, L0_ffn_per_expert_scale, L0_ffn_we_gate, L0_ffn_we_up, L0_ffn_we_down, L1_xattn_q_norm_w, L1_xattn_k_norm_w, L1_xattn_w_out, L1_ffn_w_gate, L1_ffn_w_up, L1_ffn_w_down):
    import jax
    import jax.numpy as jnp

    def _L0_xattn_ref(p, k_v, W_k, b_k, ln_gamma, ln_beta):
        import jax, jax.numpy as jnp
        import numpy as np
        EPS = 1e-06
        IMAGE_DIMS = 512
        kv = k_v @ W_k.T + b_k
        out = jnp.einsum('bij,bjd->bid', p, kv)
        scale = IMAGE_DIMS ** (-0.5)
        sim = jnp.einsum('bid,bjd->bij', out, kv) * scale
        mu = jnp.mean(sim, axis=-1, keepdims=True)
        var = jnp.var(sim, axis=-1, keepdims=True)
        sim = (sim - mu) * jax.lax.rsqrt(var + EPS) * ln_gamma + ln_beta
        attn = jax.nn.softmax(sim, axis=-1)
        return attn

    def _L0_ffn_ref(hidden_states, rn_pre1, rn_pre2, rn_post1, rn_post2, rn_post, w_gate, w_up, w_down, router_w, router_scale, per_expert_scale, we_gate, we_up, we_down):
        import jax, jax.numpy as jnp
        import numpy as np
        H = 512
        I = 2048
        MI = 256
        E = 8
        K = 2
        B, S = (2, 256)
        EPS = 1e-06
        ROOT = H ** (-0.5)

        def _rms(x, w=None, eps=EPS):
            ms = jnp.mean(x * x, axis=-1, keepdims=True) + eps
            y = x * jax.lax.rsqrt(ms)
            return y * w if w is not None else y

        def _gelu_tanh(x):
            return jax.nn.gelu(x, approximate=True)
        b, s, h = hidden_states.shape
        T = b * s
        dense_in = _rms(hidden_states, rn_pre1)
        dense_out = _gelu_tanh(dense_in @ w_gate) * (dense_in @ w_up) @ w_down
        dense_out = _rms(dense_out, rn_post1)
        x = hidden_states.reshape(T, h)
        xr = _rms(x) * router_scale * ROOT
        router_logits = xr @ router_w
        probs = jax.nn.softmax(router_logits, axis=-1)
        top_w, top_i = jax.lax.top_k(probs, K)
        top_w = top_w / jnp.sum(top_w, axis=-1, keepdims=True)
        top_w = top_w * per_expert_scale[top_i]
        aff = jnp.zeros((T, E), x.dtype).at[jnp.arange(T)[:, None], top_i].set(top_w)
        moe_in = _rms(hidden_states, rn_pre2).reshape(T, h)
        g = jnp.einsum('th,ehm->tem', moe_in, we_gate)
        u = jnp.einsum('th,ehm->tem', moe_in, we_up)
        eo = jnp.einsum('tem,emh->teh', _gelu_tanh(g) * u, we_down)
        moe_out = jnp.einsum('te,teh->th', aff, eo).reshape(b, s, h)
        moe_out = _rms(moe_out, rn_post2)
        return _rms(dense_out + moe_out, rn_post)

    def _L1_xattn_ref(q, k, v, q_norm_w, k_norm_w, w_out):
        import jax, jax.numpy as jnp
        import numpy as np
        N_HEADS = 16
        N_KV_HEADS = 4
        ROPE_THETA = 10000.0
        EPS = 1e-05

        def _rms_norm(x, w):
            var = jnp.mean(x * x, axis=-1, keepdims=True)
            return x * jax.lax.rsqrt(var + EPS) * w

        def _rope_sin_cos(T, head_dim, dtype):
            inv_freq = 1.0 / ROPE_THETA ** (jnp.arange(0, head_dim, 2, dtype=jnp.float32) / head_dim)
            t = jnp.arange(T, dtype=jnp.float32)
            freqs = jnp.outer(t, inv_freq)
            emb = jnp.concatenate([freqs, freqs], -1)
            return (jnp.sin(emb).astype(dtype)[None, None], jnp.cos(emb).astype(dtype)[None, None])

        def _rotate_half(x):
            h = x.shape[-1] // 2
            x1, x2 = (x[..., :h], x[..., h:])
            return jnp.concatenate([-x2, x1], axis=-1)
        B, T, C = q.shape
        hd = C // N_HEADS
        g = N_HEADS // N_KV_HEADS
        q = _rms_norm(q, q_norm_w)
        k = _rms_norm(k, k_norm_w)
        q = q.reshape(B, T, N_HEADS, hd).transpose(0, 2, 1, 3)
        k = k.reshape(B, T, N_KV_HEADS, hd).transpose(0, 2, 1, 3)
        v = v.reshape(B, T, N_KV_HEADS, hd).transpose(0, 2, 1, 3)
        sin, cos = _rope_sin_cos(T, hd, q.dtype)
        q = q * cos + _rotate_half(q) * sin
        k = k * cos + _rotate_half(k) * sin
        qg = q.reshape(B, N_KV_HEADS, g, T, hd)
        scale = 1.0 / jnp.sqrt(jnp.asarray(hd, q.dtype))
        scores = jnp.einsum('bgnqd,bgkd->bgnqk', qg, k) * scale
        causal = jnp.tril(jnp.ones((T, T), bool))
        scores = jnp.where(causal, scores, jnp.asarray(-1e+30, scores.dtype))
        attn = jax.nn.softmax(scores, axis=-1)
        out = jnp.einsum('bgnqk,bgkd->bgnqd', attn, v)
        out = out.reshape(B, N_HEADS, T, hd).transpose(0, 2, 1, 3).reshape(B, T, C)
        return out @ w_out.T

    def _L1_ffn_ref(x, w_gate, w_up, w_down):
        import jax, jax.numpy as jnp
        import numpy as np
        DIM_IN = 512
        DIM_HIDDEN = 2048
        gate = jnp.einsum('bsd,hd->bsh', x, w_gate)
        up = jnp.einsum('bsd,hd->bsh', x, w_up)
        gated = jax.nn.silu(gate) * up
        return jnp.einsum('bsh,dh->bsd', gated, w_down)
    x = x + _L0_xattn_ref(_layernorm(x, axis=-1), ctx_512, L0_xattn_W_k, L0_xattn_b_k, L0_xattn_ln_gamma, L0_xattn_ln_beta)
    x = x + _L0_ffn_ref(_layernorm(x, axis=-1), L0_ffn_rn_pre1, L0_ffn_rn_pre2, L0_ffn_rn_post1, L0_ffn_rn_post2, L0_ffn_rn_post, L0_ffn_w_gate, L0_ffn_w_up, L0_ffn_w_down, L0_ffn_router_w, L0_ffn_router_scale, L0_ffn_per_expert_scale, L0_ffn_we_gate, L0_ffn_we_up, L0_ffn_we_down)
    x = x + _L1_xattn_ref(_layernorm(x, axis=-1), ctx_512, ctx_512, L1_xattn_q_norm_w, L1_xattn_k_norm_w, L1_xattn_w_out)
    x = x + _L1_ffn_ref(_layernorm(x, axis=-1), L1_ffn_w_gate, L1_ffn_w_up, L1_ffn_w_down)
    return x

_drawn_inputs = setup_inputs


def setup_inputs(seed=0):
    import zlib

    import numpy as np

    out = dict(_drawn_inputs(seed))
    spreads = {'L0_xattn_b_k': (0.0, 0.8),
     'L0_xattn_ln_gamma': (1.0, 0.6),
     'L0_xattn_ln_beta': (0.0, 0.474),
     'L0_ffn_rn_pre1': (1.0, 0.2),
     'L0_ffn_rn_pre2': (1.0, 0.2),
     'L0_ffn_rn_post1': (1.0, 0.2),
     'L0_ffn_rn_post2': (1.0, 0.2),
     'L0_ffn_rn_post': (1.0, 0.2),
     'L0_ffn_router_scale': (1.0, 0.2),
     'L0_ffn_per_expert_scale': (1.0, 0.2),
     'L1_xattn_q_norm_w': (1.0, 0.598),
     'L1_xattn_k_norm_w': (1.0, 0.6)}
    factors = {'L0_xattn_W_k': 3.087}
    for name, (base, spread) in spreads.items():
        noise = np.random.default_rng([zlib.crc32(name.encode()), seed]).standard_normal(out[name].shape)
        drawn = base * np.exp(spread * noise) if base else spread * noise
        out[name] = jnp.asarray(drawn.astype(out[name].dtype))
    for name, factor in factors.items():
        out[name] = (out[name] * factor).astype(out[name].dtype)
    return out
```

```python
from contextlib import ExitStack

import concourse.bass as bass
from concourse import mybir

ALU = mybir.AluOpType
ACT = mybir.ActivationFunctionType
AX = mybir.AxisListType
F32 = mybir.dt.float32
F32R = mybir.dt.float32r
BF16 = mybir.dt.bfloat16

P = 128
CREDIT = 2


def two_layers(nc, x_in, ctx_in, ctxT_in, wkT_in, bk_in, gamma_in, beta_in, ffn_w_in, rn_pre_in, rn_post_in,
              router_in, router_scale_in, expert_scale_in, q_w_in, k_w_in, woT_in, cos_in, sin_in, out):
    B, S, D = x_in.shape
    C = ctx_in.shape[2]
    NT = B * S // P
    TB = S // P
    KD = D // P
    NH = 16
    NG = 4
    HG = NH // NG
    HD = D // NH
    E = router_in.shape[1]
    HT = ffn_w_in.shape[0] // 3
    STEPS = HT * B
    SIM_SCALE = float(D) ** -0.5
    HEAD_SCALE = float(HD) ** -0.5
    ST = 3 * HD

    ctx = ExitStack()
    with ctx:
        def sem(name):
            return ctx.enter_context(nc.semaphore(name))

        def sb(name, shape, dt=F32, scope=None):
            return (scope or ctx).enter_context(nc.sbuf_tensor(name, shape, dt))

        ps = ctx.enter_context(nc.psum_tensor("ps", [P, 8, 512], F32))

        x = sb("x", [P, NT, D])
        ident = sb("ident", [P, P])
        identb = sb("identb", [P, P], BF16)
        maskb = sb("maskb", [P, P], BF16)
        bst = sb("bst", [P, NT, 6])
        mv = sb("mv", [P, NT, 2])
        vv = sb("vv", [P, NT])
        sd = sb("sd", [P, NT])
        r0 = sb("r0", [P, NT])
        r1 = sb("r1", [P, NT])
        rs = sb("rs", [P, NT])
        nmr = sb("nmr", [P, NT])

        xt_scope = ExitStack()
        xTh = sb("xTh", [P, KD, NT * P], F32R, xt_scope)
        xTl = sb("xTl", [P, KD, NT * P], F32R, xt_scope)
        xn = sb("xn", [P, 2, D], F32, xt_scope)

        a_scope = ExitStack()
        gammaB = sb("gammaB", [P, D], F32, a_scope)
        betaB = sb("betaB", [P, D], F32, a_scope)
        bk = sb("bk", [P, 1], F32, a_scope)
        wk32 = sb("wk32", [P, C], F32, a_scope)
        wkh = sb("wkh", [P, C], F32R, a_scope)
        wkl = sb("wkl", [P, C], F32R, a_scope)
        cT32 = sb("cT32", [P, S], F32, a_scope)
        cTh = sb("cTh", [P, S], F32R, a_scope)
        cTl = sb("cTl", [P, S], F32R, a_scope)
        kvf = sb("kvf", [P, S], F32, a_scope)
        kvTh = sb("kvTh", [P, B, S], F32R, a_scope)
        kvTl = sb("kvTl", [P, B, S], F32R, a_scope)
        kvh = sb("kvh", [P, NT, C], F32R, a_scope)
        kvl = sb("kvl", [P, NT, C], F32R, a_scope)
        oTh = sb("oTh", [P, S], F32R, a_scope)
        oTl = sb("oTl", [P, S], F32R, a_scope)
        sim = sb("sim", [P, NT, D], F32, a_scope)
        va = sb("va", [P, 2, D], F32, a_scope)
        vb = sb("vb", [P, 2, D], F32, a_scope)
        vc = sb("vc", [P, 2, D], F32, a_scope)
        mxa = sb("mxa", [P, NT], F32, a_scope)
        nma = sb("nma", [P, NT], F32, a_scope)
        sma = sb("sma", [P, NT], F32, a_scope)
        rca = sb("rca", [P, NT], F32, a_scope)
        a_scope.close()

        acc_scope = ExitStack()
        accD = sb("accD", [P, NT, D], F32, acc_scope)
        accM = x
        lgT = accD[0:E, 0:B, :]
        f_scope = ExitStack()
        raw = sb("raw", [P, 2, 3, D], F32, f_scope)
        wh = sb("wh", [P, 2, 3, D], F32R, f_scope)
        wl = sb("wl", [P, 2, 3, D], F32R, f_scope)
        act_o = sb("act_o", [P, 2, S], F32, f_scope)
        hid = sb("hid", [P, 2, S], F32, f_scope)
        hidh = sb("hidh", [P, 2, S], F32R, f_scope)
        hidl = sb("hidl", [P, 2, S], F32R, f_scope)
        affB = sb("affB", [P, B, S], F32, f_scope)
        rnp = sb("rnp", [P, 2, KD], F32, f_scope)
        rw32 = sb("rw32", [P, KD, E], F32, f_scope)
        rsc = sb("rsc", [P, KD], F32, f_scope)
        rws = sb("rws", [P, KD, E], F32, f_scope)
        rwh = sb("rwh", [P, KD, E], F32R, f_scope)
        rwl = sb("rwl", [P, KD, E], F32R, f_scope)
        pesB = sb("pesB", [P, E], F32, f_scope)
        desc = sb("desc", [P, E], F32, f_scope)
        lg, lg2, key, oh1, oh2 = (sb("r_" + n, [P, NT, E], F32, f_scope) for n in ("lg", "lg2", "key", "oh1", "oh2"))
        m1, m2, pk = (sb("r_" + n, [P, NT], F32, f_scope) for n in ("m1", "m2", "pk"))
        f_scope.close()
        g_scope = ExitStack()
        postB = sb("postB", [P, 3, D], F32, g_scope)
        xr = sb("xr", [P, 4, D], F32, g_scope)
        sq = sb("sq", [P, D], F32, g_scope)
        ta = sb("ta", [P, 2, D], F32, g_scope)
        tb = sb("tb", [P, 2, D], F32, g_scope)
        tc_ = sb("tc_", [P, NT, D], F32, g_scope)
        ssq = sb("ssq", [P, 3, NT], F32, g_scope)
        rr = sb("rr", [P, 3, NT], F32, g_scope)
        g_scope.close()
        acc_scope.close()
        xt_scope.close()

        b_scope = ExitStack()
        V = sb("V", [P, NT, C], F32, b_scope)
        KT = sb("KT", [ST, B * NG, S], F32R, b_scope)
        cosB = sb("cosB", [P, TB, HD], F32, b_scope)
        sinB = sb("sinB", [P, TB, HD], F32, b_scope)
        wcos = sb("wcos", [P, TB, D], F32, b_scope)
        wsin = sb("wsin", [P, TB, D], F32, b_scope)
        woh = sb("woh", [P, KD, D], F32R, b_scope)
        wol = sb("wol", [P, KD, D], F32R, b_scope)
        k_scope = ExitStack()
        qwB = sb("qwB", [P, 2, D], F32, k_scope)
        kwB = sb("kwB", [P, 2, C], F32, k_scope)
        kcos = sb("kcos", [P, TB, C], F32, k_scope)
        ksin = sb("ksin", [P, TB, C], F32, k_scope)
        wo32 = sb("wo32", [P, KD, D], F32, k_scope)
        ku = sb("ku", [P, NT, C], F32, k_scope)
        ka = sb("ka", [P, NT, C], F32, k_scope)
        kb = sb("kb", [P, NT, C], F32, k_scope)
        kst = sb("kst", [P, NT, NG, ST], F32, k_scope)
        ksq = sb("ksq", [P, C], F32, k_scope)
        kss = sb("kss", [P, NT], F32, k_scope)
        k_scope.close()
        QT = sb("QT", [ST, NH, S], F32R, b_scope)
        Pr = sb("Pr", [P, 2, HG, S], F32, b_scope)
        PT = sb("PT", [P, 2, HG * P], F32, b_scope)
        Vb = sb("Vb", [P, TB, C], F32, b_scope)
        aT = sb("aT", [P, NG, S], F32, b_scope)
        aTh = sb("aTh", [P, NG, S], F32R, b_scope)
        aTl = sb("aTl", [P, NG, S], F32R, b_scope)
        u = sb("u", [P, D], F32, b_scope)
        qa = sb("qa", [P, D], F32, b_scope)
        qb = sb("qb", [P, D], F32, b_scope)
        qst = sb("qst", [P, NH, ST], F32, b_scope)
        rE = sb("rE", [P, 2, HG, HD], F32, b_scope)
        Rs = sb("Rs", [P, 2, P], F32, b_scope)
        mxb = sb("mxb", [P, 2, 2], F32, b_scope)
        nmb = sb("nmb", [P, 2, 2], F32, b_scope)
        smb = sb("smb", [P, 2, HG], F32, b_scope)
        rcb = sb("rcb", [P, 2, HG], F32, b_scope)
        b_scope.close()

        x_dram = nc.dram_tensor("x_dram", (P, NT, D), F32, kind="Internal").ap()
        aff_dram = nc.dram_tensor("aff_dram", (E, NT * P), F32, kind="Internal").ap()

        def sems(*names):
            return [sem(n) for n in names]

        phase_done, consts_ready = sems("phase_done", "consts_ready")
        x_loaded = sems(*(f"x_loaded{b}" for b in range(B)))
        stored = sems(*(f"stored{b}" for b in range(B)))
        small_loaded, ctxT_loaded = sems("small_loaded", "ctxT_loaded")
        dve_chain, act_chain, pool_chain = sems("dve_chain", "act_chain", "pool_chain")
        root_asked, root_done = sems("root_asked", "root_done")
        xn_ready, xt_turned, xt_high, xt_low = sems("xn_ready", "xt_turned", "xt_high", "xt_low")
        wk_high, ctx_high, ctx_low, kv_done, kv_biased, kvT_high, kvT_low, kv_turned, kv_high, kv_low = sems(
            "wk_high", "ctx_high", "ctx_low", "kv_done", "kv_biased", "kvT_high", "kvT_low", "kv_turned", "kv_high", "kv_low")
        pkv_done, pkv_high, pkv_low, sim_done, sim_copied = sems("pkv_done", "pkv_high", "pkv_low", "sim_done", "sim_copied")
        a_weighed, a_scaled, a_max, a_exp, a_added = sems("a_weighed", "a_scaled", "a_max", "a_exp", "a_added")
        x_spilled, rw_scaled, rw_high, rw_low, lg_done, lg_copied, lg_turned = sems(
            "x_spilled", "rw_scaled", "rw_high", "rw_low", "lg_done", "lg_copied", "lg_turned")
        aff_ready, aff_turned, aff_copied, aff_stored, acc_zero, aff_asked, aff_exp = sems(
            "aff_ready", "aff_turned", "aff_copied", "aff_stored", "acc_zero", "aff_asked", "aff_exp")
        w_loaded = sems("w_loaded0", "w_loaded1")
        aff_loaded = sems(*(f"aff_loaded{b}" for b in range(B)))
        w_high, w_low, gate_done, up_done, out_done = sems("w_high", "w_low", "gate_done", "up_done", "out_done")
        act_ready, aff_applied, hid_ready, hid_high, hid_low, acc_added = sems(
            "act_ready", "aff_applied", "hid_ready", "hid_high", "hid_low", "acc_added")
        squares_ready, g_parts, g_sum, g_added = sems("squares_ready", "g_parts", "g_sum", "g_added")
        xr_loaded = sems(*(f"xr_loaded{i}" for i in range(4)))
        b_loaded, k_ready, k_stacked_high, k_stacked, k_turned, k_copied, wo_high = sems(
            "b_loaded", "k_ready", "k_stacked_high", "k_stacked", "k_turned", "k_copied", "wo_high")
        u_ready, qb_ready, qs_ready, qh_ready, ql_ready, q_turned, q_copied_act, q_copied_dve, vb_ready, qa_ready = sems(
            "u_ready", "qb_ready", "qs_ready", "qh_ready", "ql_ready", "q_turned", "q_copied_act", "q_copied_dve", "vb_ready", "qa_ready")
        s_done, negmax_ready, exp_done, rinv_ready, p_turned, p_copied, pv_done, o_done, rinv_copied, attn_ready = sems(
            "s_done", "negmax_ready", "exp_done", "rinv_ready", "p_turned", "p_copied", "pv_done", "o_done", "rinv_copied", "attn_ready")
        attn_high, attn_low, proj_done, proj_added, max_done, recip_done = sems(
            "attn_high", "attn_low", "proj_done", "proj_added", "max_done", "recip_done")

        block = ctx.enter_context(nc.Block())

        ENGINES = 5
        LN_EPS, RMS0_EPS, RMS1_EPS = 1e-5, 1e-6, 1e-5
        UNITS = [(g, qt) for g in range(NG) for qt in range(TB)]
        NU = len(UNITS)
        CHUNKS = [(n, kt) for n, (g, qt) in enumerate(UNITS) for kt in range(qt + 1)]
        NC = len(CHUNKS)

        def end_phase(eng, n):
            eng.drain().then_inc(phase_done, 1)
            eng.wait_ge(phase_done, ENGINES * n)

        def step_no(part, i, j):
            return i * (2 * B) + (part * STEPS + j)

        def next_tile(part, i, j, chain_end):
            k = j // B + 1
            if j % B == 0:
                return None
            if isinstance(i, int) and 2 * i + k >= HT:
                if chain_end:
                    return None
                return part + 1, i * 2 + (part * HT + k), k % 2
            return part, i * 2 + (part * HT + k), k % 2

        @block.sync
        def _(sp):
            load = nc.sync.dma_start
            for b in range(B):
                load(x[:, TB * b:TB * b + TB, :], x_in[b].rearrange("(t p) d -> p t d", p=P)).then_inc(x_loaded[b], 16)
            load(wk32[:, :], wkT_in).then_inc(small_loaded, 16)
            load(bk[:, :], bk_in.rearrange("(p o) -> p o", o=1)).then_inc(small_loaded, 16)
            load(gammaB[:, :], gamma_in.broadcast_to((P, D))).then_inc(small_loaded, 16)
            load(betaB[:, :], beta_in.broadcast_to((P, D))).then_inc(small_loaded, 16)
            for b in range(B):
                if b:
                    sp.wait_ge(ctx_low, b)
                load(cT32[:, :], ctxT_in[:, b * S:(b + 1) * S]).then_inc(ctxT_loaded, 16)
            end_phase(sp, 1)

            load(x_dram, x[:, :, :]).then_inc(x_spilled, 16)
            load(rnp[:, :, :], rn_pre_in).then_inc(small_loaded, 16)
            load(rw32[:, :, :], router_in.rearrange("(k p) e -> p k e", p=P)).then_inc(small_loaded, 16)
            load(rsc[:, :], router_scale_in).then_inc(small_loaded, 16)
            load(pesB[:, :], expert_scale_in.broadcast_to((P, E))).then_inc(small_loaded, 16)
            for q in range(2):
                load(raw[:, q, :, :], ffn_w_in[q]).then_inc(w_loaded[q], 16)
            sp.wait_ge(aff_copied, 1)
            load(aff_dram, lgT).then_inc(aff_stored, 16)

            def stream(part, i):
                for q in range(2):
                    sp.wait_ge(w_low, i * 6 + 3 * (part * HT + q + 1))
                    load(raw[:, q, :, :], ffn_w_in[bass.ds(i * 2 + (part * HT + q + 2), 1)].rearrange("o p m n -> p (o m) n")).then_inc(w_loaded[q], 16)

            with sp.Fori(0, HT // 2 - 1) as i:
                stream(0, i)
            sp.wait_ge(aff_stored, 16)
            for b in range(B):
                load(affB[:, b, :], aff_dram[0:1, b * S:(b + 1) * S].broadcast_to((P, S))).then_inc(aff_loaded[b], 16)
            for q in range(2):
                sp.wait_ge(w_low, 3 * (HT - 2 + q) + 3)
                load(raw[:, q, :, :], ffn_w_in[HT + q]).then_inc(w_loaded[q], 16)
            with sp.Fori(0, HT // 2 - 1) as i:
                stream(1, i)
                for b in range(B):
                    sp.wait_ge(aff_applied, step_no(0, i, B + b + 1))
                    load(affB[:, b, :], aff_dram[bass.ds(i + 1, 1), b * S:(b + 1) * S].broadcast_to((P, S))).then_inc(aff_loaded[b], 16)
            end_phase(sp, 2)

            for k in range(3):
                load(postB[:, k, :], rn_post_in[k:k + 1, :].broadcast_to((P, D))).then_inc(small_loaded, 16)
            for t in range(NT):
                if t >= 4:
                    sp.wait_ge(g_added, t - 3)
                load(xr[:, t % 4, :], x_dram[:, t, :]).then_inc(xr_loaded[t % 4], 16)
            end_phase(sp, 3)

            load(V[:, :, :], ctx_in.rearrange("b (t p) c -> p (b t) c", p=P)).then_inc(b_loaded, 16)
            load(cosB[:, :, :], cos_in.rearrange("(t p) c -> p t c", p=P)).then_inc(b_loaded, 16)
            load(sinB[:, :, :], sin_in.rearrange("(t p) c -> p t c", p=P)).then_inc(b_loaded, 16)
            for k in range(2):
                load(qwB[:, k, :], q_w_in[k:k + 1, :].broadcast_to((P, D))).then_inc(b_loaded, 16)
                load(kwB[:, k, :], k_w_in[k:k + 1, :].broadcast_to((P, C))).then_inc(b_loaded, 16)
            load(wo32[:, :, :], woT_in.rearrange("(k p) n -> p k n", p=P)).then_inc(b_loaded, 16)
            end_phase(sp, 4)
            end_phase(sp, 5)

            for q in range(2):
                load(raw[:, q, :, :], ffn_w_in[2 * HT + q]).then_inc(w_loaded[q], 16)
            with sp.Fori(0, HT // 2 - 1) as i:
                stream(2, i)
            for b in range(B):
                sp.wait_ge(acc_added, 3 * STEPS - B + b + 1 + CREDIT)
                load(out[b].rearrange("(t p) d -> p t d", p=P), x[:, TB * b:TB * b + TB, :]).then_inc(stored[b], 16)
            for b in range(B):
                sp.wait_ge(stored[b], 16)

        @block.gpsimd
        def _(pool):
            chained = [0]

            def link(ins):
                chained[0] += 1
                ins.then_inc(pool_chain, 1)
                pool.wait_ge(pool_chain, chained[0])

            link(nc.gpsimd.memset(ident[:, :], 1.0))
            link(nc.gpsimd.affine_select(out=ident[:, :], in_=ident[:, :], compare_op=ALU.is_equal, fill=0.0, base=0,
                                         pattern=[[-1, P]], channel_multiplier=1))
            link(nc.gpsimd.tensor_copy(identb[:, :], ident[:, :]))
            link(nc.gpsimd.memset(maskb[:, :], 0.0))
            nc.gpsimd.affine_select(out=maskb[:, :], in_=maskb[:, :], compare_op=ALU.is_ge, fill=-1e30, base=0,
                                    pattern=[[-1, P]], channel_multiplier=1).then_inc(consts_ready, 1)
            end_phase(pool, 1)

            nc.gpsimd.iota(desc[:, :], pattern=[[-1, E]], base=E, channel_multiplier=0,
                           allow_small_or_imprecise_dtypes=True).then_inc(consts_ready, 1)
            pool.wait_ge(x_spilled, 16)
            pool.wait_ge(xn_ready, 2 * NT)
            nc.gpsimd.memset(accM[:, :, :], 0.0).then_inc(acc_zero, 1)
            pool.wait_ge(aff_stored, 16)
            nc.gpsimd.memset(accD[:, :, :], 0.0).then_inc(acc_zero, 1)
            end_phase(pool, 2)

            for t in range(NT):
                pool.wait_ge(g_parts, t + 1)
                nc.gpsimd.tensor_tensor(out=tc_[:, t, :], in0=ta[:, t % 2, :], in1=tb[:, t % 2, :], op=ALU.add).then_inc(g_sum, 1)
            end_phase(pool, 3)
            end_phase(pool, 4)

            H2 = HD // 2
            with pool.Fori(0, B) as b:
                for t in range(TB):
                    uv = u[:, :].rearrange("p (h c) -> p h c", c=HD)
                    qv = qb[:, :].rearrange("p (h c) -> p h c", c=HD)
                    sv = wsin[:, t, :].rearrange("p (h c) -> p h c", c=HD)
                    pool.wait_ge(u_ready, b * TB + (t + 1))
                    nc.gpsimd.tensor_tensor(out=qv[:, :, 0:H2], in0=uv[:, :, H2:HD], in1=sv[:, :, 0:H2], op=ALU.mult)
                    nc.gpsimd.tensor_tensor(out=qv[:, :, H2:HD], in0=uv[:, :, 0:H2], in1=sv[:, :, H2:HD], op=ALU.mult).then_inc(qb_ready, 1)
            end_phase(pool, 5)

        @block.tensor
        def _(pe):
            mm, turn = nc.tensor.matmul, nc.tensor.transpose

            def three(out_ap, ah, al, bh, bl, start, stop):
                mm(out_ap, ah, bh, start=start, stop=False)
                mm(out_ap, ah, bl, start=False, stop=False)
                return mm(out_ap, al, bh, start=False, stop=stop)

            def prep(k):
                for t in range(NT):
                    pe.wait_ge(xn_ready, NT * k + t + 1)
                    if t >= 2:
                        pe.wait_ge(xt_low, NT * k + t - 1)
                    for d in range(KD):
                        last = turn(ps[:, t % 2, d * P:(d + 1) * P], xn[:, t % 2, d * P:(d + 1) * P], ident[:, :])
                    last.then_inc(xt_turned, 1)

            def gate_up(part, i, j):
                s = step_no(part, i, j)
                w, q, b = j // B % 2, j % 2, j % B
                bs = slice(b * S, (b + 1) * S)
                if j % B == 0:
                    pe.wait_ge(w_low, i * 6 + (3 * (part * HT + j // B) + 2))
                pe.wait_ge(hid_low, s + (CREDIT - 1))
                for m, done in ((0, gate_done), (1, up_done)):
                    for d in range(KD):
                        dsl = slice(d * P, (d + 1) * P)
                        last = three(ps[:, 2 * m + q, :], wh[:, w, m, dsl], wl[:, w, m, dsl], xTh[:, d, bs], xTl[:, d, bs], d == 0, d == KD - 1)
                    last.then_inc(done, 1)

            def down(part, i, j):
                s = step_no(part, i, j)
                w, q = j // B % 2, j % 2
                if j % B == 0:
                    pe.wait_ge(w_low, i * 6 + (3 * (part * HT + j // B) + 3))
                pe.wait_ge(hid_low, s + (CREDIT + 1))
                pe.wait_ge(acc_added, s + CREDIT)
                for t in range(TB):
                    tsl = slice(t * P, (t + 1) * P)
                    last = three(ps[:, 4 + t, :], hidh[:, q, tsl], hidl[:, q, tsl], wh[:, w, 2, :], wl[:, w, 2, :], True, True)
                last.then_inc(out_done, 1)

            def ffn(part, chain_start, chain_end):
                if chain_start:
                    gate_up(part, 0, 0)
                with pe.Fori(0, HT // 2 - 1) as i:
                    for j in range(2 * B):
                        gate_up(part, i, j + 1)
                        down(part, i, j)
                for j in range(2 * B):
                    if j < 2 * B - 1 or not chain_end:
                        gate_up(part, HT // 2 - 1, j + 1)
                    down(part, HT // 2 - 1, j)

            pe.wait_ge(consts_ready, 1)
            pe.sem_inc(out_done, CREDIT)
            pe.sem_inc(pv_done, CREDIT)
            pe.sem_inc(o_done, CREDIT)
            for b in range(B):
                pe.wait_ge(ctx_low, b + 1)
                three(ps[:, 4, :], wkh[:, :], wkl[:, :], cTh[:, :], cTl[:, :], True, True).then_inc(kv_done, 1)
                pe.wait_ge(kv_biased, b + 1)
                if b:
                    pe.wait_ge(kv_low, b)
                for j in range(TB):
                    last = turn(ps[:, 5, j * P:(j + 1) * P], kvf[:, j * P:(j + 1) * P], ident[:, :])
                last.then_inc(kv_turned, 1)
            prep(0)
            for b in range(B):
                bs = slice(b * S, (b + 1) * S)
                pe.wait_ge(xt_low, TB * (b + 1))
                pe.wait_ge(kv_low, b + 1)
                for j in range(KD):
                    last = three(ps[:, 2, :], kvh[:, TB * b + j, :], kvl[:, TB * b + j, :], xTh[:, j, bs], xTl[:, j, bs], j == 0, j == KD - 1)
                last.then_inc(pkv_done, 1)
                pe.wait_ge(pkv_low, b + 1)
                for i in range(TB):
                    n = TB * b + i
                    if n >= 2:
                        pe.wait_ge(sim_copied, n - 1)
                    isl = slice(i * P, (i + 1) * P)
                    three(ps[:, 6 + n % 2, :], oTh[:, isl], oTl[:, isl], kvTh[:, b, :], kvTl[:, b, :], True, True).then_inc(sim_done, 1)
            end_phase(pe, 1)

            prep(1)
            pe.wait_ge(rw_low, 1)
            pe.wait_ge(xt_low, 2 * NT)
            for b in range(B):
                bs = slice(b * S, (b + 1) * S)
                for d in range(KD):
                    last = three(ps[0:E, 4 + b, :], rwh[:, d, :], rwl[:, d, :], xTh[:, d, bs], xTl[:, d, bs], d == 0, d == KD - 1)
            last.then_inc(lg_done, 1)
            pe.wait_ge(lg_copied, 1)
            for t in range(NT):
                last = turn(ps[:, 2, t * E:(t + 1) * E], lgT[:, t // TB, t % TB * P:(t % TB + 1) * P], ident[0:E, 0:E])
            last.then_inc(lg_turned, 1)
            pe.wait_ge(aff_ready, 1)
            for t in range(NT):
                last = turn(ps[0:E, 4 + t // TB, t % TB * P:(t % TB + 1) * P], lg[:, t, :], ident[:, :])
            last.then_inc(aff_turned, 1)
            pe.wait_ge(aff_copied, 1)
            ffn(0, True, False)
            ffn(1, False, True)
            end_phase(pe, 2)
            end_phase(pe, 3)

            pe.wait_ge(k_stacked, 1)
            for c in range(B * NG):
                if c >= 2:
                    pe.wait_ge(k_copied, c - 1)
                for t in range(TB):
                    last = turn(ps[0:ST, c % 2, t * P:(t + 1) * P], kst[:, c // NG * TB + t, c % NG, :], ident[:, :])
                last.then_inc(k_turned, 1)
            end_phase(pe, 4)

            def scores(b, n, hp):
                g, qt = UNITS[n]
                L = max(256, (qt + 1) * P)
                pe.wait_ge(exp_done, b * (2 * NU) + (2 * n + hp - 1 + CREDIT))
                for bank in (2 * hp, 2 * hp + 1):
                    mm(ps[:, bank, 0:L], QT[:, g * HG + bank, qt * P:(qt + 1) * P],
                       KT[:, bass.ds(b * NG + g, 1), 0:L].rearrange("p o n -> p (o n)"), start=True, stop=True)
                    last = mm(ps[:, bank, qt * P:(qt + 1) * P], identb[:, :], maskb[:, :], start=False, stop=True, skip_group_check=True)
                last.then_inc(s_done, 1)

            def turn_p(b, n, kt):
                c = CHUNKS.index((n, kt))
                if kt == 0:
                    pe.wait_ge(exp_done, b * (2 * NU) + (2 * n + 2 + CREDIT))
                pe.wait_ge(p_copied, b * NC + (c - 1 + CREDIT))
                for h in range(HG):
                    last = turn(ps[:, 4 + c % 2, h * P:(h + 1) * P], Pr[:, n % 2, h, kt * P:(kt + 1) * P], ident[:, :])
                last.then_inc(p_turned, 1)

            def values(b, n, kt):
                g, qt = UNITS[n]
                c = CHUNKS.index((n, kt))
                pe.wait_ge(p_copied, b * NC + (c + 1 + CREDIT))
                if kt == 0:
                    pe.wait_ge(attn_ready, b * NU + (n - 1 + CREDIT))
                for h in range(HG):
                    last = mm(ps[h * HD:(h + 1) * HD, 6 + n % 2, 0:P], Vb[:, kt, g * HD:(g + 1) * HD], PT[:, c % 2, h * P:(h + 1) * P],
                              start=(kt == 0), stop=(kt == qt))
                last.then_inc(pv_done, 1)
                if kt == qt:
                    pe.wait_ge(rinv_ready, b * NU + (n + 1))
                    turn(ps[:, 6 + n % 2, P:2 * P], rE[:, n % 2, :, :].rearrange("p h c -> p (h c)"), ident[:, :]).then_inc(o_done, 1)

            with pe.Fori(0, B) as b:
                for t in range(TB):
                    pe.wait_ge(ql_ready, b * TB + (t + 1 + CREDIT))
                    for g in range(NG):
                        pe.wait_ge(q_copied_dve if g % 2 else q_copied_act, b * (TB * 2) + (t * 2 + g // 2 + CREDIT))
                        for h in range(HG):
                            last = turn(ps[0:ST, 4 + g % 2, h * P:(h + 1) * P], qst[:, g * HG + h, :], ident[:, :])
                        last.then_inc(q_turned, 1)
                pe.wait_ge(q_copied_act, b * (TB * 2) + (TB * 2 + CREDIT))
                pe.wait_ge(q_copied_dve, b * (TB * 2) + (TB * 2 + CREDIT))
                pe.wait_ge(vb_ready, b + 1)
                scores(b, 0, 0)
                scores(b, 0, 1)
                for n, (g, qt) in enumerate(UNITS):
                    if n + 1 < NU:
                        scores(b, n + 1, 0)
                    turn_p(b, n, 0)
                    if n + 1 < NU:
                        scores(b, n + 1, 1)
                    for kt in range(1, qt + 1):
                        turn_p(b, n, kt)
                        values(b, n, kt - 1)
                    values(b, n, qt)
                pe.wait_ge(attn_low, b + 1)
                for t in range(TB):
                    tsl = slice(t * P, (t + 1) * P)
                    for g in range(NG):
                        last = three(ps[:, t, :], aTh[:, g, tsl], aTl[:, g, tsl], woh[:, g, :], wol[:, g, :], g == 0, g == NG - 1)
                last.then_inc(proj_done, 1)
                pe.wait_ge(proj_added, b + 1)
            end_phase(pe, 5)

            prep(2)
            pe.wait_ge(xt_low, 3 * NT)
            ffn(2, True, True)

        @block.scalar
        def _(act):
            func = nc.scalar.activation
            chained, roots = [0], [0]

            def link(ins):
                chained[0] += 1
                ins.then_inc(act_chain, 1)
                act.wait_ge(act_chain, chained[0])

            def root():
                roots[0] += 1
                act.wait_ge(root_asked, roots[0])
                func(sd[:, :], vv[:, :], ACT.Sqrt).then_inc(root_done, 1)

            def prep(k):
                root()
                for t in range(NT):
                    act.wait_ge(xt_turned, NT * k + t + 1)
                    func(xTh[:, :, t * P:(t + 1) * P], ps[:, t % 2, :].rearrange("p (k n) -> p k n", k=KD), ACT.Copy).then_inc(xt_high, 1)

            def split_high(part, T, w, m):
                if m == 0:
                    act.wait_ge(out_done, T * B + (CREDIT - B))
                if part < 2 and m < 2:
                    for d in range(KD):
                        dsl = slice(d * P, (d + 1) * P)
                        last = func(wh[:, w, m, dsl], raw[:, w, m, dsl], ACT.Copy, scale=rnp[:, part, d:d + 1])
                else:
                    last = func(wh[:, w, m, :], raw[:, w, m, :], ACT.Copy)
                last.then_inc(w_high, 1)

            def step(part, i, j, chain_end):
                s, q = step_no(part, i, j), j % 2
                act.wait_ge(gate_done, s + 1)
                act.wait_ge(hid_ready, s + (CREDIT - 1))
                func(act_o[:, q, :], ps[:, q, :], ACT.Silu if part == 2 else ACT.Gelu_apprx_tanh).then_inc(act_ready, 1)
                nxt = next_tile(part, i, j, chain_end)
                if nxt:
                    p2, T, w = nxt
                    if j % B == 1:
                        act.wait_ge(w_loaded[w], i * 16 + 16 * ((part * HT + j // B + 1) // 2 + 1))
                    split_high(p2, T, w, j % B - 1)
                act.wait_ge(hid_ready, s + (CREDIT + 1))
                act.wait_ge(out_done, s + (CREDIT - 1))
                func(hidh[:, q, :], hid[:, q, :], ACT.Copy).then_inc(hid_high, 1)

            def ffn(part, chain_start, chain_end):
                if chain_start:
                    act.wait_ge(w_loaded[0], 16 * (part * HT // 2 + 1))
                    for m in range(3):
                        split_high(part, part * HT, 0, m) if part else first_split(m)
                with act.Fori(0, HT // 2 - 1) as i:
                    for j in range(2 * B):
                        step(part, i, j, chain_end)
                for j in range(2 * B):
                    step(part, HT // 2 - 1, j, chain_end)

            def first_split(m):
                if m < 2:
                    for d in range(KD):
                        dsl = slice(d * P, (d + 1) * P)
                        last = func(wh[:, 0, m, dsl], raw[:, 0, m, dsl], ACT.Copy, scale=rnp[:, 0, d:d + 1])
                else:
                    last = func(wh[:, 0, m, :], raw[:, 0, m, :], ACT.Copy)
                last.then_inc(w_high, 1)

            act.wait_ge(small_loaded, 64)
            func(wkh[:, :], wk32[:, :], ACT.Copy).then_inc(wk_high, 1)
            for b in range(B):
                act.wait_ge(ctxT_loaded, 16 * (b + 1))
                if b:
                    act.wait_ge(kv_done, b)
                func(cTh[:, :], cT32[:, :], ACT.Copy).then_inc(ctx_high, 1)
                act.wait_ge(kv_done, b + 1)
                if b:
                    act.wait_ge(kv_turned, b)
                    act.wait_ge(kvT_low, b)
                func(kvf[:, :], ps[:, 4, :], ACT.Identity, bias=bk[:, 0:1]).then_inc(kv_biased, 1)
                act.wait_ge(kv_biased, b + 1)
                func(kvTh[:, b, :], kvf[:, :], ACT.Copy).then_inc(kvT_high, 1)
                act.wait_ge(kv_turned, b + 1)
                func(kvh[:, TB * b:TB * (b + 1), :], ps[:, 5, :].rearrange("p (j c) -> p j c", c=C), ACT.Copy).then_inc(kv_high, 1)
            prep(0)
            for b in range(B):
                act.wait_ge(pkv_done, b + 1)
                if b:
                    act.wait_ge(sim_done, TB * b)
                func(oTh[:, :], ps[:, 2, :], ACT.Copy).then_inc(pkv_high, 1)
                for i in range(TB):
                    n = TB * b + i
                    act.wait_ge(sim_done, n + 1)
                    func(sim[:, n, :], ps[:, 6 + n % 2, :], ACT.Copy).then_inc(sim_copied, 1)
            root()
            for t in range(NT):
                act.wait_ge(a_weighed, t + 1)
                if t >= 2:
                    act.wait_ge(a_exp, t - 1)
                func(vb[:, t % 2, :], va[:, t % 2, :], ACT.Copy, scale=rs[:, t:t + 1]).then_inc(a_scaled, 1)
                act.wait_ge(a_max, t + 1)
                if t >= 2:
                    act.wait_ge(a_added, t - 1)
                func(vc[:, t % 2, :], vb[:, t % 2, :], ACT.Exp, bias=nma[:, t:t + 1], accum_out=sma[:, t:t + 1]).then_inc(a_exp, 1)
            end_phase(act, 1)

            prep(1)
            act.wait_ge(rw_scaled, 1)
            func(rwh[:, :, :], rws[:, :, :], ACT.Copy).then_inc(rw_high, 1)
            act.wait_ge(lg_done, 1)
            func(lgT, ps[0:E, 4:8, :], ACT.Copy).then_inc(lg_copied, 1)
            act.wait_ge(aff_asked, 1)
            func(key[:, :, :], lg2[:, :, :], ACT.Exp).then_inc(aff_exp, 1)
            act.wait_ge(aff_turned, 1)
            func(lgT, ps[0:E, 4:8, :], ACT.Copy).then_inc(aff_copied, 1)
            act.wait_ge(small_loaded, 128)
            ffn(0, True, False)
            ffn(1, False, True)
            end_phase(act, 2)

            for k, a in ((0, accD), (1, accM)):
                for t in range(NT):
                    link(func(sq[:, :], a[:, t, :], ACT.Square, accum_out=ssq[:, k, t:t + 1]))
            act.sem_inc(squares_ready, 1)
            root()
            root()
            for t in range(NT):
                act.wait_ge(g_sum, t + 1)
                link(func(sq[:, :], tc_[:, t, :], ACT.Square, accum_out=ssq[:, 2, t:t + 1]))
            act.sem_inc(squares_ready, 1)
            root()
            end_phase(act, 3)

            act.wait_ge(b_loaded, 16 * 8)
            for t in range(NT):
                link(func(ksq[:, :], V[:, t, :], ACT.Square, accum_out=kss[:, t:t + 1]))
            act.sem_inc(squares_ready, 1)
            root()
            func(woh[:, :, :], wo32[:, :, :], ACT.Copy).then_inc(wo_high, 1)
            act.wait_ge(k_ready, 1)
            for z in (0, 1):
                last = func(kst[:, :, :, z * HD:(z + 1) * HD].bitcast(F32R), ka[:, :, :].rearrange("p t (g c) -> p t g c", g=NG), ACT.Copy)
            last.then_inc(k_stacked_high, 1)
            for c in range(B * NG):
                act.wait_ge(k_turned, c + 1)
                func(KT[:, c, :], ps[0:ST, c % 2, :], ACT.Copy).then_inc(k_copied, 1)
            root()
            act.sem_inc(q_copied_act, CREDIT)
            act.sem_inc(exp_done, CREDIT)
            end_phase(act, 4)

            def sums_copy(b, m):
                act.wait_ge(o_done, b * NU + (m + 1 + CREDIT))
                act.wait_ge(attn_ready, b * NU + (m - 1 + CREDIT))
                func(Rs[:, m % 2, :], ps[:, 6 + m % 2, P:2 * P], ACT.Copy).then_inc(rinv_copied, 1)

            with act.Fori(0, B) as b:
                for t in range(TB):
                    act.wait_ge(qs_ready, b * TB + (t + CREDIT))
                    func(u[:, :], x[:, bass.ds(b * TB + t, 1), :].rearrange("p o d -> p (o d)"), ACT.Identity,
                         bias=nmr[:, bass.ds(b * TB + t, 1)], scale=rs[:, bass.ds(b * TB + t, 1)]).then_inc(u_ready, 1)
                    act.wait_ge(qs_ready, b * TB + (t + 1 + CREDIT))
                    act.wait_ge(q_turned, b * (TB * NG) + (t * NG + CREDIT))
                    for z in (0, 2):
                        last = func(qst[:, :, z * HD:(z + 1) * HD].bitcast(F32R), qa[:, :].rearrange("p (h c) -> p h c", c=HD), ACT.Copy)
                    last.then_inc(qh_ready, 1)
                    for g in (0, 2):
                        act.wait_ge(q_turned, b * (TB * NG) + (t * NG + g + 1 + CREDIT))
                        func(QT[:, g * HG:(g + 1) * HG, t * P:(t + 1) * P], ps[0:ST, 4, :].rearrange("p (h n) -> p h n", h=HG), ACT.Copy).then_inc(q_copied_act, 1)
                for m, (g, qt) in enumerate(UNITS):
                    L = (qt + 1) * P
                    act.wait_ge(o_done, b * NU + (m - 1 + CREDIT))
                    for hp in range(2):
                        act.wait_ge(negmax_ready, b * (2 * NU) + (2 * m + hp + 1))
                        for h in range(2):
                            bank = 2 * hp + h
                            last = func(Pr[:, m % 2, bank, 0:L], ps[:, bank, 0:L], ACT.Exp, bias=nmb[:, hp, h:h + 1], scale=HEAD_SCALE,
                                        accum_out=smb[:, m % 2, bank:bank + 1])
                        last.then_inc(exp_done, 1)
                    if m >= 1:
                        sums_copy(b, m - 1)
                sums_copy(b, NU - 1)
                act.wait_ge(attn_ready, b * NU + (NU + CREDIT))
                func(aTh[:, :, :], aT[:, :, :], ACT.Copy).then_inc(attn_high, 1)
            end_phase(act, 5)

            prep(2)
            ffn(2, True, True)

        @block.vector
        def _(dve):
            V_ = nc.vector
            chained, roots = [0], [0]

            def link(ins):
                chained[0] += 1
                ins.then_inc(dve_chain, 1)
                dve.wait_ge(dve_chain, chained[0])

            def rsqrt(dst):
                roots[0] += 1
                dve.sem_inc(root_asked, 1)
                dve.wait_ge(root_done, roots[0])
                link(V_.reciprocal(r0[:, :], sd[:, :]))
                link(V_.tensor_tensor(out=r1[:, :], in0=r0[:, :], in1=r0[:, :], op=ALU.mult))
                link(V_.tensor_tensor(out=r1[:, :], in0=r1[:, :], in1=vv[:, :], op=ALU.mult))
                link(V_.tensor_scalar(r1[:, :], r1[:, :], -0.5, 1.5, ALU.mult, ALU.add))
                link(V_.tensor_tensor(out=dst, in0=r0[:, :], in1=r1[:, :], op=ALU.mult))

            def deviations(mul, add, factor=None):
                for t in range(NT):
                    last = V_.bn_aggr(mv[:, t, :], bst[:, t, :])
                link(last)
                link(V_.tensor_scalar(vv[:, :], mv[:, :, 1], mul, add, ALU.mult, ALU.add))
                rsqrt(rs[:, :])
                if factor is not None:
                    link(V_.tensor_scalar(rs[:, :], rs[:, :], factor, None, ALU.mult))
                link(V_.scalar_tensor_tensor(out=nmr[:, :], in0=mv[:, :, 0], scalar=-1.0, in1=rs[:, :], op0=ALU.mult, op1=ALU.mult))

            def x_stats(arrivals=None):
                for t in range(NT):
                    if arrivals and t % TB == 0:
                        dve.wait_ge(arrivals[t // TB], 16)
                    last = V_.bn_stats(bst[:, t, :], x[:, t, :])
                link(last)

            def prep(k):
                def low(t):
                    dve.wait_ge(xt_high, NT * k + t + 1)
                    V_.tensor_tensor(out=xTl[:, :, t * P:(t + 1) * P], in0=ps[:, t % 2, :].rearrange("p (k n) -> p k n", k=KD),
                                     in1=xTh[:, :, t * P:(t + 1) * P].bitcast(F32), op=ALU.subtract).then_inc(xt_low, 1)
                for t in range(NT):
                    if t >= 2:
                        dve.wait_ge(xt_turned, NT * k + t - 1)
                    V_.tensor_scalar(xn[:, t % 2, :], x[:, t, :], mv[:, t, 0:1], rs[:, t:t + 1], ALU.subtract, ALU.mult).then_inc(xn_ready, 1)
                    if t >= 1:
                        low(t - 1)
                low(NT - 1)

            def split_low(part, T, w, m):
                dve.wait_ge(w_high, T * 3 + (m + 1))
                if part < 2 and m < 2:
                    for d in range(KD):
                        dsl = slice(d * P, (d + 1) * P)
                        last = V_.scalar_tensor_tensor(out=wl[:, w, m, dsl], in0=raw[:, w, m, dsl], scalar=rnp[:, part, d:d + 1],
                                                       in1=wh[:, w, m, dsl].bitcast(F32), op0=ALU.mult, op1=ALU.subtract)
                else:
                    last = V_.tensor_tensor(out=wl[:, w, m, :], in0=raw[:, w, m, :], in1=wh[:, w, m, :].bitcast(F32), op=ALU.subtract)
                last.then_inc(w_low, 1)

            def hidden(part, i, j, nxt):
                s, q, b = step_no(part, i, j), j % 2, j % B
                dve.wait_ge(act_ready, s + 1)
                if part == 1:
                    if j // B % 2 == 0:
                        dve.wait_ge(aff_loaded[b], i * 16 + 16 * (j // (2 * B) + 1))
                    V_.tensor_tensor(out=act_o[:, q, :], in0=act_o[:, q, :], in1=affB[:, b, :], op=ALU.mult).then_inc(aff_applied, 1)
                    dve.wait_ge(aff_applied, step_no(0, i, j) + 1)
                dve.wait_ge(up_done, s + 1)
                dve.wait_ge(hid_low, s + (CREDIT - 1))
                V_.tensor_tensor(out=hid[:, q, :], in0=act_o[:, q, :], in1=ps[:, 2 + q, :], op=ALU.mult).then_inc(hid_ready, 1)
                if nxt:
                    split_low(nxt[0], nxt[1], nxt[2], j % B - 1)
                dve.wait_ge(hid_high, s + 1)
                V_.tensor_tensor(out=hidl[:, q, :], in0=hid[:, q, :], in1=hidh[:, q, :].bitcast(F32), op=ALU.subtract).then_inc(hid_low, 1)

            def add(part, i, j):
                s, b = step_no(part, i, j), j % B
                acc = (accD, accM, x)[part][:, TB * b:TB * (b + 1), :]
                dve.wait_ge(out_done, s + (CREDIT + 1))
                dve.wait_ge(acc_added, s + (CREDIT - 1))
                V_.tensor_tensor(out=acc, in0=acc, in1=ps[:, 4:8, :], op=ALU.add).then_inc(acc_added, 1)

            def ffn(part, chain_start, chain_end):
                if chain_start:
                    for m in range(3):
                        split_low(part, part * HT, 0, m)
                    hidden(part, 0, 0, None)
                with dve.Fori(0, HT // 2 - 1) as i:
                    for j in range(2 * B):
                        hidden(part, i, j + 1, next_tile(part, i, j + 1, chain_end))
                        add(part, i, j)
                i = HT // 2 - 1
                for j in range(2 * B):
                    if j < 2 * B - 1:
                        hidden(part, i, j + 1, next_tile(part, i, j + 1, chain_end))
                    elif not chain_end:
                        hidden(part + 1, 0, 0, None)
                    add(part, i, j)

            for s_, k in ((hid_low, CREDIT), (acc_added, CREDIT), (hid_ready, CREDIT), (qs_ready, CREDIT),
                          (ql_ready, CREDIT), (q_copied_dve, CREDIT), (p_copied, CREDIT), (attn_ready, CREDIT), (q_turned, CREDIT)):
                dve.sem_inc(s_, k)

            dve.wait_ge(wk_high, 1)
            V_.tensor_tensor(out=wkl[:, :], in0=wk32[:, :], in1=wkh[:, :].bitcast(F32), op=ALU.subtract)
            for b in range(B):
                dve.wait_ge(ctx_high, b + 1)
                V_.tensor_tensor(out=cTl[:, :], in0=cT32[:, :], in1=cTh[:, :].bitcast(F32), op=ALU.subtract).then_inc(ctx_low, 1)
                dve.wait_ge(kvT_high, b + 1)
                V_.tensor_tensor(out=kvTl[:, b, :], in0=kvf[:, :], in1=kvTh[:, b, :].bitcast(F32), op=ALU.subtract).then_inc(kvT_low, 1)
                dve.wait_ge(kv_high, b + 1)
                V_.tensor_tensor(out=kvl[:, TB * b:TB * (b + 1), :], in0=ps[:, 5, :].rearrange("p (j c) -> p j c", c=C),
                                 in1=kvh[:, TB * b:TB * (b + 1), :].bitcast(F32), op=ALU.subtract).then_inc(kv_low, 1)
            x_stats(x_loaded)
            deviations(1.0, LN_EPS)
            prep(0)
            for b in range(B):
                dve.wait_ge(pkv_high, b + 1)
                V_.tensor_tensor(out=oTl[:, :], in0=ps[:, 2, :], in1=oTh[:, :].bitcast(F32), op=ALU.subtract).then_inc(pkv_low, 1)
                for i in range(TB):
                    n = TB * b + i
                    dve.wait_ge(sim_copied, n + 1)
                    last = V_.bn_stats(bst[:, n, :], sim[:, n, :])
            link(last)
            deviations(SIM_SCALE * SIM_SCALE, 1e-6, SIM_SCALE)

            def a_residual(t):
                dve.wait_ge(a_exp, t + 1)
                link(V_.reciprocal(rca[:, t:t + 1], sma[:, t:t + 1]))
                V_.scalar_tensor_tensor(out=x[:, t, :], in0=vc[:, t % 2, :], scalar=rca[:, t:t + 1], in1=x[:, t, :],
                                        op0=ALU.mult, op1=ALU.add).then_inc(a_added, 1)

            for t in range(NT):
                if t >= 2:
                    dve.wait_ge(a_scaled, t - 1)
                V_.scalar_tensor_tensor(out=va[:, t % 2, :], in0=sim[:, t, :], scalar=mv[:, t, 0:1], in1=gammaB[:, :],
                                        op0=ALU.subtract, op1=ALU.mult).then_inc(a_weighed, 1)
                if t >= 1:
                    a_residual(t - 1)
                dve.wait_ge(a_scaled, t + 1)
                link(V_.tensor_tensor_reduce(vb[:, t % 2, :], vb[:, t % 2, :], betaB[:, :], 1.0, -3.0e38, ALU.add, ALU.max, mxa[:, t:t + 1]))
                V_.tensor_scalar(nma[:, t:t + 1], mxa[:, t:t + 1], -1.0, None, ALU.mult).then_inc(a_max, 1)
            a_residual(NT - 1)
            dve.wait_ge(a_added, NT)
            end_phase(dve, 1)

            x_stats()
            deviations(1.0 + RMS0_EPS, RMS0_EPS * LN_EPS)
            prep(1)
            dve.wait_ge(small_loaded, 128)
            link(V_.tensor_scalar(rsc[:, :], rsc[:, :], float(D) ** -0.5, None, ALU.mult))
            for d in range(KD):
                last = V_.tensor_scalar(rws[:, d, :], rw32[:, d, :], rsc[:, d:d + 1], None, ALU.mult)
            last.then_inc(rw_scaled, 1)
            dve.wait_ge(rw_high, 1)
            V_.tensor_tensor(out=rwl[:, :, :], in0=rws[:, :, :], in1=rwh[:, :, :].bitcast(F32), op=ALU.subtract).then_inc(rw_low, 1)
            dve.wait_ge(lg_turned, 1)
            dve.wait_ge(consts_ready, 2)

            def over_e(a):
                return a.unsqueeze(2).broadcast_to((P, NT, E))

            descB = desc[:, :].unsqueeze(1).broadcast_to((P, NT, E))
            link(V_.tensor_copy(lg[:, :, :], ps[:, 2, 0:NT * E].rearrange("p (t e) -> p t e", e=E)))

            def largest(src, m, oh):
                link(V_.tensor_reduce(m[:, :], src[:, :, :], AX.X, ALU.max))
                link(V_.tensor_tensor(out=key[:, :, :], in0=src[:, :, :], in1=over_e(m[:, :]), op=ALU.is_equal))
                link(V_.tensor_tensor(out=key[:, :, :], in0=key[:, :, :], in1=descB, op=ALU.mult))
                link(V_.tensor_reduce(pk[:, :], key[:, :, :], AX.X, ALU.max))
                link(V_.tensor_tensor(out=oh[:, :, :], in0=key[:, :, :], in1=over_e(pk[:, :]), op=ALU.is_equal))

            largest(lg, m1, oh1)
            link(V_.scalar_tensor_tensor(out=lg2[:, :, :], in0=oh1[:, :, :], scalar=-3.0e38, in1=lg[:, :, :], op0=ALU.mult, op1=ALU.add))
            largest(lg2, m2, oh2)
            V_.tensor_tensor(out=lg2[:, :, :], in0=lg[:, :, :], in1=over_e(m1[:, :]), op=ALU.subtract).then_inc(aff_asked, 1)
            link(V_.tensor_tensor(out=oh1[:, :, :], in0=oh1[:, :, :], in1=oh2[:, :, :], op=ALU.add))
            dve.wait_ge(aff_exp, 1)
            link(V_.tensor_tensor(out=key[:, :, :], in0=key[:, :, :], in1=oh1[:, :, :], op=ALU.mult))
            link(V_.tensor_reduce(m1[:, :], key[:, :, :], AX.X, ALU.add))
            link(V_.reciprocal(m2[:, :], m1[:, :]))
            link(V_.tensor_tensor(out=key[:, :, :], in0=key[:, :, :], in1=over_e(m2[:, :]), op=ALU.mult))
            V_.tensor_tensor(out=lg[:, :, :], in0=key[:, :, :], in1=pesB[:, :].unsqueeze(1).broadcast_to((P, NT, E)), op=ALU.mult).then_inc(aff_ready, 1)
            dve.wait_ge(acc_zero, 2)
            ffn(0, True, False)
            ffn(1, False, True)
            end_phase(dve, 2)

            dve.wait_ge(small_loaded, 176)
            dve.wait_ge(squares_ready, 1)
            for k in range(2):
                link(V_.tensor_scalar(vv[:, :], ssq[:, k, :], 1.0 / D, RMS0_EPS, ALU.mult, ALU.add))
                rsqrt(rr[:, k, :])
            for t in range(NT):
                if t >= 2:
                    dve.wait_ge(g_sum, t - 1)
                V_.scalar_tensor_tensor(out=ta[:, t % 2, :], in0=accD[:, t, :], scalar=rr[:, 0, t:t + 1], in1=postB[:, 0, :], op0=ALU.mult, op1=ALU.mult)
                V_.scalar_tensor_tensor(out=tb[:, t % 2, :], in0=accM[:, t, :], scalar=rr[:, 1, t:t + 1], in1=postB[:, 1, :],
                                        op0=ALU.mult, op1=ALU.mult).then_inc(g_parts, 1)
            dve.wait_ge(squares_ready, 2)
            link(V_.tensor_scalar(vv[:, :], ssq[:, 2, :], 1.0 / D, RMS0_EPS, ALU.mult, ALU.add))
            rsqrt(rr[:, 2, :])
            for t in range(NT):
                link(V_.scalar_tensor_tensor(out=ta[:, t % 2, :], in0=tc_[:, t, :], scalar=rr[:, 2, t:t + 1], in1=postB[:, 2, :], op0=ALU.mult, op1=ALU.mult))
                dve.wait_ge(xr_loaded[t % 4], 16 * (t // 4 + 1))
                V_.tensor_tensor(out=x[:, t, :], in0=ta[:, t % 2, :], in1=xr[:, t % 4, :], op=ALU.add).then_inc(g_added, 1)
            dve.wait_ge(g_added, NT)
            end_phase(dve, 3)

            dve.wait_ge(b_loaded, 16 * 8)
            for t in range(TB):
                for w_, c_, s_, n in ((qwB, wcos, wsin, NH), (kwB, kcos, ksin, NG)):
                    for k, o_, tab in ((0, c_, cosB), (1, s_, sinB)):
                        last = V_.tensor_tensor(out=o_[:, t, :].rearrange("p (h c) -> p h c", c=HD), in0=w_[:, k, :].rearrange("p (h c) -> p h c", c=HD),
                                                in1=tab[:, t:t + 1, :].broadcast_to((P, n, HD)), op=ALU.mult)
            link(last)
            dve.wait_ge(squares_ready, 3)
            link(V_.tensor_scalar(vv[:, :], kss[:, :], 1.0 / C, RMS1_EPS, ALU.mult, ALU.add))
            rsqrt(rs[:, :])
            link(V_.tensor_tensor(out=ku[:, :, :], in0=V[:, :, :], in1=rs[:, :].unsqueeze(2).broadcast_to((P, NT, C)), op=ALU.mult))
            H2 = HD // 2
            for b in range(B):
                bt = slice(b * TB, (b + 1) * TB)
                V_.tensor_tensor(out=ka[:, bt, :], in0=ku[:, bt, :], in1=kcos[:, :, :], op=ALU.mult)
                for t in range(TB):
                    kuv, kbv = (a[:, b * TB + t, :].rearrange("p (g c) -> p g c", c=HD) for a in (ku, kb))
                    ksv = ksin[:, t, :].rearrange("p (g c) -> p g c", c=HD)
                    V_.tensor_tensor(out=kbv[:, :, 0:H2], in0=kuv[:, :, H2:HD], in1=ksv[:, :, 0:H2], op=ALU.mult)
                    last = V_.tensor_tensor(out=kbv[:, :, H2:HD], in0=kuv[:, :, 0:H2], in1=ksv[:, :, H2:HD], op=ALU.mult)
            link(last)
            V_.tensor_tensor(out=ka[:, :, :], in0=ka[:, :, :], in1=kb[:, :, :], op=ALU.add).then_inc(k_ready, 1)
            dve.wait_ge(wo_high, 1)
            V_.tensor_tensor(out=wol[:, :, :], in0=wo32[:, :, :], in1=woh[:, :, :].bitcast(F32), op=ALU.subtract)
            dve.wait_ge(k_stacked_high, 1)
            for g in range(NG):
                last = V_.tensor_tensor(out=kst[:, :, g, 2 * HD:ST].bitcast(F32R), in0=ka[:, :, g * HD:(g + 1) * HD],
                                        in1=kst[:, :, g, 0:HD], op=ALU.subtract)
            last.then_inc(k_stacked, 1)
            x_stats()
            deviations(1.0 + RMS1_EPS, RMS1_EPS * LN_EPS)
            end_phase(dve, 4)

            def maximum(b, n, hp):
                L = (UNITS[n][1] + 1) * P
                dve.wait_ge(s_done, b * (2 * NU) + (2 * n + hp + 1))
                V_.tensor_reduce(mxb[:, hp, :], ps[:, 2 * hp:2 * hp + 2, 0:L], AX.X, ALU.max).then_inc(max_done, 1)
                dve.wait_ge(max_done, b * (2 * NU) + (2 * n + hp + 1))
                V_.tensor_scalar(nmb[:, hp, :], mxb[:, hp, :], -HEAD_SCALE, None, ALU.mult).then_inc(negmax_ready, 1)

            def copy_p(b, n, kt):
                c = CHUNKS.index((n, kt))
                dve.wait_ge(p_turned, b * NC + (c + 1))
                dve.wait_ge(pv_done, b * NC + (c - 1 + CREDIT))
                V_.tensor_copy(PT[:, c % 2, :], ps[:, 4 + c % 2, :]).then_inc(p_copied, 1)

            def inverse(b, n):
                dve.wait_ge(exp_done, b * (2 * NU) + (2 * n + 2 + CREDIT))
                V_.reciprocal(rcb[:, n % 2, :], smb[:, n % 2, :]).then_inc(recip_done, 1)
                dve.wait_ge(recip_done, b * NU + (n + 1))
                V_.tensor_copy(rE[:, n % 2, :, :], rcb[:, n % 2, :].unsqueeze(2).broadcast_to((P, HG, HD))).then_inc(rinv_ready, 1)

            def normed(b, n):
                g, qt = UNITS[n]
                dve.wait_ge(rinv_copied, b * NU + (n + 1))
                V_.tensor_tensor(out=aT[:, g, qt * P:(qt + 1) * P], in0=ps[:, 6 + n % 2, 0:P], in1=Rs[:, n % 2, :], op=ALU.mult).then_inc(attn_ready, 1)

            with dve.Fori(0, B) as b:
                V_.tensor_copy(Vb[:, :, :], V[:, bass.ds(b * TB, TB), :]).then_inc(vb_ready, 1)
                for t in range(TB):
                    dve.wait_ge(u_ready, b * TB + (t + 1))
                    dve.wait_ge(ql_ready, b * TB + (t + CREDIT))
                    V_.tensor_tensor(out=qa[:, :], in0=u[:, :], in1=wcos[:, t, :], op=ALU.mult).then_inc(qa_ready, 1)
                    dve.wait_ge(qa_ready, b * TB + (t + 1))
                    dve.wait_ge(qb_ready, b * TB + (t + 1))
                    V_.tensor_tensor(out=qa[:, :], in0=qa[:, :], in1=qb[:, :], op=ALU.add).then_inc(qs_ready, 1)
                    dve.wait_ge(qh_ready, b * TB + (t + 1))
                    V_.tensor_tensor(out=qst[:, :, HD:2 * HD].bitcast(F32R), in0=qa[:, :].rearrange("p (h c) -> p h c", c=HD),
                                     in1=qst[:, :, 0:HD], op=ALU.subtract).then_inc(ql_ready, 1)
                    for g in (1, 3):
                        dve.wait_ge(q_turned, b * (TB * NG) + (t * NG + g + 1 + CREDIT))
                        V_.tensor_copy(QT[:, g * HG:(g + 1) * HG, t * P:(t + 1) * P], ps[0:ST, 5, :].rearrange("p (h n) -> p h n", h=HG)).then_inc(q_copied_dve, 1)
                maximum(b, 0, 0)
                maximum(b, 0, 1)
                for n, (g, qt) in enumerate(UNITS):
                    if n + 1 < NU:
                        maximum(b, n + 1, 0)
                    copy_p(b, n, 0)
                    inverse(b, n)
                    if n >= 1:
                        normed(b, n - 1)
                    if n + 1 < NU:
                        maximum(b, n + 1, 1)
                    for kt in range(1, qt + 1):
                        copy_p(b, n, kt)
                normed(b, NU - 1)
                dve.wait_ge(attn_high, b + 1)
                V_.tensor_tensor(out=aTl[:, :, :], in0=aT[:, :, :], in1=aTh[:, :, :].bitcast(F32), op=ALU.subtract).then_inc(attn_low, 1)
                dve.wait_ge(proj_done, b + 1)
                V_.tensor_tensor(out=x[:, bass.ds(b * TB, TB), :], in0=x[:, bass.ds(b * TB, TB), :], in1=ps[:, 0:TB, :], op=ALU.add).then_inc(proj_added, 1)
            end_phase(dve, 5)

            x_stats()
            deviations(1.0, LN_EPS)
            prep(2)
            ffn(2, True, True)


def kernel(**inputs):
    import numpy as np
    import concourse.bacc as bacc
    from concourse.bass_utils import run_bass_kernel_spmd

    def a(name):
        return np.asarray(inputs[name])

    def tiles(gate, up, down):
        n = down.shape[0] // P
        cols = [w.reshape(-1, P, n, P).transpose(2, 1, 0, 3).reshape(n, P, 1, -1) for w in (gate, up)]
        return np.concatenate([*cols, down.reshape(n, P, 1, -1)], axis=2)

    we = [a("L0_ffn_we_" + n) for n in ("gate", "up", "down")]
    ffn_w = np.concatenate([
        tiles(a("L0_ffn_w_gate"), a("L0_ffn_w_up"), a("L0_ffn_w_down")),
        tiles(we[0].transpose(1, 0, 2).reshape(512, -1), we[1].transpose(1, 0, 2).reshape(512, -1), we[2].reshape(-1, 512)),
        tiles(a("L1_ffn_w_gate").T, a("L1_ffn_w_up").T, a("L1_ffn_w_down").T)])

    HD, T = 32, 512
    freq = (np.float32(1.0) / np.float32(10000.0) ** (np.arange(0, HD, 2, dtype=np.float32) / np.float32(HD))).astype(np.float32)
    angle = np.outer(np.arange(T, dtype=np.float32), freq).astype(np.float32)
    cos = np.cos(np.concatenate([angle, angle], -1)).astype(np.float32)
    sin = np.concatenate([-np.sin(angle), np.sin(angle)], -1).astype(np.float32)

    def with_halves_swapped(w):
        return np.stack([w, w.reshape(-1, 2, HD // 2)[:, ::-1].reshape(-1)])

    def columns(w):
        return w.reshape(-1, P).T

    arrays = {
        "x": a("x"), "ctx": a("ctx_512"), "ctxT": a("ctx_512").reshape(-1, 128).T, "wkT": a("L0_xattn_W_k").T,
        "bk": a("L0_xattn_b_k"), "gamma": a("L0_xattn_ln_gamma")[None], "beta": a("L0_xattn_ln_beta")[None],
        "ffn_w": ffn_w, "rn_pre": np.stack([columns(a("L0_ffn_rn_pre1")), columns(a("L0_ffn_rn_pre2"))], 1),
        "rn_post": np.stack([a("L0_ffn_rn_post1"), a("L0_ffn_rn_post2"), a("L0_ffn_rn_post")]),
        "router": a("L0_ffn_router_w"), "router_scale": columns(a("L0_ffn_router_scale")), "expert_scale": a("L0_ffn_per_expert_scale")[None],
        "q_w": with_halves_swapped(a("L1_xattn_q_norm_w")), "k_w": with_halves_swapped(a("L1_xattn_k_norm_w")),
        "woT": a("L1_xattn_w_out").T, "cos": cos, "sin": sin,
    }
    nc = bacc.Bacc("TRN2", target_bir_lowering=False, num_devices=1)
    args, given = [], {}
    for name, v in arrays.items():
        v = np.ascontiguousarray(v)
        given[f"in_{name}"] = v
        args.append(nc.dram_tensor(f"in_{name}", v.shape, mybir.dt.from_np(v.dtype), kind="ExternalInput").ap())
    shape = a("x").shape
    out = nc.dram_tensor("out_x", shape, F32, kind="ExternalOutput").ap()
    two_layers(nc, *args, out)
    r = run_bass_kernel_spmd(nc, [given], core_ids=[0])
    return r.results[0]["out_x"]
```

```python
from contextlib import ExitStack

import concourse.bass as bass
from concourse import mybir

ALU = mybir.AluOpType
ACT = mybir.ActivationFunctionType
AX = mybir.AxisListType
F32 = mybir.dt.float32
F32R = mybir.dt.float32r
BF16 = mybir.dt.bfloat16

P = 128
CREDIT = 2
LEAD = 4


def two_layers(nc, x_in, ctx_in, ctxT_in, wkT_in, bk_in, gamma_in, beta_in, ffn_w_in, rn_pre_in, rn_post_in,
              router_in, router_scale_in, expert_scale_in, q_w_in, k_w_in, woT_in, cos_in, sin_in, out):
    B, S, D = x_in.shape
    C = ctx_in.shape[2]
    NT = B * S // P
    TB = S // P
    KD = D // P
    NH = 16
    NG = 4
    HG = NH // NG
    HD = D // NH
    E = router_in.shape[1]
    HT = ffn_w_in.shape[0] // 3
    STEPS = HT * B
    SIM_SCALE = float(D) ** -0.5
    HEAD_SCALE = float(HD) ** -0.5
    ST = 3 * HD

    ctx = ExitStack()
    with ctx:
        def sem(name):
            return ctx.enter_context(nc.semaphore(name))

        def sb(name, shape, dt=F32, scope=None):
            return (scope or ctx).enter_context(nc.sbuf_tensor(name, shape, dt))

        ps = ctx.enter_context(nc.psum_tensor("ps", [P, 8, 512], F32))

        x = sb("x", [P, NT, D])
        ident = sb("ident", [P, P])
        identb = sb("identb", [P, P], BF16)
        maskb = sb("maskb", [P, P], BF16)
        bst = sb("bst", [P, NT, 6])
        mv = sb("mv", [P, NT, 2])
        vv = sb("vv", [P, NT])
        sd = sb("sd", [P, NT])
        r0 = sb("r0", [P, NT])
        r1 = sb("r1", [P, NT])
        rs = sb("rs", [P, NT])
        nmr = sb("nmr", [P, NT])

        xt_scope = ExitStack()
        xTh = sb("xTh", [P, KD, NT * P], F32R, xt_scope)
        xTl = sb("xTl", [P, KD, NT * P], F32R, xt_scope)
        xn = sb("xn", [P, 2, D], F32, xt_scope)

        a_scope = ExitStack()
        gammaB = sb("gammaB", [P, D], F32, a_scope)
        betaB = sb("betaB", [P, D], F32, a_scope)
        bk = sb("bk", [P, 1], F32, a_scope)
        wk32 = sb("wk32", [P, C], F32, a_scope)
        wkh = sb("wkh", [P, C], F32R, a_scope)
        wkl = sb("wkl", [P, C], F32R, a_scope)
        cT32 = sb("cT32", [P, S], F32, a_scope)
        cTh = sb("cTh", [P, S], F32R, a_scope)
        cTl = sb("cTl", [P, S], F32R, a_scope)
        kvf = sb("kvf", [P, S], F32, a_scope)
        kvTh = sb("kvTh", [P, B, S], F32R, a_scope)
        kvTl = sb("kvTl", [P, B, S], F32R, a_scope)
        kvh = sb("kvh", [P, NT, C], F32R, a_scope)
        kvl = sb("kvl", [P, NT, C], F32R, a_scope)
        oTh = sb("oTh", [P, S], F32R, a_scope)
        oTl = sb("oTl", [P, S], F32R, a_scope)
        sim = sb("sim", [P, NT, D], F32, a_scope)
        va = sb("va", [P, 2, D], F32, a_scope)
        vb = sb("vb", [P, 2, D], F32, a_scope)
        vc = sb("vc", [P, 2, D], F32, a_scope)
        mxa = sb("mxa", [P, NT], F32, a_scope)
        nma = sb("nma", [P, NT], F32, a_scope)
        sma = sb("sma", [P, NT], F32, a_scope)
        rca = sb("rca", [P, NT], F32, a_scope)
        a_scope.close()

        acc_scope = ExitStack()
        accD = sb("accD", [P, NT, D], F32, acc_scope)
        accM = x
        lgT = accD[0:E, 0:B, :]
        f_scope = ExitStack()
        raw = sb("raw", [P, 2, 3, D], F32, f_scope)
        wh = sb("wh", [P, 2, 3, D], F32R, f_scope)
        wl = sb("wl", [P, 2, 3, D], F32R, f_scope)
        act_o = sb("act_o", [P, 2, S], F32, f_scope)
        hid = sb("hid", [P, 2, S], F32, f_scope)
        hidh = sb("hidh", [P, 2, S], F32R, f_scope)
        hidl = sb("hidl", [P, 2, S], F32R, f_scope)
        affB = sb("affB", [P, B, S], F32, f_scope)
        rnp = sb("rnp", [P, 2, KD], F32, f_scope)
        rw32 = sb("rw32", [P, KD, E], F32, f_scope)
        rsc = sb("rsc", [P, KD], F32, f_scope)
        rws = sb("rws", [P, KD, E], F32, f_scope)
        rwh = sb("rwh", [P, KD, E], F32R, f_scope)
        rwl = sb("rwl", [P, KD, E], F32R, f_scope)
        pesB = sb("pesB", [P, E], F32, f_scope)
        desc = sb("desc", [P, E], F32, f_scope)
        lg, lg2, key, oh1, oh2 = (sb("r_" + n, [P, NT, E], F32, f_scope) for n in ("lg", "lg2", "key", "oh1", "oh2"))
        m1, m2, pk = (sb("r_" + n, [P, NT], F32, f_scope) for n in ("m1", "m2", "pk"))
        f_scope.close()
        g_scope = ExitStack()
        postB = sb("postB", [P, 3, D], F32, g_scope)
        xr = sb("xr", [P, 4, D], F32, g_scope)
        sq = sb("sq", [P, D], F32, g_scope)
        ta = sb("ta", [P, 2, D], F32, g_scope)
        tb = sb("tb", [P, 2, D], F32, g_scope)
        tc_ = sb("tc_", [P, NT, D], F32, g_scope)
        ssq = sb("ssq", [P, 3, NT], F32, g_scope)
        rr = sb("rr", [P, 3, NT], F32, g_scope)
        g_scope.close()
        acc_scope.close()
        xt_scope.close()

        b_scope = ExitStack()
        V = sb("V", [P, NT, C], F32, b_scope)
        KT = sb("KT", [ST, B * NG, S], F32R, b_scope)
        QT = sb("QT", [ST, TB, HG, NG, P], F32R, b_scope)
        woh = sb("woh", [P, KD, D], F32R, b_scope)
        wol = sb("wol", [P, KD, D], F32R, b_scope)
        k_scope = ExitStack()
        cosB = sb("cosB", [P, TB, HD], F32, k_scope)
        sinB = sb("sinB", [P, TB, HD], F32, k_scope)
        wcos = sb("wcos", [P, TB, D], F32, k_scope)
        wsin = sb("wsin", [P, TB, D], F32, k_scope)
        qwB = sb("qwB", [P, 2, D], F32, k_scope)
        kwB = sb("kwB", [P, 2, C], F32, k_scope)
        kcos = sb("kcos", [P, TB, C], F32, k_scope)
        ksin = sb("ksin", [P, TB, C], F32, k_scope)
        ku = sb("ku", [P, NT, C], F32, k_scope)
        ka = sb("ka", [P, NT, C], F32, k_scope)
        kb = sb("kb", [P, TB, C], F32, k_scope)
        ksq = sb("ksq", [P, C], F32, k_scope)
        kss = sb("kss", [P, NT], F32, k_scope)
        u = sb("u", [P, TB, D], F32, k_scope)
        wo32 = u
        qa = sb("qa", [P, 2, D], F32, k_scope)
        qb = sb("qb", [P, 2, D], F32, k_scope)
        th = sb("th", [P, 2, D], F32R, k_scope)
        tl = sb("tl", [P, 2, D], F32R, k_scope)
        k_scope.close()
        Pr = sb("Pr", [P, 2, HG, S], F32, b_scope)
        PT = sb("PT", [P, 4, HG * P], F32, b_scope)
        Vb = sb("Vb", [P, TB, C], F32, b_scope)
        aT = sb("aT", [P, 2, NG, P], F32, b_scope)
        aTh = sb("aTh", [P, 2, NG, P], F32R, b_scope)
        aTl = sb("aTl", [P, 2, NG, P], F32R, b_scope)
        rE = sb("rE", [P, 4, HG, HD], F32, b_scope)
        rT = sb("rT", [P, 2, P], F32, b_scope)
        mnb = sb("mnb", [P, 2, HG], F32, b_scope)
        smb = sb("smb", [P, 4, HG], F32, b_scope)
        b_scope.close()

        x_dram = nc.dram_tensor("x_dram", (P, NT, D), F32, kind="Internal").ap()
        q_dram = nc.dram_tensor("q_dram", (2, NT, P, D), F32R, kind="Internal").ap()
        k_dram = nc.dram_tensor("k_dram", (2, B, P, S), F32R, kind="Internal").ap()
        aff_dram = nc.dram_tensor("aff_dram", (E, NT * P), F32, kind="Internal").ap()

        def sems(*names):
            return [sem(n) for n in names]

        phase_done, consts_ready = sems("phase_done", "consts_ready")
        x_loaded = sems(*(f"x_loaded{b}" for b in range(B)))
        stored = sems(*(f"stored{b}" for b in range(B)))
        small_loaded, ctxT_loaded = sems("small_loaded", "ctxT_loaded")
        dve_chain, act_chain, pool_chain = sems("dve_chain", "act_chain", "pool_chain")
        root_asked, root_done = sems("root_asked", "root_done")
        xn_ready, xt_turned, xt_high, xt_low = sems("xn_ready", "xt_turned", "xt_high", "xt_low")
        wk_high, ctx_high, ctx_low, kv_done, kv_biased, kvT_high, kvT_low, kv_turned, kv_high, kv_low = sems(
            "wk_high", "ctx_high", "ctx_low", "kv_done", "kv_biased", "kvT_high", "kvT_low", "kv_turned", "kv_high", "kv_low")
        pkv_done, pkv_high, pkv_low, sim_done, sim_copied = sems("pkv_done", "pkv_high", "pkv_low", "sim_done", "sim_copied")
        a_weighed, a_scaled, a_max, a_exp, a_added = sems("a_weighed", "a_scaled", "a_max", "a_exp", "a_added")
        x_spilled, rw_scaled, rw_high, rw_low, lg_done, lg_copied, lg_turned = sems(
            "x_spilled", "rw_scaled", "rw_high", "rw_low", "lg_done", "lg_copied", "lg_turned")
        aff_ready, aff_turned, aff_copied, aff_stored, acc_zero, aff_asked, aff_exp = sems(
            "aff_ready", "aff_turned", "aff_copied", "aff_stored", "acc_zero", "aff_asked", "aff_exp")
        w_loaded = sems("w_loaded0", "w_loaded1")
        aff_loaded = sems(*(f"aff_loaded{b}" for b in range(B)))
        w_high, w_low, gate_done, up_done, out_done = sems("w_high", "w_low", "gate_done", "up_done", "out_done")
        act_ready, aff_applied, hid_ready, hid_high, hid_low, acc_added = sems(
            "act_ready", "aff_applied", "hid_ready", "hid_high", "hid_low", "acc_added")
        squares_ready, g_parts, g_sum, g_added = sems("squares_ready", "g_parts", "g_sum", "g_added")
        xr_loaded = sems(*(f"xr_loaded{i}" for i in range(4)))
        b_loaded, k_ready, k_turned, k_high, k_low, k_spun, wo_high, wo_low = sems(
            "b_loaded", "k_ready", "k_turned", "k_high", "k_low", "k_spun", "wo_high", "wo_low")
        u_ready, qa_ready, qb_ready, qs_ready, q_turned, q_high, q_low = sems(
            "u_ready", "qa_ready", "qb_ready", "qs_ready", "q_turned", "q_high", "q_low")
        k_stored, kt_loaded, rows_scaled = sems("k_stored", "kt_loaded", "rows_scaled")
        q_high_stored = sems("q_high_stored0", "q_high_stored1")
        q_low_stored = sems("q_low_stored0", "q_low_stored1")
        qt_loaded = sems(*(f"qt_loaded{t}" for t in range(TB)))
        s_done, min_ready, exp_done, rinv_ready, p_turned, p_copied_act, p_copied_dve, pv_done, o_done, rt_copied, attn_ready = sems(
            "s_done", "min_ready", "exp_done", "rinv_ready", "p_turned", "p_copied_act", "p_copied_dve", "pv_done", "o_done",
            "rt_copied", "attn_ready")
        attn_high, attn_low, proj_done, proj_added, vb_ready = sems("attn_high", "attn_low", "proj_done", "proj_added", "vb_ready")

        block = ctx.enter_context(nc.Block())

        ENGINES = 5
        LN_EPS, RMS0_EPS, RMS1_EPS = 1e-5, 1e-6, 1e-5
        NU, LAG = TB * NG, 3

        def unit(n):
            return n % NU // NG, n % NG, n // NU

        def units_order(units, waiting, last):
            steps, waiting = [], list(waiting)
            for n in units:
                more = not (last and n + 1 == NU)
                done = n >= NG + LAG - 1 and (n - LAG + 1) % NG == 0
                if more:
                    steps.append(("scores", n + 1, 0))
                for kt in range(unit(n)[0] + 1):
                    if len(waiting) == 2:
                        steps.append(("values", *waiting.pop(0)))
                    if kt == 0 and more:
                        steps.append(("scores", n + 1, 1))
                    if kt == 0 and done:
                        steps.append(("split", (n - LAG + 1) // NG - 1, 0))
                    steps.append(("turn", n, kt))
                    waiting.append((n, kt))
                if done:
                    steps.append(("project", (n - LAG + 1) // NG - 1, 0))
            if last:
                steps += [("values", *w) for w in waiting] + [("split", TB - 1, 0), ("project", TB - 1, 0)]
            return steps

        WAITING = [(LAG - 2, 0), (LAG - 1, 0)]
        FIRST = units_order(range(LAG), [], False)
        BODY = units_order(range(LAG, NU + LAG), WAITING, False)
        LAST = units_order(range(LAG, NU), WAITING, True)
        KEYS = [(n, kt) for n in range(NU + LAG) for kt in range(unit(n)[0] + 1)]
        PER_SEQ = TB * (TB + 1) // 2 * NG
        ACT_KEYS = [k for k in KEYS if k[1] % 2 == 0]
        DVE_KEYS = [k for k in KEYS if k[1] % 2 == 1]
        ACT_PER_SEQ, DVE_PER_SEQ = (sum(k[0] < NU for k in keys) for keys in (ACT_KEYS, DVE_KEYS))

        def bank_of(steps, i):
            before = 0 if steps is FIRST else LAG
            return 4 + (before + sum(s_[0] in ("turn", "project") for s_ in steps[:i])) % 2

        def count(b, per_seq, k):
            return b * per_seq + (k + LEAD)

        def end_of_unit(n, kt):
            return kt == unit(n)[0]

        def end_phase(eng, n):
            eng.drain().then_inc(phase_done, 1)
            eng.wait_ge(phase_done, ENGINES * n)

        def step_no(part, i, j):
            return i * (2 * B) + (part * STEPS + j)

        def next_tile(part, i, j, chain_end):
            k = j // B + 1
            if j % B == 0:
                return None
            if isinstance(i, int) and 2 * i + k >= HT:
                if chain_end:
                    return None
                return part + 1, i * 2 + (part * HT + k), k % 2
            return part, i * 2 + (part * HT + k), k % 2

        @block.sync
        def _(sp):
            load = nc.sync.dma_start
            for b in range(B):
                load(x[:, TB * b:TB * b + TB, :], x_in[b].rearrange("(t p) d -> p t d", p=P)).then_inc(x_loaded[b], 16)
            load(wk32[:, :], wkT_in).then_inc(small_loaded, 16)
            load(bk[:, :], bk_in.rearrange("(p o) -> p o", o=1)).then_inc(small_loaded, 16)
            load(gammaB[:, :], gamma_in.broadcast_to((P, D))).then_inc(small_loaded, 16)
            load(betaB[:, :], beta_in.broadcast_to((P, D))).then_inc(small_loaded, 16)
            for b in range(B):
                if b:
                    sp.wait_ge(ctx_low, b)
                load(cT32[:, :], ctxT_in[:, b * S:(b + 1) * S]).then_inc(ctxT_loaded, 16)
            end_phase(sp, 1)

            load(x_dram, x[:, :, :]).then_inc(x_spilled, 16)
            load(rnp[:, :, :], rn_pre_in).then_inc(small_loaded, 16)
            load(rw32[:, :, :], router_in.rearrange("(k p) e -> p k e", p=P)).then_inc(small_loaded, 16)
            load(rsc[:, :], router_scale_in).then_inc(small_loaded, 16)
            load(pesB[:, :], expert_scale_in.broadcast_to((P, E))).then_inc(small_loaded, 16)
            for q in range(2):
                load(raw[:, q, :, :], ffn_w_in[q]).then_inc(w_loaded[q], 16)
            sp.wait_ge(aff_copied, 1)
            load(aff_dram, lgT).then_inc(aff_stored, 16)

            def stream(part, i):
                for q in range(2):
                    sp.wait_ge(w_low, i * 6 + 3 * (part * HT + q + 1))
                    load(raw[:, q, :, :], ffn_w_in[bass.ds(i * 2 + (part * HT + q + 2), 1)].rearrange("o p m n -> p (o m) n")).then_inc(w_loaded[q], 16)

            with sp.Fori(0, HT // 2 - 1) as i:
                stream(0, i)
            sp.wait_ge(aff_stored, 16)
            for b in range(B):
                load(affB[:, b, :], aff_dram[0:1, b * S:(b + 1) * S].broadcast_to((P, S))).then_inc(aff_loaded[b], 16)
            for q in range(2):
                sp.wait_ge(w_low, 3 * (HT - 2 + q) + 3)
                load(raw[:, q, :, :], ffn_w_in[HT + q]).then_inc(w_loaded[q], 16)
            with sp.Fori(0, HT // 2 - 1) as i:
                stream(1, i)
                for b in range(B):
                    sp.wait_ge(aff_applied, step_no(0, i, B + b + 1))
                    load(affB[:, b, :], aff_dram[bass.ds(i + 1, 1), b * S:(b + 1) * S].broadcast_to((P, S))).then_inc(aff_loaded[b], 16)
            end_phase(sp, 2)

            for k in range(3):
                load(postB[:, k, :], rn_post_in[k:k + 1, :].broadcast_to((P, D))).then_inc(small_loaded, 16)
            for t in range(NT):
                if t >= 4:
                    sp.wait_ge(g_added, t - 3)
                load(xr[:, t % 4, :], x_dram[:, t, :]).then_inc(xr_loaded[t % 4], 16)
            end_phase(sp, 3)

            load(V[:, :, :], ctx_in.rearrange("b (t p) c -> p (b t) c", p=P)).then_inc(b_loaded, 16)
            load(cosB[:, :, :], cos_in.rearrange("(t p) c -> p t c", p=P)).then_inc(b_loaded, 16)
            load(sinB[:, :, :], sin_in.rearrange("(t p) c -> p t c", p=P)).then_inc(b_loaded, 16)
            for k in range(2):
                load(qwB[:, k, :], q_w_in[k:k + 1, :].broadcast_to((P, D))).then_inc(b_loaded, 16)
                load(kwB[:, k, :], k_w_in[k:k + 1, :].broadcast_to((P, C))).then_inc(b_loaded, 16)
            load(wo32[:, :, :], woT_in.rearrange("(k p) n -> p k n", p=P)).then_inc(b_loaded, 16)
            for b in range(B):
                sp.wait_ge(k_high, b + 1)
                load(k_dram[0, b].bitcast(F32), th[:, b % 2, :].bitcast(F32)).then_inc(k_stored, 16)
                sp.wait_ge(k_low, b + 1)
                load(k_dram[1, b].bitcast(F32), tl[:, b % 2, :].bitcast(F32)).then_inc(k_stored, 16)
                sp.wait_ge(k_stored, 32 * (b + 1))
                sp.sem_inc(k_spun, 1)
            for t in range(NT):
                sp.wait_ge(q_high, t + 1)
                load(q_dram[0, t].bitcast(F32), th[:, t % 2, :].bitcast(F32)).then_inc(q_high_stored[t % 2], 16)
                sp.wait_ge(q_low, t + 1)
                load(q_dram[1, t].bitcast(F32), tl[:, t % 2, :].bitcast(F32)).then_inc(q_low_stored[t % 2], 16)
            for q in range(2):
                sp.wait_ge(q_high_stored[q], 16 * (NT // 2))
                sp.wait_ge(q_low_stored[q], 16 * (NT // 2))
            end_phase(sp, 4)
            end_phase(sp, 5)

            for q in range(2):
                load(raw[:, q, :, :], ffn_w_in[2 * HT + q]).then_inc(w_loaded[q], 16)
            with sp.Fori(0, HT // 2 - 1) as i:
                stream(2, i)
            for b in range(B):
                sp.wait_ge(acc_added, 3 * STEPS - B + b + 1 + CREDIT)
                load(out[b].rearrange("(t p) d -> p t d", p=P), x[:, TB * b:TB * b + TB, :]).then_inc(stored[b], 16)
            for b in range(B):
                sp.wait_ge(stored[b], 16)

        @block.gpsimd
        def _(pool):
            chained = [0]

            def link(ins):
                chained[0] += 1
                ins.then_inc(pool_chain, 1)
                pool.wait_ge(pool_chain, chained[0])

            link(nc.gpsimd.memset(ident[:, :], 1.0))
            link(nc.gpsimd.affine_select(out=ident[:, :], in_=ident[:, :], compare_op=ALU.is_equal, fill=0.0, base=0,
                                         pattern=[[-1, P]], channel_multiplier=1))
            link(nc.gpsimd.tensor_copy(identb[:, :], ident[:, :]))
            link(nc.gpsimd.memset(maskb[:, :], 0.0))
            nc.gpsimd.affine_select(out=maskb[:, :], in_=maskb[:, :], compare_op=ALU.is_ge, fill=1e30, base=0,
                                    pattern=[[-1, P]], channel_multiplier=1).then_inc(consts_ready, 1)
            end_phase(pool, 1)

            nc.gpsimd.iota(desc[:, :], pattern=[[-1, E]], base=E, channel_multiplier=0,
                           allow_small_or_imprecise_dtypes=True).then_inc(consts_ready, 1)
            pool.wait_ge(x_spilled, 16)
            pool.wait_ge(xn_ready, 2 * NT)
            nc.gpsimd.memset(accM[:, :, :], 0.0).then_inc(acc_zero, 1)
            pool.wait_ge(aff_stored, 16)
            nc.gpsimd.memset(accD[:, :, :], 0.0).then_inc(acc_zero, 1)
            end_phase(pool, 2)

            for t in range(NT):
                pool.wait_ge(g_parts, t + 1)
                nc.gpsimd.tensor_tensor(out=tc_[:, t, :], in0=ta[:, t % 2, :], in1=tb[:, t % 2, :], op=ALU.add).then_inc(g_sum, 1)
            end_phase(pool, 3)

            for b in range(B):
                pool.wait_ge(k_spun, b + 1)
                for r, part in enumerate((0, 0, 1)):
                    nc.gpsimd.dma_start(KT[r * HD:(r + 1) * HD, b * NG:(b + 1) * NG, :],
                                        k_dram[part, b].rearrange("(g c) n -> c g n", c=HD)).then_inc(kt_loaded, 16)

            def load_queries(t, q_tile):
                for r, part in enumerate((0, 1, 0)):
                    nc.gpsimd.dma_start(QT[r * HD:(r + 1) * HD, t, :, :, :].rearrange("c h g n -> c h (g n)"),
                                        q_tile(part).rearrange("(h c) m -> c h m", c=HD)).then_inc(qt_loaded[t], 16)

            H2 = HD // 2
            for t in range(NT):
                uv = u[:, t % TB, :].rearrange("p (h c) -> p h c", c=HD)
                qv = qb[:, t % 2, :].rearrange("p (h c) -> p h c", c=HD)
                sv = wsin[:, t % TB, :].rearrange("p (h c) -> p h c", c=HD)
                pool.wait_ge(u_ready, t + 1)
                if t >= 2:
                    pool.wait_ge(qs_ready, t - 1)
                nc.gpsimd.tensor_tensor(out=qv[:, :, 0:H2], in0=uv[:, :, H2:HD], in1=sv[:, :, 0:H2], op=ALU.mult)
                nc.gpsimd.tensor_tensor(out=qv[:, :, H2:HD], in0=uv[:, :, 0:H2], in1=sv[:, :, H2:HD], op=ALU.mult).then_inc(qb_ready, 1)
                if 3 <= t < 3 + TB:
                    pool.wait_ge(q_high_stored[(t - 3) % 2], 16 * ((t - 3) // 2 + 1))
                    pool.wait_ge(q_low_stored[(t - 3) % 2], 16 * ((t - 3) // 2 + 1))
                    load_queries(t - 3, lambda part: q_dram[part, t - 3])
            end_phase(pool, 4)
            with pool.Fori(0, B - 1) as b:
                for t in range(TB):
                    pool.wait_ge(s_done, count(b, 2 * NU, 2 * NG * (t + 1)))
                    load_queries(t, lambda part: q_dram[part, bass.ds(b * TB + (TB + t), 1)].rearrange("o p m -> (o p) m"))
            end_phase(pool, 5)

        @block.tensor
        def _(pe):
            mm, turn = nc.tensor.matmul, nc.tensor.transpose

            def three(out_ap, ah, al, bh, bl, start, stop):
                mm(out_ap, ah, bh, start=start, stop=False)
                mm(out_ap, ah, bl, start=False, stop=False)
                return mm(out_ap, al, bh, start=False, stop=stop)

            def prep(k):
                for t in range(NT):
                    pe.wait_ge(xn_ready, NT * k + t + 1)
                    if t >= 2:
                        pe.wait_ge(xt_low, NT * k + t - 1)
                    for d in range(KD):
                        last = turn(ps[:, t % 2, d * P:(d + 1) * P], xn[:, t % 2, d * P:(d + 1) * P], ident[:, :])
                    last.then_inc(xt_turned, 1)

            def gate_up(part, i, j):
                s = step_no(part, i, j)
                w, q, b = j // B % 2, j % 2, j % B
                bs = slice(b * S, (b + 1) * S)
                if j % B == 0:
                    pe.wait_ge(w_low, i * 6 + (3 * (part * HT + j // B) + 2))
                pe.wait_ge(hid_low, s + (CREDIT - 1))
                for m, done in ((0, gate_done), (1, up_done)):
                    for d in range(KD):
                        dsl = slice(d * P, (d + 1) * P)
                        last = three(ps[:, 2 * m + q, :], wh[:, w, m, dsl], wl[:, w, m, dsl], xTh[:, d, bs], xTl[:, d, bs], d == 0, d == KD - 1)
                    last.then_inc(done, 1)

            def down(part, i, j):
                s = step_no(part, i, j)
                w, q = j // B % 2, j % 2
                if j % B == 0:
                    pe.wait_ge(w_low, i * 6 + (3 * (part * HT + j // B) + 3))
                pe.wait_ge(hid_low, s + (CREDIT + 1))
                pe.wait_ge(acc_added, s + CREDIT)
                for t in range(TB):
                    tsl = slice(t * P, (t + 1) * P)
                    last = three(ps[:, 4 + t, :], hidh[:, q, tsl], hidl[:, q, tsl], wh[:, w, 2, :], wl[:, w, 2, :], True, True)
                last.then_inc(out_done, 1)

            def ffn(part, chain_start, chain_end):
                if chain_start:
                    gate_up(part, 0, 0)
                with pe.Fori(0, HT // 2 - 1) as i:
                    for j in range(2 * B):
                        gate_up(part, i, j + 1)
                        down(part, i, j)
                for j in range(2 * B):
                    if j < 2 * B - 1 or not chain_end:
                        gate_up(part, HT // 2 - 1, j + 1)
                    down(part, HT // 2 - 1, j)

            pe.wait_ge(consts_ready, 1)
            pe.sem_inc(out_done, CREDIT)
            for s_ in (s_done, p_turned, pv_done, o_done, proj_done):
                pe.sem_inc(s_, LEAD)
            for b in range(B):
                pe.wait_ge(ctx_low, b + 1)
                three(ps[:, 4, :], wkh[:, :], wkl[:, :], cTh[:, :], cTl[:, :], True, True).then_inc(kv_done, 1)
                pe.wait_ge(kv_biased, b + 1)
                if b:
                    pe.wait_ge(kv_low, b)
                for j in range(TB):
                    last = turn(ps[:, 5, j * P:(j + 1) * P], kvf[:, j * P:(j + 1) * P], ident[:, :])
                last.then_inc(kv_turned, 1)
            prep(0)
            for b in range(B):
                bs = slice(b * S, (b + 1) * S)
                pe.wait_ge(xt_low, TB * (b + 1))
                pe.wait_ge(kv_low, b + 1)
                for j in range(KD):
                    last = three(ps[:, 2, :], kvh[:, TB * b + j, :], kvl[:, TB * b + j, :], xTh[:, j, bs], xTl[:, j, bs], j == 0, j == KD - 1)
                last.then_inc(pkv_done, 1)
                pe.wait_ge(pkv_low, b + 1)
                for i in range(TB):
                    n = TB * b + i
                    if n >= 2:
                        pe.wait_ge(sim_copied, n - 1)
                    isl = slice(i * P, (i + 1) * P)
                    three(ps[:, 6 + n % 2, :], oTh[:, isl], oTl[:, isl], kvTh[:, b, :], kvTl[:, b, :], True, True).then_inc(sim_done, 1)
            end_phase(pe, 1)

            prep(1)
            pe.wait_ge(rw_low, 1)
            pe.wait_ge(xt_low, 2 * NT)
            for b in range(B):
                bs = slice(b * S, (b + 1) * S)
                for d in range(KD):
                    last = three(ps[0:E, 4 + b, :], rwh[:, d, :], rwl[:, d, :], xTh[:, d, bs], xTl[:, d, bs], d == 0, d == KD - 1)
            last.then_inc(lg_done, 1)
            pe.wait_ge(lg_copied, 1)
            for t in range(NT):
                last = turn(ps[:, 2, t * E:(t + 1) * E], lgT[:, t // TB, t % TB * P:(t % TB + 1) * P], ident[0:E, 0:E])
            last.then_inc(lg_turned, 1)
            pe.wait_ge(aff_ready, 1)
            for t in range(NT):
                last = turn(ps[0:E, 4 + t // TB, t % TB * P:(t % TB + 1) * P], lg[:, t, :], ident[:, :])
            last.then_inc(aff_turned, 1)
            pe.wait_ge(aff_copied, 1)
            ffn(0, True, False)
            ffn(1, False, True)
            end_phase(pe, 2)
            end_phase(pe, 3)

            pe.wait_ge(k_ready, 1)
            for b in range(B):
                if b >= 2:
                    pe.wait_ge(k_low, b - 1)
                for t in range(TB):
                    last = turn(ps[:, b % 2, t * P:(t + 1) * P], ka[:, b * TB + t, :], ident[:, :])
                last.then_inc(k_turned, 1)
            pe.wait_ge(k_low, B)
            for t in range(NT):
                pe.wait_ge(qs_ready, t + 1)
                if t >= 2:
                    pe.wait_ge(q_low, t - 1)
                for d in range(KD):
                    last = turn(ps[:, t % 2, d * P:(d + 1) * P], qa[:, t % 2, d * P:(d + 1) * P], ident[:, :])
                last.then_inc(q_turned, 1)
            end_phase(pe, 4)

            def scores(b, n, hp):
                qt, g, db = unit(n)
                L = max(256, (qt + 1) * P)
                pe.wait_ge(exp_done, b * (2 * NU) + (2 * (n - 1) + hp + 1 + LEAD))
                if g == 0 and hp == 0:
                    pe.wait_ge(qt_loaded[qt], b * 48 + 48 * (db + 1))
                for h in (2 * hp, 2 * hp + 1):
                    mm(ps[:, h, 0:L], QT[:, qt, h, g, :],
                       KT[:, bass.ds(b * NG + (db * NG + g), 1), 0:L].rearrange("p o n -> p (o n)"), start=True, stop=True)
                    last = mm(ps[:, h, qt * P:(qt + 1) * P], identb[:, :], maskb[:, :], start=False, stop=True, skip_group_check=True)
                last.then_inc(s_done, 1)

            def bank_free(b, steps, i):
                users = [s_ for s_ in steps[:i] if s_[0] in ("turn", "project")]
                if len(users) >= 2:
                    kind, n, kt = users[-2]
                    if kind == "project":
                        pe.wait_ge(proj_added, count(b, TB, n + 1))
                    else:
                        wait_copied(b, n, kt)
                elif steps is not FIRST:
                    wait_copied(b, LAG - 1, 0)
                    pe.wait_ge(proj_added, count(b, TB, 0))

            def wait_copied(b, n, kt):
                if kt % 2:
                    pe.wait_ge(p_copied_dve, count(b, DVE_PER_SEQ, DVE_KEYS.index((n, kt)) + 1))
                else:
                    pe.wait_ge(p_copied_act, count(b, ACT_PER_SEQ, ACT_KEYS.index((n, kt)) + 1))

            def turn_p(b, n, kt, bank):
                if kt == 0:
                    pe.wait_ge(exp_done, count(b, 2 * NU, 2 * n + 2))
                for h in range(HG):
                    last = turn(ps[:, bank, h * P:(h + 1) * P], Pr[:, n % 2, h, kt * P:(kt + 1) * P], ident[:, :])
                last.then_inc(p_turned, 1)

            def values(b, n, kt):
                qt, g, _ = unit(n)
                wait_copied(b, n, kt)
                if kt == 0:
                    pe.wait_ge(attn_ready, count(b, NU, n - 1))
                if (n % NU, kt) == (0, 0):
                    pe.wait_ge(vb_ready, b + (1 + n // NU))
                for h in range(HG):
                    last = mm(ps[h * HD:(h + 1) * HD, 6 + n % 2, 0:P], Vb[:, kt, g * HD:(g + 1) * HD],
                              PT[:, KEYS.index((n, kt)) % 4, h * P:(h + 1) * P], start=(kt == 0), stop=end_of_unit(n, kt))
                last.then_inc(pv_done, 1)
                if end_of_unit(n, kt):
                    pe.wait_ge(rinv_ready, count(b, NU, n + 1))
                    turn(ps[:, 6 + n % 2, P:2 * P], rE[:, n % 4, :, :].rearrange("p h c -> p (h c)"), ident[:, :]).then_inc(o_done, 1)

            def project(b, qt, bank):
                pe.wait_ge(attn_low, count(b, TB, qt + 1))
                for g in range(NG):
                    last = three(ps[:, bank, :], aTh[:, qt % 2, g, :], aTl[:, qt % 2, g, :], woh[:, g, :], wol[:, g, :], g == 0, g == NG - 1)
                last.then_inc(proj_done, 1)

            def attend(b, steps):
                for i, (kind, n, k) in enumerate(steps):
                    if kind == "scores":
                        scores(b, n, k)
                    elif kind == "values":
                        values(b, n, k)
                    elif kind == "turn":
                        bank_free(b, steps, i)
                        turn_p(b, n, k, bank_of(steps, i))
                    elif kind == "project":
                        bank_free(b, steps, i)
                        project(b, n, bank_of(steps, i))

            pe.wait_ge(kt_loaded, 16 * 3 * B)
            scores(0, 0, 0)
            scores(0, 0, 1)
            attend(0, FIRST)
            with pe.Fori(0, B - 1) as b:
                attend(b, BODY)
            attend(B - 1, LAST)
            end_phase(pe, 5)

            prep(2)
            pe.wait_ge(xt_low, 3 * NT)
            ffn(2, True, True)

        @block.scalar
        def _(act):
            func = nc.scalar.activation
            chained, roots = [0], [0]

            def link(ins):
                chained[0] += 1
                ins.then_inc(act_chain, 1)
                act.wait_ge(act_chain, chained[0])

            def root():
                roots[0] += 1
                act.wait_ge(root_asked, roots[0])
                func(sd[:, :], vv[:, :], ACT.Sqrt).then_inc(root_done, 1)

            def prep(k):
                root()
                for t in range(NT):
                    act.wait_ge(xt_turned, NT * k + t + 1)
                    func(xTh[:, :, t * P:(t + 1) * P], ps[:, t % 2, :].rearrange("p (k n) -> p k n", k=KD), ACT.Copy).then_inc(xt_high, 1)

            def split_high(part, T, w, m):
                if m == 0:
                    act.wait_ge(out_done, T * B + (CREDIT - B))
                if part < 2 and m < 2:
                    for d in range(KD):
                        dsl = slice(d * P, (d + 1) * P)
                        last = func(wh[:, w, m, dsl], raw[:, w, m, dsl], ACT.Copy, scale=rnp[:, part, d:d + 1])
                else:
                    last = func(wh[:, w, m, :], raw[:, w, m, :], ACT.Copy)
                last.then_inc(w_high, 1)

            def step(part, i, j, chain_end):
                s, q = step_no(part, i, j), j % 2
                act.wait_ge(gate_done, s + 1)
                act.wait_ge(hid_ready, s + (CREDIT - 1))
                func(act_o[:, q, :], ps[:, q, :], ACT.Silu if part == 2 else ACT.Gelu_apprx_tanh).then_inc(act_ready, 1)
                nxt = next_tile(part, i, j, chain_end)
                if nxt:
                    p2, T, w = nxt
                    if j % B == 1:
                        act.wait_ge(w_loaded[w], i * 16 + 16 * ((part * HT + j // B + 1) // 2 + 1))
                    split_high(p2, T, w, j % B - 1)
                act.wait_ge(hid_ready, s + (CREDIT + 1))
                act.wait_ge(out_done, s + (CREDIT - 1))
                func(hidh[:, q, :], hid[:, q, :], ACT.Copy).then_inc(hid_high, 1)

            def ffn(part, chain_start, chain_end):
                if chain_start:
                    act.wait_ge(w_loaded[0], 16 * (part * HT // 2 + 1))
                    for m in range(3):
                        split_high(part, part * HT, 0, m) if part else first_split(m)
                with act.Fori(0, HT // 2 - 1) as i:
                    for j in range(2 * B):
                        step(part, i, j, chain_end)
                for j in range(2 * B):
                    step(part, HT // 2 - 1, j, chain_end)

            def first_split(m):
                if m < 2:
                    for d in range(KD):
                        dsl = slice(d * P, (d + 1) * P)
                        last = func(wh[:, 0, m, dsl], raw[:, 0, m, dsl], ACT.Copy, scale=rnp[:, 0, d:d + 1])
                else:
                    last = func(wh[:, 0, m, :], raw[:, 0, m, :], ACT.Copy)
                last.then_inc(w_high, 1)

            act.wait_ge(small_loaded, 64)
            func(wkh[:, :], wk32[:, :], ACT.Copy).then_inc(wk_high, 1)
            for b in range(B):
                act.wait_ge(ctxT_loaded, 16 * (b + 1))
                if b:
                    act.wait_ge(kv_done, b)
                func(cTh[:, :], cT32[:, :], ACT.Copy).then_inc(ctx_high, 1)
                act.wait_ge(kv_done, b + 1)
                if b:
                    act.wait_ge(kv_turned, b)
                    act.wait_ge(kvT_low, b)
                func(kvf[:, :], ps[:, 4, :], ACT.Identity, bias=bk[:, 0:1]).then_inc(kv_biased, 1)
                act.wait_ge(kv_biased, b + 1)
                func(kvTh[:, b, :], kvf[:, :], ACT.Copy).then_inc(kvT_high, 1)
                act.wait_ge(kv_turned, b + 1)
                func(kvh[:, TB * b:TB * (b + 1), :], ps[:, 5, :].rearrange("p (j c) -> p j c", c=C), ACT.Copy).then_inc(kv_high, 1)
            prep(0)
            for b in range(B):
                act.wait_ge(pkv_done, b + 1)
                if b:
                    act.wait_ge(sim_done, TB * b)
                func(oTh[:, :], ps[:, 2, :], ACT.Copy).then_inc(pkv_high, 1)
                for i in range(TB):
                    n = TB * b + i
                    act.wait_ge(sim_done, n + 1)
                    func(sim[:, n, :], ps[:, 6 + n % 2, :], ACT.Copy).then_inc(sim_copied, 1)
            root()
            for t in range(NT):
                act.wait_ge(a_weighed, t + 1)
                if t >= 2:
                    act.wait_ge(a_exp, t - 1)
                func(vb[:, t % 2, :], va[:, t % 2, :], ACT.Copy, scale=rs[:, t:t + 1]).then_inc(a_scaled, 1)
                act.wait_ge(a_max, t + 1)
                if t >= 2:
                    act.wait_ge(a_added, t - 1)
                func(vc[:, t % 2, :], vb[:, t % 2, :], ACT.Exp, bias=nma[:, t:t + 1], accum_out=sma[:, t:t + 1]).then_inc(a_exp, 1)
            end_phase(act, 1)

            prep(1)
            act.wait_ge(rw_scaled, 1)
            func(rwh[:, :, :], rws[:, :, :], ACT.Copy).then_inc(rw_high, 1)
            act.wait_ge(lg_done, 1)
            func(lgT, ps[0:E, 4:8, :], ACT.Copy).then_inc(lg_copied, 1)
            act.wait_ge(aff_asked, 1)
            func(key[:, :, :], lg2[:, :, :], ACT.Exp).then_inc(aff_exp, 1)
            act.wait_ge(aff_turned, 1)
            func(lgT, ps[0:E, 4:8, :], ACT.Copy).then_inc(aff_copied, 1)
            act.wait_ge(small_loaded, 128)
            ffn(0, True, False)
            ffn(1, False, True)
            end_phase(act, 2)

            for k, a in ((0, accD), (1, accM)):
                for t in range(NT):
                    link(func(sq[:, :], a[:, t, :], ACT.Square, accum_out=ssq[:, k, t:t + 1]))
            act.sem_inc(squares_ready, 1)
            root()
            root()
            for t in range(NT):
                act.wait_ge(g_sum, t + 1)
                link(func(sq[:, :], tc_[:, t, :], ACT.Square, accum_out=ssq[:, 2, t:t + 1]))
            act.sem_inc(squares_ready, 1)
            root()
            end_phase(act, 3)

            act.wait_ge(b_loaded, 16 * 8)
            for t in range(NT):
                link(func(ksq[:, :], V[:, t, :], ACT.Square, accum_out=kss[:, t:t + 1]))
            act.sem_inc(squares_ready, 1)
            root()
            func(woh[:, :, :], wo32[:, :, :], ACT.Copy).then_inc(wo_high, 1)
            for b in range(B):
                act.wait_ge(k_turned, b + 1)
                if b >= 2:
                    act.wait_ge(k_spun, b - 1)
                func(th[:, b % 2, :], ps[:, b % 2, :], ACT.Copy).then_inc(k_high, 1)
            root()
            act.wait_ge(rows_scaled, 1)
            act.wait_ge(wo_low, 1)
            act.wait_ge(k_spun, B)

            def query_high(t):
                act.wait_ge(q_turned, t + 1)
                if t >= 2:
                    act.wait_ge(q_high_stored[t % 2], 16 * (t // 2))
                func(th[:, t % 2, :], ps[:, t % 2, :], ACT.Copy).then_inc(q_high, 1)

            for t in range(NT):
                if t >= TB:
                    act.wait_ge(qs_ready, t - TB + 1)
                func(u[:, t % TB, :], x[:, t, :], ACT.Identity, bias=nmr[:, t:t + 1], scale=rs[:, t:t + 1]).then_inc(u_ready, 1)
                if t >= 2:
                    query_high(t - 2)
            query_high(NT - 2)
            query_high(NT - 1)
            for s_ in (exp_done, attn_high, p_copied_act, rt_copied):
                act.sem_inc(s_, LEAD)
            end_phase(act, 4)

            def exponential(b, n, hp):
                act.wait_ge(min_ready, count(b, 2 * NU, 2 * n + hp + 1))
                if hp == 0:
                    act.wait_ge(p_turned, count(b, PER_SEQ, KEYS.index((n - 1, 0)) if n else 0))
                    act.wait_ge(rinv_ready, count(b, NU, n - 3))
                for h in (2 * hp, 2 * hp + 1):
                    last = func(Pr[:, n % 2, h, 0:(unit(n)[0] + 1) * P], ps[:, h, 0:(unit(n)[0] + 1) * P], ACT.Exp,
                                bias=mnb[:, n % 2, h:h + 1], scale=-1.0, accum_out=smb[:, n % 4, h:h + 1])
                last.then_inc(exp_done, 1)

            def copy_p(b, n, kt, bank):
                act.wait_ge(p_turned, count(b, PER_SEQ, KEYS.index((n, kt)) + 1))
                act.wait_ge(pv_done, count(b, PER_SEQ, KEYS.index((n, kt)) - 3))
                func(PT[:, KEYS.index((n, kt)) % 4, :], ps[:, bank, :], ACT.Copy).then_inc(p_copied_act, 1)

            def copy_inverses(b, n):
                act.wait_ge(o_done, count(b, NU, n + 1))
                act.wait_ge(attn_ready, count(b, NU, n - 1))
                func(rT[:, n % 2, :], ps[:, 6 + n % 2, P:2 * P], ACT.Copy).then_inc(rt_copied, 1)

            def attend(b, steps):
                due, finished = [], []
                for i, (kind, n, k) in enumerate(steps):
                    if kind == "scores":
                        due.append((n, k))
                    elif kind == "turn":
                        if k % 2 == 0:
                            copy_p(b, n, k, bank_of(steps, i))
                            if due:
                                exponential(b, *due.pop(0))
                        if end_of_unit(n, k):
                            while due:
                                exponential(b, *due.pop(0))
                        while finished:
                            copy_inverses(b, finished.pop(0))
                    elif kind == "values":
                        if end_of_unit(n, k):
                            finished.append(n)
                    elif kind == "split":
                        while finished:
                            copy_inverses(b, finished.pop(0))
                        act.wait_ge(attn_ready, count(b, NU, NG * (n + 1)))
                        act.wait_ge(proj_done, count(b, TB, n - 1))
                        func(aTh[:, n % 2, :, :], aT[:, n % 2, :, :], ACT.Copy).then_inc(attn_high, 1)

            exponential(0, 0, 0)
            exponential(0, 0, 1)
            attend(0, FIRST)
            with act.Fori(0, B - 1) as b:
                attend(b, BODY)
            attend(B - 1, LAST)
            end_phase(act, 5)

            prep(2)
            ffn(2, True, True)

        @block.vector
        def _(dve):
            V_ = nc.vector
            chained, roots = [0], [0]

            def link(ins):
                chained[0] += 1
                ins.then_inc(dve_chain, 1)
                dve.wait_ge(dve_chain, chained[0])

            def rsqrt(dst):
                roots[0] += 1
                dve.sem_inc(root_asked, 1)
                dve.wait_ge(root_done, roots[0])
                link(V_.reciprocal(r0[:, :], sd[:, :]))
                link(V_.tensor_tensor(out=r1[:, :], in0=r0[:, :], in1=r0[:, :], op=ALU.mult))
                link(V_.tensor_tensor(out=r1[:, :], in0=r1[:, :], in1=vv[:, :], op=ALU.mult))
                link(V_.tensor_scalar(r1[:, :], r1[:, :], -0.5, 1.5, ALU.mult, ALU.add))
                link(V_.tensor_tensor(out=dst, in0=r0[:, :], in1=r1[:, :], op=ALU.mult))

            def deviations(mul, add, factor=None):
                for t in range(NT):
                    last = V_.bn_aggr(mv[:, t, :], bst[:, t, :])
                link(last)
                link(V_.tensor_scalar(vv[:, :], mv[:, :, 1], mul, add, ALU.mult, ALU.add))
                rsqrt(rs[:, :])
                if factor is not None:
                    link(V_.tensor_scalar(rs[:, :], rs[:, :], factor, None, ALU.mult))
                link(V_.scalar_tensor_tensor(out=nmr[:, :], in0=mv[:, :, 0], scalar=-1.0, in1=rs[:, :], op0=ALU.mult, op1=ALU.mult))

            def x_stats(arrivals=None):
                for t in range(NT):
                    if arrivals and t % TB == 0:
                        dve.wait_ge(arrivals[t // TB], 16)
                    last = V_.bn_stats(bst[:, t, :], x[:, t, :])
                link(last)

            def prep(k):
                def low(t):
                    dve.wait_ge(xt_high, NT * k + t + 1)
                    V_.tensor_tensor(out=xTl[:, :, t * P:(t + 1) * P], in0=ps[:, t % 2, :].rearrange("p (k n) -> p k n", k=KD),
                                     in1=xTh[:, :, t * P:(t + 1) * P].bitcast(F32), op=ALU.subtract).then_inc(xt_low, 1)
                for t in range(NT):
                    if t >= 2:
                        dve.wait_ge(xt_turned, NT * k + t - 1)
                    V_.tensor_scalar(xn[:, t % 2, :], x[:, t, :], mv[:, t, 0:1], rs[:, t:t + 1], ALU.subtract, ALU.mult).then_inc(xn_ready, 1)
                    if t >= 1:
                        low(t - 1)
                low(NT - 1)

            def split_low(part, T, w, m):
                dve.wait_ge(w_high, T * 3 + (m + 1))
                if part < 2 and m < 2:
                    for d in range(KD):
                        dsl = slice(d * P, (d + 1) * P)
                        last = V_.scalar_tensor_tensor(out=wl[:, w, m, dsl], in0=raw[:, w, m, dsl], scalar=rnp[:, part, d:d + 1],
                                                       in1=wh[:, w, m, dsl].bitcast(F32), op0=ALU.mult, op1=ALU.subtract)
                else:
                    last = V_.tensor_tensor(out=wl[:, w, m, :], in0=raw[:, w, m, :], in1=wh[:, w, m, :].bitcast(F32), op=ALU.subtract)
                last.then_inc(w_low, 1)

            def hidden(part, i, j, nxt):
                s, q, b = step_no(part, i, j), j % 2, j % B
                dve.wait_ge(act_ready, s + 1)
                if part == 1:
                    if j // B % 2 == 0:
                        dve.wait_ge(aff_loaded[b], i * 16 + 16 * (j // (2 * B) + 1))
                    V_.tensor_tensor(out=act_o[:, q, :], in0=act_o[:, q, :], in1=affB[:, b, :], op=ALU.mult).then_inc(aff_applied, 1)
                    dve.wait_ge(aff_applied, step_no(0, i, j) + 1)
                dve.wait_ge(up_done, s + 1)
                dve.wait_ge(hid_low, s + (CREDIT - 1))
                V_.tensor_tensor(out=hid[:, q, :], in0=act_o[:, q, :], in1=ps[:, 2 + q, :], op=ALU.mult).then_inc(hid_ready, 1)
                if nxt:
                    split_low(nxt[0], nxt[1], nxt[2], j % B - 1)
                dve.wait_ge(hid_high, s + 1)
                V_.tensor_tensor(out=hidl[:, q, :], in0=hid[:, q, :], in1=hidh[:, q, :].bitcast(F32), op=ALU.subtract).then_inc(hid_low, 1)

            def add(part, i, j):
                s, b = step_no(part, i, j), j % B
                acc = (accD, accM, x)[part][:, TB * b:TB * (b + 1), :]
                dve.wait_ge(out_done, s + (CREDIT + 1))
                dve.wait_ge(acc_added, s + (CREDIT - 1))
                V_.tensor_tensor(out=acc, in0=acc, in1=ps[:, 4:8, :], op=ALU.add).then_inc(acc_added, 1)

            def ffn(part, chain_start, chain_end):
                if chain_start:
                    for m in range(3):
                        split_low(part, part * HT, 0, m)
                    hidden(part, 0, 0, None)
                with dve.Fori(0, HT // 2 - 1) as i:
                    for j in range(2 * B):
                        hidden(part, i, j + 1, next_tile(part, i, j + 1, chain_end))
                        add(part, i, j)
                i = HT // 2 - 1
                for j in range(2 * B):
                    if j < 2 * B - 1:
                        hidden(part, i, j + 1, next_tile(part, i, j + 1, chain_end))
                    elif not chain_end:
                        hidden(part + 1, 0, 0, None)
                    add(part, i, j)

            for s_, k in ((hid_low, CREDIT), (acc_added, CREDIT), (hid_ready, CREDIT),
                          *((s_, LEAD) for s_ in (min_ready, rinv_ready, p_copied_dve, attn_ready, attn_low, proj_added))):
                dve.sem_inc(s_, k)

            dve.wait_ge(wk_high, 1)
            V_.tensor_tensor(out=wkl[:, :], in0=wk32[:, :], in1=wkh[:, :].bitcast(F32), op=ALU.subtract)
            for b in range(B):
                dve.wait_ge(ctx_high, b + 1)
                V_.tensor_tensor(out=cTl[:, :], in0=cT32[:, :], in1=cTh[:, :].bitcast(F32), op=ALU.subtract).then_inc(ctx_low, 1)
                dve.wait_ge(kvT_high, b + 1)
                V_.tensor_tensor(out=kvTl[:, b, :], in0=kvf[:, :], in1=kvTh[:, b, :].bitcast(F32), op=ALU.subtract).then_inc(kvT_low, 1)
                dve.wait_ge(kv_high, b + 1)
                V_.tensor_tensor(out=kvl[:, TB * b:TB * (b + 1), :], in0=ps[:, 5, :].rearrange("p (j c) -> p j c", c=C),
                                 in1=kvh[:, TB * b:TB * (b + 1), :].bitcast(F32), op=ALU.subtract).then_inc(kv_low, 1)
            x_stats(x_loaded)
            deviations(1.0, LN_EPS)
            prep(0)
            for b in range(B):
                dve.wait_ge(pkv_high, b + 1)
                V_.tensor_tensor(out=oTl[:, :], in0=ps[:, 2, :], in1=oTh[:, :].bitcast(F32), op=ALU.subtract).then_inc(pkv_low, 1)
                for i in range(TB):
                    n = TB * b + i
                    dve.wait_ge(sim_copied, n + 1)
                    last = V_.bn_stats(bst[:, n, :], sim[:, n, :])
            link(last)
            deviations(SIM_SCALE * SIM_SCALE, 1e-6, SIM_SCALE)

            def a_residual(t):
                dve.wait_ge(a_exp, t + 1)
                link(V_.reciprocal(rca[:, t:t + 1], sma[:, t:t + 1]))
                V_.scalar_tensor_tensor(out=x[:, t, :], in0=vc[:, t % 2, :], scalar=rca[:, t:t + 1], in1=x[:, t, :],
                                        op0=ALU.mult, op1=ALU.add).then_inc(a_added, 1)

            for t in range(NT):
                if t >= 2:
                    dve.wait_ge(a_scaled, t - 1)
                V_.scalar_tensor_tensor(out=va[:, t % 2, :], in0=sim[:, t, :], scalar=mv[:, t, 0:1], in1=gammaB[:, :],
                                        op0=ALU.subtract, op1=ALU.mult).then_inc(a_weighed, 1)
                if t >= 1:
                    a_residual(t - 1)
                dve.wait_ge(a_scaled, t + 1)
                link(V_.tensor_tensor_reduce(vb[:, t % 2, :], vb[:, t % 2, :], betaB[:, :], 1.0, -3.0e38, ALU.add, ALU.max, mxa[:, t:t + 1]))
                V_.tensor_scalar(nma[:, t:t + 1], mxa[:, t:t + 1], -1.0, None, ALU.mult).then_inc(a_max, 1)
            a_residual(NT - 1)
            dve.wait_ge(a_added, NT)
            end_phase(dve, 1)

            x_stats()
            deviations(1.0 + RMS0_EPS, RMS0_EPS * LN_EPS)
            prep(1)
            dve.wait_ge(small_loaded, 128)
            link(V_.tensor_scalar(rsc[:, :], rsc[:, :], float(D) ** -0.5, None, ALU.mult))
            for d in range(KD):
                last = V_.tensor_scalar(rws[:, d, :], rw32[:, d, :], rsc[:, d:d + 1], None, ALU.mult)
            last.then_inc(rw_scaled, 1)
            dve.wait_ge(rw_high, 1)
            V_.tensor_tensor(out=rwl[:, :, :], in0=rws[:, :, :], in1=rwh[:, :, :].bitcast(F32), op=ALU.subtract).then_inc(rw_low, 1)
            dve.wait_ge(lg_turned, 1)
            dve.wait_ge(consts_ready, 2)

            def over_e(a):
                return a.unsqueeze(2).broadcast_to((P, NT, E))

            descB = desc[:, :].unsqueeze(1).broadcast_to((P, NT, E))
            link(V_.tensor_copy(lg[:, :, :], ps[:, 2, 0:NT * E].rearrange("p (t e) -> p t e", e=E)))

            def largest(src, m, oh):
                link(V_.tensor_reduce(m[:, :], src[:, :, :], AX.X, ALU.max))
                link(V_.tensor_tensor(out=key[:, :, :], in0=src[:, :, :], in1=over_e(m[:, :]), op=ALU.is_equal))
                link(V_.tensor_tensor(out=key[:, :, :], in0=key[:, :, :], in1=descB, op=ALU.mult))
                link(V_.tensor_reduce(pk[:, :], key[:, :, :], AX.X, ALU.max))
                link(V_.tensor_tensor(out=oh[:, :, :], in0=key[:, :, :], in1=over_e(pk[:, :]), op=ALU.is_equal))

            largest(lg, m1, oh1)
            link(V_.scalar_tensor_tensor(out=lg2[:, :, :], in0=oh1[:, :, :], scalar=-3.0e38, in1=lg[:, :, :], op0=ALU.mult, op1=ALU.add))
            largest(lg2, m2, oh2)
            V_.tensor_tensor(out=lg2[:, :, :], in0=lg[:, :, :], in1=over_e(m1[:, :]), op=ALU.subtract).then_inc(aff_asked, 1)
            link(V_.tensor_tensor(out=oh1[:, :, :], in0=oh1[:, :, :], in1=oh2[:, :, :], op=ALU.add))
            dve.wait_ge(aff_exp, 1)
            link(V_.tensor_tensor(out=key[:, :, :], in0=key[:, :, :], in1=oh1[:, :, :], op=ALU.mult))
            link(V_.tensor_reduce(m1[:, :], key[:, :, :], AX.X, ALU.add))
            link(V_.reciprocal(m2[:, :], m1[:, :]))
            link(V_.tensor_tensor(out=key[:, :, :], in0=key[:, :, :], in1=over_e(m2[:, :]), op=ALU.mult))
            V_.tensor_tensor(out=lg[:, :, :], in0=key[:, :, :], in1=pesB[:, :].unsqueeze(1).broadcast_to((P, NT, E)), op=ALU.mult).then_inc(aff_ready, 1)
            dve.wait_ge(acc_zero, 2)
            ffn(0, True, False)
            ffn(1, False, True)
            end_phase(dve, 2)

            dve.wait_ge(small_loaded, 176)
            dve.wait_ge(squares_ready, 1)
            for k in range(2):
                link(V_.tensor_scalar(vv[:, :], ssq[:, k, :], 1.0 / D, RMS0_EPS, ALU.mult, ALU.add))
                rsqrt(rr[:, k, :])
            for t in range(NT):
                if t >= 2:
                    dve.wait_ge(g_sum, t - 1)
                V_.scalar_tensor_tensor(out=ta[:, t % 2, :], in0=accD[:, t, :], scalar=rr[:, 0, t:t + 1], in1=postB[:, 0, :], op0=ALU.mult, op1=ALU.mult)
                V_.scalar_tensor_tensor(out=tb[:, t % 2, :], in0=accM[:, t, :], scalar=rr[:, 1, t:t + 1], in1=postB[:, 1, :],
                                        op0=ALU.mult, op1=ALU.mult).then_inc(g_parts, 1)
            dve.wait_ge(squares_ready, 2)
            link(V_.tensor_scalar(vv[:, :], ssq[:, 2, :], 1.0 / D, RMS0_EPS, ALU.mult, ALU.add))
            rsqrt(rr[:, 2, :])
            for t in range(NT):
                link(V_.scalar_tensor_tensor(out=ta[:, t % 2, :], in0=tc_[:, t, :], scalar=rr[:, 2, t:t + 1], in1=postB[:, 2, :], op0=ALU.mult, op1=ALU.mult))
                dve.wait_ge(xr_loaded[t % 4], 16 * (t // 4 + 1))
                V_.tensor_tensor(out=x[:, t, :], in0=ta[:, t % 2, :], in1=xr[:, t % 4, :], op=ALU.add).then_inc(g_added, 1)
            dve.wait_ge(g_added, NT)
            end_phase(dve, 3)

            dve.wait_ge(b_loaded, 16 * 8)
            link(V_.tensor_scalar(qwB[:, :, :], qwB[:, :, :], -HEAD_SCALE, None, ALU.mult))
            for t in range(TB):
                for w_, c_, s_, n in ((qwB, wcos, wsin, NH), (kwB, kcos, ksin, NG)):
                    for k, o_, tab in ((0, c_, cosB), (1, s_, sinB)):
                        last = V_.tensor_tensor(out=o_[:, t, :].rearrange("p (h c) -> p h c", c=HD), in0=w_[:, k, :].rearrange("p (h c) -> p h c", c=HD),
                                                in1=tab[:, t:t + 1, :].broadcast_to((P, n, HD)), op=ALU.mult)
            link(last)
            dve.wait_ge(squares_ready, 3)
            link(V_.tensor_scalar(vv[:, :], kss[:, :], 1.0 / C, RMS1_EPS, ALU.mult, ALU.add))
            rsqrt(rs[:, :])
            link(V_.tensor_tensor(out=ku[:, :, :], in0=V[:, :, :], in1=rs[:, :].unsqueeze(2).broadcast_to((P, NT, C)), op=ALU.mult))
            H2 = HD // 2
            for b in range(B):
                bt = slice(b * TB, (b + 1) * TB)
                V_.tensor_tensor(out=ka[:, bt, :], in0=ku[:, bt, :], in1=kcos[:, :, :], op=ALU.mult)
                for t in range(TB):
                    kuv, kbv = (a.rearrange("p (g c) -> p g c", c=HD) for a in (ku[:, b * TB + t, :], kb[:, t, :]))
                    ksv = ksin[:, t, :].rearrange("p (g c) -> p g c", c=HD)
                    V_.tensor_tensor(out=kbv[:, :, 0:H2], in0=kuv[:, :, H2:HD], in1=ksv[:, :, 0:H2], op=ALU.mult)
                    last = V_.tensor_tensor(out=kbv[:, :, H2:HD], in0=kuv[:, :, 0:H2], in1=ksv[:, :, H2:HD], op=ALU.mult)
                link(last)
                last = V_.tensor_tensor(out=ka[:, bt, :], in0=ka[:, bt, :], in1=kb[:, :, :], op=ALU.add)
                if b < B - 1:
                    link(last)
            last.then_inc(k_ready, 1)
            dve.wait_ge(wo_high, 1)
            V_.tensor_tensor(out=wol[:, :, :], in0=wo32[:, :, :], in1=woh[:, :, :].bitcast(F32), op=ALU.subtract).then_inc(wo_low, 1)
            for b in range(B):
                dve.wait_ge(k_high, b + 1)
                if b >= 2:
                    dve.wait_ge(k_spun, b - 1)
                V_.tensor_tensor(out=tl[:, b % 2, :], in0=ps[:, b % 2, :], in1=th[:, b % 2, :].bitcast(F32), op=ALU.subtract).then_inc(k_low, 1)
            x_stats()
            deviations(1.0 + RMS1_EPS, RMS1_EPS * LN_EPS)
            dve.sem_inc(rows_scaled, 1)

            def query_low(t):
                dve.wait_ge(q_high, t + 1)
                if t >= 2:
                    dve.wait_ge(q_low_stored[t % 2], 16 * (t // 2))
                V_.tensor_tensor(out=tl[:, t % 2, :], in0=ps[:, t % 2, :], in1=th[:, t % 2, :].bitcast(F32), op=ALU.subtract).then_inc(q_low, 1)

            dve.wait_ge(k_spun, B)
            for t in range(NT):
                dve.wait_ge(u_ready, t + 1)
                if t >= 2:
                    dve.wait_ge(q_turned, t - 1)
                V_.tensor_tensor(out=qa[:, t % 2, :], in0=u[:, t % TB, :], in1=wcos[:, t % TB, :], op=ALU.mult).then_inc(qa_ready, 1)
                if t >= 2:
                    query_low(t - 2)
                dve.wait_ge(qa_ready, t + 1)
                dve.wait_ge(qb_ready, t + 1)
                V_.tensor_tensor(out=qa[:, t % 2, :], in0=qa[:, t % 2, :], in1=qb[:, t % 2, :], op=ALU.add).then_inc(qs_ready, 1)
            query_low(NT - 2)
            query_low(NT - 1)
            end_phase(dve, 4)

            def minimum(b, n, hp):
                dve.wait_ge(s_done, count(b, 2 * NU, 2 * n + hp + 1))
                V_.tensor_reduce(mnb[:, n % 2, 2 * hp:2 * hp + 2], ps[:, 2 * hp:2 * hp + 2, 0:(unit(n)[0] + 1) * P], AX.X, ALU.min).then_inc(min_ready, 1)

            def inverse(b, n):
                dve.wait_ge(exp_done, count(b, 2 * NU, 2 * n + 2))
                dve.wait_ge(o_done, count(b, NU, n - 3))
                V_.reciprocal(rE[:, n % 4, :, :], smb[:, n % 4, :].unsqueeze(2).broadcast_to((P, HG, HD))).then_inc(rinv_ready, 1)

            def normed(b, n):
                qt, g, _ = unit(n)
                if g == 0:
                    dve.wait_ge(attn_low, count(b, TB, n // NG - 1))
                dve.wait_ge(rt_copied, count(b, NU, n + 1))
                V_.tensor_tensor(out=aT[:, qt % 2, g, :], in0=ps[:, 6 + n % 2, 0:P], in1=rT[:, n % 2, :], op=ALU.mult).then_inc(attn_ready, 1)

            def copy_p(b, n, kt, bank):
                dve.wait_ge(p_turned, count(b, PER_SEQ, KEYS.index((n, kt)) + 1))
                dve.wait_ge(pv_done, count(b, PER_SEQ, KEYS.index((n, kt)) - 3))
                V_.tensor_copy(PT[:, KEYS.index((n, kt)) % 4, :], ps[:, bank, :]).then_inc(p_copied_dve, 1)

            def attend(b, steps):
                finished = []
                for i, (kind, n, k) in enumerate(steps):
                    if kind == "scores":
                        minimum(b, n, k)
                        if k == 0:
                            inverse(b, n - 1)
                        if (n, k) == (NU + 2, 0):
                            dve.wait_ge(pv_done, count(b, PER_SEQ, PER_SEQ))
                            V_.tensor_copy(Vb[:, :, :], V[:, bass.ds(b * TB + TB, TB), :]).then_inc(vb_ready, 1)
                    elif kind == "values":
                        if end_of_unit(n, k):
                            finished.append(n)
                    elif kind == "turn":
                        if steps is LAST and (n, k) == (NU - 1, 0):
                            inverse(b, n)
                        if k % 2 == 1:
                            copy_p(b, n, k, bank_of(steps, i))
                        while finished:
                            normed(b, finished.pop(0))
                    elif kind == "split":
                        while finished:
                            normed(b, finished.pop(0))
                        dve.wait_ge(attn_high, count(b, TB, n + 1))
                        V_.tensor_tensor(out=aTl[:, n % 2, :, :], in0=aT[:, n % 2, :, :], in1=aTh[:, n % 2, :, :].bitcast(F32),
                                         op=ALU.subtract).then_inc(attn_low, 1)
                    elif kind == "project":
                        dve.wait_ge(proj_done, count(b, TB, n + 1))
                        row = x[:, bass.ds(b * TB + n, 1), :].rearrange("p o d -> p (o d)")
                        V_.tensor_tensor(out=row, in0=row, in1=ps[:, bank_of(steps, i), :], op=ALU.add).then_inc(proj_added, 1)

            V_.tensor_copy(Vb[:, :, :], V[:, 0:TB, :]).then_inc(vb_ready, 1)
            minimum(0, 0, 0)
            minimum(0, 0, 1)
            attend(0, FIRST)
            with dve.Fori(0, B - 1) as b:
                attend(b, BODY)
            attend(B - 1, LAST)
            dve.wait_ge(proj_added, count(B, TB, 0))
            end_phase(dve, 5)

            x_stats()
            deviations(1.0, LN_EPS)
            prep(2)
            ffn(2, True, True)


def kernel(**inputs):
    import numpy as np
    import concourse.bacc as bacc
    from concourse.bass_utils import run_bass_kernel_spmd

    def a(name):
        return np.asarray(inputs[name])

    def tiles(gate, up, down):
        n = down.shape[0] // P
        cols = [w.reshape(-1, P, n, P).transpose(2, 1, 0, 3).reshape(n, P, 1, -1) for w in (gate, up)]
        return np.concatenate([*cols, down.reshape(n, P, 1, -1)], axis=2)

    we = [a("L0_ffn_we_" + n) for n in ("gate", "up", "down")]
    ffn_w = np.concatenate([
        tiles(a("L0_ffn_w_gate"), a("L0_ffn_w_up"), a("L0_ffn_w_down")),
        tiles(we[0].transpose(1, 0, 2).reshape(512, -1), we[1].transpose(1, 0, 2).reshape(512, -1), we[2].reshape(-1, 512)),
        tiles(a("L1_ffn_w_gate").T, a("L1_ffn_w_up").T, a("L1_ffn_w_down").T)])

    HD, T = 32, 512
    freq = (np.float32(1.0) / np.float32(10000.0) ** (np.arange(0, HD, 2, dtype=np.float32) / np.float32(HD))).astype(np.float32)
    angle = np.outer(np.arange(T, dtype=np.float32), freq).astype(np.float32)
    cos = np.cos(np.concatenate([angle, angle], -1)).astype(np.float32)
    sin = np.concatenate([-np.sin(angle), np.sin(angle)], -1).astype(np.float32)

    def with_halves_swapped(w):
        return np.stack([w, w.reshape(-1, 2, HD // 2)[:, ::-1].reshape(-1)])

    def columns(w):
        return w.reshape(-1, P).T

    arrays = {
        "x": a("x"), "ctx": a("ctx_512"), "ctxT": a("ctx_512").reshape(-1, 128).T, "wkT": a("L0_xattn_W_k").T,
        "bk": a("L0_xattn_b_k"), "gamma": a("L0_xattn_ln_gamma")[None], "beta": a("L0_xattn_ln_beta")[None],
        "ffn_w": ffn_w, "rn_pre": np.stack([columns(a("L0_ffn_rn_pre1")), columns(a("L0_ffn_rn_pre2"))], 1),
        "rn_post": np.stack([a("L0_ffn_rn_post1"), a("L0_ffn_rn_post2"), a("L0_ffn_rn_post")]),
        "router": a("L0_ffn_router_w"), "router_scale": columns(a("L0_ffn_router_scale")), "expert_scale": a("L0_ffn_per_expert_scale")[None],
        "q_w": with_halves_swapped(a("L1_xattn_q_norm_w")), "k_w": with_halves_swapped(a("L1_xattn_k_norm_w")),
        "woT": a("L1_xattn_w_out").T, "cos": cos, "sin": sin,
    }
    nc = bacc.Bacc("TRN2", target_bir_lowering=False, num_devices=1)
    args, given = [], {}
    for name, v in arrays.items():
        v = np.ascontiguousarray(v)
        given[f"in_{name}"] = v
        args.append(nc.dram_tensor(f"in_{name}", v.shape, mybir.dt.from_np(v.dtype), kind="ExternalInput").ap())
    shape = a("x").shape
    out = nc.dram_tensor("out_x", shape, F32, kind="ExternalOutput").ap()
    two_layers(nc, *args, out)
    r = run_bass_kernel_spmd(nc, [given], core_ids=[0])
    return r.results[0]["out_x"]
```

```python
from contextlib import ExitStack

import concourse.bass as bass
from concourse import mybir

ALU = mybir.AluOpType
ACT = mybir.ActivationFunctionType
AX = mybir.AxisListType
F32 = mybir.dt.float32
F32R = mybir.dt.float32r
BF16 = mybir.dt.bfloat16

P = 128
CREDIT = 2
LEAD = 4


def two_layers(nc, x_in, ctx_in, ctxT_in, wkT_in, bk_in, gamma_in, beta_in, ffn_w_in, rn_pre_in, rn_post_in,
              router_in, router_scale_in, expert_scale_in, q_w_in, k_w_in, woT_in, cos_in, sin_in, out):
    B, S, D = x_in.shape
    C = ctx_in.shape[2]
    NT = B * S // P
    TB = S // P
    KD = D // P
    NH = 16
    NG = 4
    HG = NH // NG
    HD = D // NH
    E = router_in.shape[1]
    HT = ffn_w_in.shape[0] // 3
    STEPS = HT * B
    NB = (2 * NT * P - E) // S + E
    STEP0 = (0, STEPS, STEPS + 2 * NB)
    TILE0 = (0, HT, HT + 2 * NB)
    SIM_SCALE = float(D) ** -0.5
    HEAD_SCALE = float(HD) ** -0.5
    ST = 3 * HD

    ctx = ExitStack()
    with ctx:
        def sem(name):
            return ctx.enter_context(nc.semaphore(name))

        def sb(name, shape, dt=F32, scope=None):
            return (scope or ctx).enter_context(nc.sbuf_tensor(name, shape, dt))

        ps = ctx.enter_context(nc.psum_tensor("ps", [P, 8, 512], F32))

        x = sb("x", [P, NT, D])
        ident = sb("ident", [P, P])
        identb = sb("identb", [P, P], BF16)
        maskb = sb("maskb", [P, P], BF16)
        bst = sb("bst", [P, NT, 6])
        mv = sb("mv", [P, NT, 2])
        vv = sb("vv", [P, NT])
        sd = sb("sd", [P, NT])
        r0 = sb("r0", [P, NT])
        r1 = sb("r1", [P, NT])
        rs = sb("rs", [P, NT])
        nmr = sb("nmr", [P, NT])
        a_bst = sb("a_bst", [P, 3, TB, 6])
        a_mv = sb("a_mv", [P, 3, TB, 2])
        a_vv, a_sd, a_r0, a_r1, a_rs, a_nmr = (sb("a_" + n, [P, 3, TB]) for n in ("vv", "sd", "r0", "r1", "rs", "nmr"))

        rnp = sb("rnp", [P, 2, KD])
        rw32 = sb("rw32", [P, KD, E])
        rsc = sb("rsc", [P, KD])
        rws = sb("rws", [P, KD, E])
        rwh = sb("rwh", [P, KD, E], F32R)
        rwl = sb("rwl", [P, KD, E], F32R)

        kss = sb("kss", [P, NT])
        krs = sb("krs", [P, NT])
        ssq = sb("ssq", [P, 3, NT])
        pv, psd, py, pz, rr = (sb("p_" + n, [P, 2, NT]) for n in ("v", "sd", "y", "z", "r"))
        kv_raw = x[:, 0:4, :].rearrange("p a (t c) -> p (a t) c", c=C)
        k_mul = x[:, 4:8, :].rearrange("p a (t c) -> p (a t) c", c=C)
        k_rot = x[:, 12:16, :].rearrange("p a (t c) -> p (a t) c", c=C)
        kcos, ksin = (x[:, i, :].rearrange("p (t c) -> p t c", c=C) for i in (8, 9))
        kwB = x[:, 10, 0:2 * C].rearrange("p (k c) -> p k c", c=C)
        cosB, sinB = (x[:, 10, i:i + TB * HD].rearrange("p (t c) -> p t c", c=HD) for i in (2 * C, 3 * C))
        qwB = x[:, 8:10, :]
        wcos32, wsin32 = x[:, 0:4, :], x[:, 4:8, :]

        tri = sb("tri", [P, P])
        ones = sb("ones", [P, P])
        slot = sb("slot", [P, 2, NT], mybir.dt.uint32)
        wgt = sb("wgt", [P, 2, NT])
        tile_no = sb("tile_no", [P, NB], mybir.dt.int32)
        xs, yo = x[:, 0:TB, :], x[:, 2 * TB:3 * TB, :]

        s_scope = ExitStack()
        kvTh = sb("kvTh", [P, B, S], F32R, s_scope)
        kvTl = sb("kvTl", [P, B, S], F32R, s_scope)
        kvh = sb("kvh", [P, NT, C], F32R, s_scope)
        kvl = sb("kvl", [P, NT, C], F32R, s_scope)
        s_scope.close()
        s_scope = ExitStack()
        accD = sb("accD", [P, NT, D], F32, s_scope)
        accM = x
        s_scope.close()
        KT = sb("KT", [ST, B * NG, S], F32R)

        xt_scope = ExitStack()
        xTh = sb("xTh", [P, KD, NT * P], F32R, xt_scope)
        xTl = sb("xTl", [P, KD, NT * P], F32R, xt_scope)
        xn = sb("xn", [P, 2, D], F32, xt_scope)

        a_scope = ExitStack()
        gammaB = sb("gammaB", [P, D], F32, a_scope)
        betaB = sb("betaB", [P, D], F32, a_scope)
        bk = sb("bk", [P, 1], F32, a_scope)
        wk32 = sb("wk32", [P, C], F32, a_scope)
        wkh = sb("wkh", [P, C], F32R, a_scope)
        wkl = sb("wkl", [P, C], F32R, a_scope)
        cT32 = sb("cT32", [P, S], F32, a_scope)
        cTh = sb("cTh", [P, S], F32R, a_scope)
        cTl = sb("cTl", [P, S], F32R, a_scope)
        kvf = sb("kvf", [P, S], F32, a_scope)
        oTh = sb("oTh", [P, S], F32R, a_scope)
        oTl = sb("oTl", [P, S], F32R, a_scope)
        ctx_rows = sb("ctx_rows", [P, NT, C], F32, a_scope)
        ksq = sb("ksq", [P, C], F32, a_scope)
        va = sb("va", [P, TB, D], F32, a_scope)
        vb = sb("vb", [P, TB, D], F32, a_scope)
        vc = sb("vc", [P, TB, D], F32, a_scope)
        mxa = sb("mxa", [P, NT], F32, a_scope)
        nma = sb("nma", [P, NT], F32, a_scope)
        sma = sb("sma", [P, NT], F32, a_scope)
        rca = sb("rca", [P, NT], F32, a_scope)
        a_scope.close()

        f_scope = ExitStack()
        raw = sb("raw", [P, 2, 3, D], F32, f_scope)
        wh = sb("wh", [P, 2, 3, D], F32R, f_scope)
        wl = sb("wl", [P, 2, 3, D], F32R, f_scope)
        act_o = sb("act_o", [P, 2, S], F32, f_scope)
        hid = sb("hid", [P, 2, S], F32, f_scope)
        hidh = sb("hidh", [P, 2, S], F32R, f_scope)
        hidl = sb("hidl", [P, 2, S], F32R, f_scope)
        pesB = sb("pesB", [P, E], F32, f_scope)
        both, pos, tot, before = (sb("r_" + n, [P, NT, E], F32, f_scope) for n in ("both", "pos", "tot", "before"))
        blocks, first = (sb("r_" + n, [P, E], F32, f_scope) for n in ("blocks", "first"))
        block_no = sb("block_no", [P, NB], F32, f_scope)
        tile_f = sb("tile_f", [P, NB], F32, f_scope)
        slot_f = sb("slot_f", [P, 2, NT], F32, f_scope)
        desc = sb("desc", [P, E], F32, f_scope)
        lg, lg2, key, oh1, oh2 = (sb("r_" + n, [P, NT, E], F32, f_scope) for n in ("lg", "lg2", "key", "oh1", "oh2"))
        m1, m2, pk = (sb("r_" + n, [P, NT], F32, f_scope) for n in ("m1", "m2", "pk"))
        lgT = sb("lgT", [E, B, S], F32, f_scope)
        f_scope.close()
        xt_scope.close()

        g_scope = ExitStack()
        postB = sb("postB", [P, 3, D], F32, g_scope)
        xr = sb("xr", [P, TB, D], F32, g_scope)
        ta = sb("ta", [P, TB, D], F32, g_scope)
        tb = sb("tb", [P, TB, D], F32, g_scope)
        sq = sb("sq", [P, D], F32, g_scope)
        g_scope.close()
        b_scope = ExitStack()
        QT = sb("QT", [ST, TB, HG, NG, P], F32R, b_scope)
        V = sb("V", [P, NT, C], F32, b_scope)
        woh = sb("woh", [P, KD, D], F32R, b_scope)
        wol = sb("wol", [P, KD, D], F32R, b_scope)
        k_scope = ExitStack()
        wcos = sb("wcos", [P, TB, D], F32, k_scope)
        wsin = sb("wsin", [P, TB, D], F32, k_scope)
        ka = sb("ka", [P, NT, C], F32, k_scope)
        u = sb("u", [P, TB, D], F32, k_scope)
        wo32 = u
        qa = sb("qa", [P, 2, D], F32, k_scope)
        qb = sb("qb", [P, 2, D], F32, k_scope)
        th = sb("th", [P, 2, D], F32R, k_scope)
        tl = sb("tl", [P, 2, D], F32R, k_scope)
        k_scope.close()
        Pr = sb("Pr", [P, 2, HG, S], F32, b_scope)
        PT = sb("PT", [P, 4, HG * P], F32, b_scope)
        Vb = sb("Vb", [P, TB, C], F32, b_scope)
        aT = sb("aT", [P, 2, NG, P], F32, b_scope)
        aTh = sb("aTh", [P, 2, NG, P], F32R, b_scope)
        aTl = sb("aTl", [P, 2, NG, P], F32R, b_scope)
        rE = sb("rE", [P, 4, HG, HD], F32, b_scope)
        rcb = sb("rcb", [P, 4, HG], F32, b_scope)
        rT = sb("rT", [P, 2, P], F32, b_scope)
        mnb = sb("mnb", [P, 2, HG], F32, b_scope)
        smb = sb("smb", [P, 4, HG], F32, b_scope)
        b_scope.close()

        x_dram = nc.dram_tensor("x_dram", (P, NT, D), F32, kind="Internal").ap()
        ka_dram = nc.dram_tensor("ka_dram", (P, NT, C), F32, kind="Internal").ap()
        w_dram = nc.dram_tensor("w_dram", (2, P, TB, D), F32, kind="Internal").ap()
        q_dram = nc.dram_tensor("q_dram", (2, NT, P, D), F32R, kind="Internal").ap()
        k_dram = nc.dram_tensor("k_dram", (2, B, P, S), F32R, kind="Internal").ap()
        xhat_dram = nc.dram_tensor("xhat_dram", (P, NT, D), F32, kind="Internal").ap()
        xg_dram = nc.dram_tensor("xg_dram", (NB * S, D), F32, kind="Internal").ap()
        y_dram = nc.dram_tensor("y_dram", (NB * S, D), F32, kind="Internal").ap()

        def sems(*names):
            return [sem(n) for n in names]

        phase_done, consts_ready = sems("phase_done", "consts_ready")
        x_loaded = sems(*(f"x_loaded{b}" for b in range(B)))
        stored = sems(*(f"stored{b}" for b in range(B)))
        small_loaded, ctxT_loaded = sems("small_loaded", "ctxT_loaded")
        dve_chain, act_chain, pool_chain = sems("dve_chain", "act_chain", "pool_chain")
        root_asked, root_done = sems("root_asked", "root_done")
        xn_ready, xt_turned, xt_high, xt_low = sems("xn_ready", "xt_turned", "xt_high", "xt_low")
        wk_high, ctx_high, ctx_low, kv_done, kv_biased, kvT_high, kvT_low, kv_turned, kv_high, kv_low = sems(
            "wk_high", "ctx_high", "ctx_low", "kv_done", "kv_biased", "kvT_high", "kvT_low", "kv_turned", "kv_high", "kv_low")
        pkv_done, pkv_high, pkv_low, sim_done = sems("pkv_done", "pkv_high", "pkv_low", "sim_done")
        a_weighed, a_scaled, a_max, a_exp, a_added = sems("a_weighed", "a_scaled", "a_max", "a_exp", "a_added")
        wk_loaded, ctx_loaded = sems("wk_loaded", "ctx_loaded")
        scales_ready = sem("scales_ready")
        x_spilled, rw_scaled, rw_high, rw_low, lg_done, lg_copied, lg_turned = sems(
            "x_spilled", "rw_scaled", "rw_high", "rw_low", "lg_done", "lg_copied", "lg_turned")
        acc_zero, exp_asked, exp_taken = sems("acc_zero", "exp_asked", "exp_taken")
        w_loaded = sems("w_loaded0", "w_loaded1")
        xhat_stored = sems("xhat_stored0", "xhat_stored1")
        both_ready, ranks_done, slots_ready, xg_zeroed, xhat_loaded, xg_filled, tri_ready = sems(
            "both_ready", "ranks_done", "slots_ready", "xg_zeroed", "xhat_loaded", "xg_filled", "tri_ready")
        xs_loaded, xg_turned, xg_high, xg_low, y_ready, y_stored = sems(
            "xs_loaded", "xg_turned", "xg_high", "xg_low", "y_ready", "y_stored")
        y_summed, y_free, rows_loaded, part_squared = sems("y_summed", "y_free", "rows_loaded", "part_squared")
        y_fetched = sems(*(f"y_fetched{i}" for i in range(TB)))
        w_high, w_low, gate_done, up_done, out_done = sems("w_high", "w_low", "gate_done", "up_done", "out_done")
        act_ready, hid_ready, hid_high, hid_low, acc_added = sems(
            "act_ready", "hid_ready", "hid_high", "hid_low", "acc_added")
        squares_ready, g_parts, g_sum, g_added = sems("squares_ready", "g_parts", "g_sum", "g_added")
        xr_loaded = sems(*(f"xr_loaded{i}" for i in range(TB)))
        k_in_loaded, kw_loaded, qw_loaded, tables_stored, sum_squared, g_final, k_scaled = sems(
            "k_in_loaded", "kw_loaded", "qw_loaded", "tables_stored", "sum_squared", "g_final", "k_scaled")
        g_scaled = sem("g_scaled")
        v_loaded, wo_loaded, post_loaded = sems("v_loaded", "wo_loaded", "post_loaded")
        b_loaded, k_turned, k_high, k_low, k_parts_stored, wo_high, wo_low = sems(
            "b_loaded", "k_turned", "k_high", "k_low", "k_parts_stored", "wo_high", "wo_low")
        u_ready, qa_ready, qb_ready, q_turned, q_high, q_low = sems(
            "u_ready", "qa_ready", "qb_ready", "q_turned", "q_high", "q_low")
        k_stored, kt_loaded = sems("k_stored", "kt_loaded")
        q_high_stored = sems("q_high_stored0", "q_high_stored1")
        q_low_stored = sems("q_low_stored0", "q_low_stored1")
        qt_loaded = sems(*(f"qt_loaded{t}" for t in range(TB)))
        s_done, min_ready, exp_done, rinv_ready, p_turned, p_copied_act, p_copied_dve, pv_done, o_done, rt_copied, attn_ready = sems(
            "s_done", "min_ready", "exp_done", "rinv_ready", "p_turned", "p_copied_act", "p_copied_dve", "pv_done", "o_done",
            "rt_copied", "attn_ready")
        recip_done = sem("recip_done")
        attn_high, attn_low, proj_done, proj_added, vb_ready = sems("attn_high", "attn_low", "proj_done", "proj_added", "vb_ready")

        block = ctx.enter_context(nc.Block())

        ENGINES = 5
        LN_EPS, RMS0_EPS, RMS1_EPS = 1e-5, 1e-6, 1e-5
        NU, LAG = TB * NG, 3

        def unit(n):
            return n % NU // NG, n % NG, n // NU

        def units_order(units, waiting, last):
            steps, waiting = [], list(waiting)
            for n in units:
                more = not (last and n + 1 == NU)
                done = n >= NG + LAG - 1 and (n - LAG + 1) % NG == 0
                if more:
                    steps.append(("scores", n + 1, 0))
                for kt in range(unit(n)[0] + 1):
                    if len(waiting) == 2:
                        steps.append(("values", *waiting.pop(0)))
                    if kt == 0 and more:
                        steps.append(("scores", n + 1, 1))
                    if kt == 0 and done:
                        steps.append(("split", (n - LAG + 1) // NG - 1, 0))
                    steps.append(("turn", n, kt))
                    waiting.append((n, kt))
                if done:
                    steps.append(("project", (n - LAG + 1) // NG - 1, 0))
            if last:
                steps += [("values", *w) for w in waiting] + [("split", TB - 1, 0), ("project", TB - 1, 0)]
            return steps

        WAITING = [(LAG - 2, 0), (LAG - 1, 0)]
        FIRST = units_order(range(LAG), [], False)
        BODY = units_order(range(LAG, NU + LAG), WAITING, False)
        LAST = units_order(range(LAG, NU), WAITING, True)
        KEYS = [(n, kt) for n in range(NU + LAG) for kt in range(unit(n)[0] + 1)]
        PER_SEQ = TB * (TB + 1) // 2 * NG
        ACT_KEYS = [k for k in KEYS if k[1] % 2 == 0]
        DVE_KEYS = [k for k in KEYS if k[1] % 2 == 1]
        ACT_PER_SEQ, DVE_PER_SEQ = (sum(k[0] < NU for k in keys) for keys in (ACT_KEYS, DVE_KEYS))

        def bank_of(steps, i):
            before = 0 if steps is FIRST else LAG
            return 4 + (before + sum(s_[0] in ("turn", "project") for s_ in steps[:i])) % 2

        def count(b, per_seq, k):
            return b * per_seq + (k + LEAD)

        def end_of_unit(n, kt):
            return kt == unit(n)[0]

        NORMS = [(0, 0), (0, 1), (0, 2), (1, 0), (0, 3), (1, 1), (1, 2), (1, 3)]

        def row_no(k, b, i):
            return NORMS.index((k, b)) * TB + i

        def row_bank(t):
            return t % TB if t < TB else 4 + t % TB

        def landing(t):
            return (qa, qb)[t % TB // 2][:, t % 2, :]

        def closing_kinds(b):
            return slice(0 if b + 1 < B else 1, 2 if b >= 0 else 1)

        def turn_kinds(b):
            return slice(0 if b + 1 < B else min(b - B + 2, 2), min(b + 2, 3))

        def end_phase(eng, n):
            eng.drain().then_inc(phase_done, 1)
            eng.wait_ge(phase_done, ENGINES * n)

        def step_no(part, i, j):
            return i * (2 * B) + (STEP0[part] + j)

        def next_tile(part, i, j, chain_end):
            k = j // B + 1
            if j % B == 0:
                return None
            if isinstance(i, int) and 2 * i + k >= HT:
                if chain_end:
                    return None
                return part + 1, i * 2 + (TILE0[part] + k), k % 2, i * (2 * B) + (STEP0[part] + (k - 1) * B)
            return part, i * 2 + (TILE0[part] + k), k % 2, i * (2 * B) + (STEP0[part] + (k - 1) * B)

        def xhat_stores(m):
            return sum(NORMS[r // TB][0] for r in range(m % 2, m + 1, 2))

        @block.sync
        def _(sp):
            load = nc.sync.dma_start
            load(wk32[:, :], wkT_in).then_inc(wk_loaded, 16)
            load(bk[:, :], bk_in.rearrange("(p o) -> p o", o=1)).then_inc(wk_loaded, 16)
            for b in range(B):
                if b:
                    sp.wait_ge(ctx_low, b)
                load(cT32[:, :], ctxT_in[:, b * S:(b + 1) * S]).then_inc(ctxT_loaded, 16)
                load(x[:, TB * b:TB * b + TB, :], x_in[b].rearrange("(t p) d -> p t d", p=P)).then_inc(x_loaded[b], 16)
                if b == 0:
                    load(gammaB[:, :], gamma_in.broadcast_to((P, D))).then_inc(small_loaded, 16)
                    load(betaB[:, :], beta_in.broadcast_to((P, D))).then_inc(small_loaded, 16)
                if b == 1:
                    load(ctx_rows[:, :, :], ctx_in.rearrange("b (t p) c -> p (b t) c", p=P)).then_inc(ctx_loaded, 16)
            load(rnp[:, :, :], rn_pre_in).then_inc(small_loaded, 16)
            load(rw32[:, :, :], router_in.rearrange("(k p) e -> p k e", p=P)).then_inc(small_loaded, 16)
            load(rsc[:, :], router_scale_in).then_inc(small_loaded, 16)

            def store_rows(b):
                for i in range(TB):
                    m = row_no(1, b, i)
                    sp.wait_ge(xn_ready, m + 1)
                    load(xhat_dram[:, TB * b + i, :], xn[:, m % 2, :]).then_inc(xhat_stored[m % 2], 16)

            for b in range(B - 1):
                store_rows(b)
            end_phase(sp, 1)

            load(pesB[:, :], expert_scale_in.broadcast_to((P, E))).then_inc(small_loaded, 16)
            for q in range(2):
                load(raw[:, q, :, :], ffn_w_in[q]).then_inc(w_loaded[q], 16)
            store_rows(B - 1)
            load(x_dram, x[:, :, :]).then_inc(x_spilled, 16)

            def stream(part, i):
                for q in range(2):
                    sp.wait_ge(w_low, i * 6 + 3 * (TILE0[part] + q + 1))
                    load(raw[:, q, :, :], ffn_w_in[bass.ds(i * 2 + ((0, HT, 2 * HT)[part] + q + 2), 1)].rearrange("o p m n -> p (o m) n")).then_inc(w_loaded[q], 16)

            with sp.Fori(0, HT // 2 - 1) as i:
                stream(0, i)
            for q in range(2):
                sp.wait_ge(w_low, 3 * (HT - 2 + q) + 3)
                load(raw[:, q, :, :], ffn_w_in[HT + q]).then_inc(w_loaded[q], 16)
            sp.wait_ge(slots_ready, 1)
            with sp.Fori(0, NB - 1) as k:
                tile = sp.value_load(tile_no[0:1, bass.ds(k + 1, 1)], min_val=HT, max_val=2 * HT - 2)
                for h in range(2):
                    sp.wait_ge(w_low, k * 6 + 3 * (HT + h + 1))
                    load(raw[:, h, :, :], ffn_w_in[bass.ds(tile + h, 1)].rearrange("o p m n -> p (o m) n")).then_inc(w_loaded[h], 16)
            end_phase(sp, 2)

            for k in range(3):
                load(postB[:, k, :], rn_post_in[k:k + 1, :].broadcast_to((P, D))).then_inc(post_loaded, 16)
            load(ka[:, :, :], ka_dram).then_inc(v_loaded, 16)
            for t in range(TB):
                load(xr[:, t, :], x_dram[:, t, :]).then_inc(xr_loaded[t], 16)
            sp.wait_ge(y_summed, 2 * TB)
            load(wo32[:, :, :], woT_in.rearrange("(k p) n -> p k n", p=P)).then_inc(wo_loaded, 16)
            for k, w_ in enumerate((wcos, wsin)):
                load(w_[:, :, :], w_dram[k]).then_inc(b_loaded, 16)
            load(V[:, :, :], ctx_in.rearrange("b (t p) c -> p (b t) c", p=P)).then_inc(rows_loaded, 16)

            def residual_rows(t):
                if t < NT:
                    sp.wait_ge(g_added, t - TB + 1)
                    load(xr[:, t % TB, :], x_dram[:, t, :]).then_inc(xr_loaded[t % TB], 16)

            for b in range(B):
                sp.wait_ge(k_high, b + 1)
                load(k_dram[0, b].bitcast(F32), th[:, b % 2, :].bitcast(F32)).then_inc(k_stored, 16)
                sp.wait_ge(k_low, b + 1)
                load(k_dram[1, b].bitcast(F32), tl[:, b % 2, :].bitcast(F32)).then_inc(k_stored, 16)
                sp.wait_ge(k_stored, 32 * (b + 1))
                sp.sem_inc(k_parts_stored, 1)
            for t in range(TB, 2 * TB):
                residual_rows(t)
            for t in range(NT):
                residual_rows(t + 2 * TB)
                sp.wait_ge(q_high, t + 1)
                load(q_dram[0, t].bitcast(F32), th[:, t % 2, :].bitcast(F32)).then_inc(q_high_stored[t % 2], 16)
                sp.wait_ge(q_low, t + 1)
                load(q_dram[1, t].bitcast(F32), tl[:, t % 2, :].bitcast(F32)).then_inc(q_low_stored[t % 2], 16)
            for q in range(2):
                sp.wait_ge(q_high_stored[q], 16 * (NT // 2))
                sp.wait_ge(q_low_stored[q], 16 * (NT // 2))
            end_phase(sp, 3)
            end_phase(sp, 4)

            for q in range(2):
                load(raw[:, q, :, :], ffn_w_in[2 * HT + q]).then_inc(w_loaded[q], 16)
            with sp.Fori(0, HT // 2 - 1) as i:
                stream(2, i)
            for b in range(B):
                sp.wait_ge(acc_added, STEP0[2] + STEPS - B + b + 1 + CREDIT)
                load(out[b].rearrange("(t p) d -> p t d", p=P), x[:, TB * b:TB * b + TB, :]).then_inc(stored[b], 16)
            for b in range(B):
                sp.wait_ge(stored[b], 16)

        @block.gpsimd
        def _(pool):
            chained = [0]

            def link(ins):
                chained[0] += 1
                ins.then_inc(pool_chain, 1)
                pool.wait_ge(pool_chain, chained[0])

            link(nc.gpsimd.memset(ident[:, :], 1.0))
            link(nc.gpsimd.affine_select(out=ident[:, :], in_=ident[:, :], compare_op=ALU.is_equal, fill=0.0, base=0,
                                         pattern=[[-1, P]], channel_multiplier=1))
            link(nc.gpsimd.tensor_copy(identb[:, :], ident[:, :]))
            link(nc.gpsimd.memset(maskb[:, :], 0.0))
            nc.gpsimd.affine_select(out=maskb[:, :], in_=maskb[:, :], compare_op=ALU.is_ge, fill=1e30, base=0,
                                    pattern=[[-1, P]], channel_multiplier=1).then_inc(consts_ready, 1)
            link(nc.gpsimd.memset(tri[:, :], 1.0))
            link(nc.gpsimd.affine_select(out=tri[:, :], in_=tri[:, :], compare_op=ALU.is_gt, fill=0.0, base=0,
                                         pattern=[[1, P]], channel_multiplier=-1))
            nc.gpsimd.memset(ones[:, :], 1.0).then_inc(tri_ready, 1)
            pool.wait_ge(small_loaded, 32)
            for t in range(NT):
                pool.wait_ge(a_scaled, t + 1)
                if t >= TB:
                    pool.wait_ge(a_exp, t - TB + 1)
                nc.gpsimd.tensor_tensor(out=vb[:, t % TB, :], in0=va[:, t % TB, :], in1=gammaB[:, :], op=ALU.mult).then_inc(a_weighed, 1)
            end_phase(pool, 1)

            nc.gpsimd.iota(desc[:, :], pattern=[[-1, E]], base=E, channel_multiplier=0,
                           allow_small_or_imprecise_dtypes=True).then_inc(consts_ready, 1)
            nc.gpsimd.iota(block_no[:, :], pattern=[[1, NB]], base=0, channel_multiplier=0,
                           allow_small_or_imprecise_dtypes=True).then_inc(consts_ready, 1)
            nc.gpsimd.memset(accD[:, :, :], 0.0).then_inc(acc_zero, 1)
            pool.wait_ge(x_spilled, 16)
            pool.wait_ge(xn_ready, 2 * NT)
            link(nc.gpsimd.memset(x[:, 0, :], 0.0))
            nc.gpsimd.dma_start(xg_dram.rearrange("(t p) d -> p t d", p=P), x[:, 0:1, :].broadcast_to((P, NB * TB, D))).then_inc(xg_zeroed, 16)
            pool.wait_ge(xg_zeroed, 16)
            for q in range(2):
                pool.wait_ge(xhat_stored[q], 16 * xhat_stores(2 * NT - 2 + q))
            nc.gpsimd.dma_start(x[:, :, :], xhat_dram).then_inc(xhat_loaded, 16)
            pool.wait_ge(xhat_loaded, 16)
            pool.wait_ge(slots_ready, 1)
            for t in range(NT):
                for k in range(2):
                    nc.gpsimd.indirect_dma_start(xg_dram, bass.IndirectOffsetOnAxis(ap=slot[:, k, t:t + 1], axis=0), x[:, t, :], None).then_inc(xg_filled, 16)
            pool.wait_ge(xg_filled, 16 * 2 * NT)
            mul = nc.gpsimd.tensor_tensor
            H2 = HD // 2

            def heads(a):
                return a.rearrange("p (h c) -> p h c", c=HD)

            def halves_swapped(out_, in_, table):
                mul(out=heads(out_)[:, :, 0:H2], in0=heads(in_)[:, :, H2:HD], in1=heads(table)[:, :, 0:H2], op=ALU.mult)
                return mul(out=heads(out_)[:, :, H2:HD], in0=heads(in_)[:, :, 0:H2], in1=heads(table)[:, :, H2:HD], op=ALU.mult)

            def times_table(out_, w_, table, t):
                n = out_.shape[-1] // HD
                return mul(out=heads(out_), in0=heads(w_), in1=table[:, t:t + 1, :].broadcast_to((P, n, HD)), op=ALU.mult)

            fetch = nc.gpsimd.dma_start
            fetch(kv_raw, ctx_in.rearrange("b (t p) c -> p (b t) c", p=P)).then_inc(k_in_loaded, 16)
            fetch(cosB, cos_in.rearrange("(t p) c -> p t c", p=P)).then_inc(kw_loaded, 16)
            fetch(sinB, sin_in.rearrange("(t p) c -> p t c", p=P)).then_inc(kw_loaded, 16)
            for k in range(2):
                fetch(kwB[:, k, :], k_w_in[k:k + 1, :].broadcast_to((P, C))).then_inc(kw_loaded, 16)
            pool.wait_ge(kw_loaded, 64)
            for t in range(TB):
                times_table(kcos[:, t, :], kwB[:, 0, :], cosB, t)
                last = times_table(ksin[:, t, :], kwB[:, 1, :], sinB, t)
            link(last)
            pool.wait_ge(k_in_loaded, 16)
            for b in range(B):
                mul(out=k_mul[:, b * TB:(b + 1) * TB, :], in0=kv_raw[:, b * TB:(b + 1) * TB, :], in1=kcos, op=ALU.mult)
                for t in range(TB):
                    last = halves_swapped(k_rot[:, b * TB + t, :], kv_raw[:, b * TB + t, :], ksin[:, t, :])
            link(last)
            for b in range(B):
                bt = slice(b * TB, (b + 1) * TB)
                last = mul(out=k_mul[:, bt, :], in0=k_mul[:, bt, :], in1=k_rot[:, bt, :], op=ALU.add)
            link(last)
            pool.wait_ge(k_scaled, 1)
            link(mul(out=k_mul, in0=k_mul, in1=krs[:, :].unsqueeze(2).broadcast_to((P, NT, C)), op=ALU.mult))
            fetch(ka_dram, k_mul).then_inc(tables_stored, 16)
            for k in range(2):
                fetch(qwB[:, k, :], q_w_in[k:k + 1, :].broadcast_to((P, D))).then_inc(qw_loaded, 16)
            pool.wait_ge(tables_stored, 16)
            pool.wait_ge(qw_loaded, 32)
            link(nc.gpsimd.tensor_scalar(qwB, qwB, -HEAD_SCALE, None, ALU.mult))
            for t in range(TB):
                times_table(wcos32[:, t, :], qwB[:, 0, :], cosB, t)
                last = times_table(wsin32[:, t, :], qwB[:, 1, :], sinB, t)
            link(last)
            fetch(w_dram[0], wcos32).then_inc(tables_stored, 16)
            fetch(w_dram[1], wsin32).then_inc(tables_stored, 16)
            pool.wait_ge(tables_stored, 48)
            def fetch_rows(k):
                fetch(xs, xg_dram[bass.ds(k * S, S), :].rearrange("(t p) d -> p t d", p=P)).then_inc(xs_loaded, 16)

            def store_products(k):
                pool.wait_ge(y_ready, k + 1)
                fetch(y_dram[bass.ds(k * S, S), :].rearrange("(t p) d -> p t d", p=P), yo).then_inc(y_stored, 16)
                pool.wait_ge(y_stored, k * 16 + 16)
                pool.sem_inc(y_free, 1)

            fetch_rows(0)
            pool.wait_ge(xg_turned, TB)
            fetch_rows(1)
            with pool.Fori(0, NB - 2) as k:
                pool.wait_ge(xg_turned, k * TB + 2 * TB)
                fetch_rows(k + 2)
                store_products(k)
            store_products(NB - 2)
            store_products(NB - 1)
            end_phase(pool, 2)

            pool.wait_ge(y_stored, 16 * NB)

            def fetch_products(b):
                for t in range(b * TB, b * TB + TB):
                    if t >= TB:
                        pool.wait_ge(y_summed, t - TB + 1)
                    for k, to in enumerate((accM[:, t, :], landing(t))):
                        nc.gpsimd.indirect_dma_start(to, None, y_dram, bass.IndirectOffsetOnAxis(ap=slot[:, k, t:t + 1], axis=0)).then_inc(y_fetched[t % TB], 16)

            def sum_parts(t):
                pool.wait_ge(g_parts, t + 1)
                mul(out=accD[:, t, :], in0=ta[:, t % TB, :], in1=tb[:, t % TB, :], op=ALU.add).then_inc(g_sum, 1)

            def query_sine(t):
                pool.wait_ge(u_ready, t + 1)
                if t >= 2:
                    pool.wait_ge(q_turned, t - 1)
                halves_swapped(qb[:, t % 2, :], u[:, t % TB, :], wsin[:, t % TB, :]).then_inc(qb_ready, 1)

            def load_queries(t, q_tile):
                for r, part in enumerate((0, 1, 0)):
                    fetch(QT[r * HD:(r + 1) * HD, t, :, :, :].rearrange("c h g n -> c h (g n)"),
                          q_tile(part).rearrange("(h c) m -> c h m", c=HD)).then_inc(qt_loaded[t], 16)

            def first_queries(t):
                pool.wait_ge(q_high_stored[t % 2], 16 * (t // 2 + 1))
                pool.wait_ge(q_low_stored[t % 2], 16 * (t // 2 + 1))
                load_queries(t, lambda part: q_dram[part, t])

            fetch_products(0)
            fetch_products(1)
            for i in range(TB):
                sum_parts(i)
            fetch_products(2)
            for b in range(-1, B):
                if b == 0:
                    fetch_products(3)
                    pool.wait_ge(b_loaded, 32)
                    pool.wait_ge(y_summed, NT)
                for i in range(TB):
                    if b >= 0:
                        query_sine(b * TB + i)
                    if b + 2 < B:
                        sum_parts((b + 2) * TB + i)
                    if b == B - 1 and i == 0:
                        pool.wait_ge(g_added, NT)
                        pool.wait_ge(k_parts_stored, B)
                        for r, part in enumerate((0, 0, 1)):
                            fetch(KT[r * HD:(r + 1) * HD, :, :], k_dram[part].rearrange("b (g c) n -> c (b g) n", c=HD)).then_inc(kt_loaded, 16)
                    elif b == B - 1:
                        first_queries(i - 1)
            first_queries(TB - 1)
            end_phase(pool, 3)
            with pool.Fori(0, B - 1) as b:
                for t in range(TB):
                    pool.wait_ge(s_done, count(b, 2 * NU, 2 * NG * (t + 1)))
                    load_queries(t, lambda part: q_dram[part, bass.ds(b * TB + (TB + t), 1)].rearrange("o p m -> (o p) m"))
            end_phase(pool, 4)

        @block.tensor
        def _(pe):
            mm, turn = nc.tensor.matmul, nc.tensor.transpose

            def three(out_ap, ah, al, bh, bl, start, stop):
                mm(out_ap, ah, bh, start=start, stop=False)
                mm(out_ap, ah, bl, start=False, stop=False)
                return mm(out_ap, al, bh, start=False, stop=stop)

            def turn_last_rows(tiles):
                for t in tiles:
                    pe.wait_ge(xn_ready, 2 * NT + t + 1)
                    if t >= 2 * TB:
                        pe.wait_ge(xt_low, 2 * NT + t - TB + 1)
                    for d in range(KD):
                        last = turn(ps[:, row_bank(t), d * P:(d + 1) * P], xn[:, t % 2, d * P:(d + 1) * P], ident[:, :])
                    last.then_inc(xt_turned, 1)

            def gate_up(part, i, j):
                s = step_no(part, i, j)
                w, q, b = j // B % 2, j % 2, j % B
                bs = slice(b * S, (b + 1) * S)
                if j % B == 0:
                    pe.wait_ge(w_low, i * 6 + (3 * (TILE0[part] + j // B) + 2))
                pe.wait_ge(hid_low, s + (CREDIT - 1))
                for m, done in ((0, gate_done), (1, up_done)):
                    for d in range(KD):
                        dsl = slice(d * P, (d + 1) * P)
                        last = three(ps[:, 2 * m + q, :], wh[:, w, m, dsl], wl[:, w, m, dsl], xTh[:, d, bs], xTl[:, d, bs], d == 0, d == KD - 1)
                    last.then_inc(done, 1)

            def down(part, i, j):
                s = step_no(part, i, j)
                w, q = j // B % 2, j % 2
                if j % B == 0:
                    pe.wait_ge(w_low, i * 6 + (3 * (TILE0[part] + j // B) + 3))
                pe.wait_ge(hid_low, s + (CREDIT + 1))
                pe.wait_ge(acc_added, s + CREDIT)
                for t in range(TB):
                    tsl = slice(t * P, (t + 1) * P)
                    last = three(ps[:, 4 + t, :], hidh[:, q, tsl], hidl[:, q, tsl], wh[:, w, 2, :], wl[:, w, 2, :], True, True)
                last.then_inc(out_done, 1)

            def ffn(part, chain_end, first=0):
                with pe.Fori(first, HT // 2 - 1) as i:
                    for j in range(2 * B):
                        gate_up(part, i, j + 1)
                        down(part, i, j)
                last = 2 * B - 1
                for j in range(last):
                    gate_up(part, HT // 2 - 1, j + 1)
                    if j == last - 1 and not chain_end:
                        turn_slots(-1, 0)
                    down(part, HT // 2 - 1, j)
                if not chain_end:
                    turn_slots(-1, 1)
                down(part, HT // 2 - 1, last)

            def block_step(k, h):
                return k * 2 + (STEPS + h)

            def expert_gate_up(k, h):
                s = block_step(k, h)
                pe.wait_ge(w_low, k * 6 + (3 * (HT + h) + 2))
                if h == 0:
                    pe.wait_ge(xg_low, k * TB + TB)
                pe.wait_ge(hid_low, s + (CREDIT - 1))
                for m, done in ((0, gate_done), (1, up_done)):
                    for d in range(KD):
                        dsl = slice(d * P, (d + 1) * P)
                        last = three(ps[:, 2 * m + h, :], wh[:, h, m, dsl], wl[:, h, m, dsl], xTh[:, d, 0:S], xTl[:, d, 0:S], d == 0, d == KD - 1)
                    last.then_inc(done, 1)

            def turn_slots(k, half):
                if half == 0:
                    pe.wait_ge(xs_loaded, k * 16 + 32)
                    pe.wait_ge(hid_low, k * 2 + (STEPS + 1 + CREDIT))
                else:
                    pe.wait_ge(xg_low, k * TB + (TB + 2))
                for i in (2 * half, 2 * half + 1):
                    for d in range(KD):
                        last = turn(ps[:, i % 2 * 2, d * P:(d + 1) * P], xs[:, i, d * P:(d + 1) * P], ident[:, :])
                    last.then_inc(xg_turned, 1)

            def expert_down(k, h):
                s = block_step(k, h)
                pe.wait_ge(w_low, k * 6 + (3 * (HT + h) + 3))
                pe.wait_ge(hid_low, s + (CREDIT + 1))
                if h == 0:
                    pe.wait_ge(acc_added, s + CREDIT)
                for t in range(TB):
                    tsl = slice(t * P, (t + 1) * P)
                    last = three(ps[:, 4 + t, :], hidh[:, h, tsl], hidl[:, h, tsl], wh[:, h, 2, :], wl[:, h, 2, :], h == 0, h == 1)
                last.then_inc(out_done, 1)

            def experts():
                expert_gate_up(0, 0)
                with pe.Fori(0, NB - 1) as k:
                    expert_gate_up(k, 1)
                    turn_slots(k, 0)
                    expert_down(k, 0)
                    turn_slots(k, 1)
                    expert_down(k, 1)
                    expert_gate_up(k + 1, 0)
                expert_gate_up(NB - 1, 1)
                expert_down(NB - 1, 0)
                expert_down(NB - 1, 1)

            pe.wait_ge(consts_ready, 1)
            pe.sem_inc(out_done, CREDIT)
            for s_ in (s_done, p_turned, pv_done, o_done, proj_done):
                pe.sem_inc(s_, LEAD)
            def project_context(b):
                pe.wait_ge(ctx_low, b + 1)
                three(ps[:, 2, :], wkh[:, :], wkl[:, :], cTh[:, :], cTl[:, :], True, True).then_inc(kv_done, 1)
                pe.wait_ge(kv_biased, b + 1)
                if b:
                    pe.wait_ge(kv_low, b)
                for j in range(TB):
                    last = turn(ps[:, 3, j * P:(j + 1) * P], kvf[:, j * P:(j + 1) * P], ident[:, :])
                last.then_inc(kv_turned, 1)

            def turn_rows(k, b):
                for i in range(TB):
                    m = row_no(k, b, i)
                    pe.wait_ge(xn_ready, m + 1)
                    if m >= 2:
                        pe.wait_ge(xt_low, m - 1)
                    for d in range(KD):
                        last = turn(ps[:, m % 2, d * P:(d + 1) * P], xn[:, m % 2, d * P:(d + 1) * P], ident[:, :])
                    last.then_inc(xt_turned, 1)

            def similarities(b):
                bs = slice(b * S, (b + 1) * S)
                pe.wait_ge(xt_low, row_no(0, b, TB - 1) + 1)
                pe.wait_ge(kv_low, b + 1)
                for j in range(KD):
                    last = three(ps[:, 2, :], kvh[:, TB * b + j, :], kvl[:, TB * b + j, :], xTh[:, j, bs], xTl[:, j, bs], j == 0, j == KD - 1)
                last.then_inc(pkv_done, 1)
                pe.wait_ge(pkv_low, b + 1)
                for i in range(TB):
                    if b:
                        pe.wait_ge(a_scaled, TB * (b - 1) + i + 1)
                    isl = slice(i * P, (i + 1) * P)
                    three(ps[:, 4 + i, :], oTh[:, isl], oTl[:, isl], kvTh[:, b, :], kvTl[:, b, :], True, True).then_inc(sim_done, 1)

            project_context(0)
            turn_rows(0, 0)
            similarities(0)
            for b in range(B):
                if b + 1 < B:
                    project_context(b + 1)
                    turn_rows(0, b + 1)
                    similarities(b + 1)
                if b:
                    turn_rows(1, b - 1)
            end_phase(pe, 1)
            turn_rows(1, B - 1)

            def logits(b):
                bs = slice(b * S, (b + 1) * S)
                pe.wait_ge(xt_low, row_no(1, b, TB - 1) + 1)
                for d in range(KD):
                    last = three(ps[0:E, 4 + b, :], rwh[:, d, :], rwl[:, d, :], xTh[:, d, bs], xTl[:, d, bs], d == 0, d == KD - 1)
                last.then_inc(lg_done, 1)

            pe.wait_ge(rw_low, 1)
            for b in range(B):
                logits(b)
            pe.wait_ge(lg_copied, B)
            for t in range(NT):
                last = turn(ps[:, 3, t * E:(t + 1) * E], lgT[:, t // TB, t % TB * P:(t % TB + 1) * P], ident[0:E, 0:E])
            last.then_inc(lg_turned, 1)
            gate_up(0, 0, 0)
            pe.wait_ge(both_ready, 1)
            pe.wait_ge(tri_ready, 1)
            chosen = both[:, :, :].rearrange("p t e -> p (t e)")
            mm(ps[:, 4, 0:NT * E], tri[:, :], chosen, start=True, stop=True)
            mm(ps[:, 4, NT * E:2 * NT * E], ones[:, :], chosen, start=True, stop=True).then_inc(ranks_done, 1)
            ffn(0, False)
            experts()
            end_phase(pe, 2)

            pe.wait_ge(v_loaded, 16)
            for b in range(B):
                if b >= 2:
                    pe.wait_ge(k_low, b - 1)
                for t in range(TB):
                    last = turn(ps[:, b % 2, t * P:(t + 1) * P], ka[:, b * TB + t, :], ident[:, :])
                last.then_inc(k_turned, 1)
            pe.wait_ge(k_low, B)
            for t in range(NT):
                pe.wait_ge(qa_ready, t + 1)
                pe.wait_ge(qb_ready, t + 1)
                if t >= TB:
                    pe.wait_ge(q_low, t - TB + 1)
                for d in range(KD):
                    dsl = slice(d * P, (d + 1) * P)
                    mm(ps[:, t % TB, dsl], qa[:, t % 2, dsl], ident[:, :], start=True, stop=False)
                    last = mm(ps[:, t % TB, dsl], qb[:, t % 2, dsl], ident[:, :], start=False, stop=True)
                last.then_inc(q_turned, 1)
            end_phase(pe, 3)

            def scores(b, n, hp):
                qt, g, db = unit(n)
                L = max(256, (qt + 1) * P)
                pe.wait_ge(exp_done, b * (2 * NU) + (2 * (n - 1) + hp + 1 + LEAD))
                if g == 0 and hp == 0:
                    pe.wait_ge(qt_loaded[qt], b * 48 + 48 * (db + 1))
                for h in (2 * hp, 2 * hp + 1):
                    mm(ps[:, h, 0:L], QT[:, qt, h, g, :],
                       KT[:, bass.ds(b * NG + (db * NG + g), 1), 0:L].rearrange("p o n -> p (o n)"), start=True, stop=True)
                    last = mm(ps[:, h, qt * P:(qt + 1) * P], identb[:, :], maskb[:, :], start=False, stop=True, skip_group_check=True)
                last.then_inc(s_done, 1)

            def bank_free(b, steps, i):
                users = [s_ for s_ in steps[:i] if s_[0] in ("turn", "project")]
                if len(users) >= 2:
                    kind, n, kt = users[-2]
                    if kind == "project":
                        pe.wait_ge(proj_added, count(b, TB, n + 1))
                    else:
                        wait_copied(b, n, kt)
                elif steps is not FIRST:
                    wait_copied(b, LAG - 1, 0)
                    pe.wait_ge(proj_added, count(b, TB, 0))

            def wait_copied(b, n, kt):
                if kt % 2:
                    pe.wait_ge(p_copied_dve, count(b, DVE_PER_SEQ, DVE_KEYS.index((n, kt)) + 1))
                else:
                    pe.wait_ge(p_copied_act, count(b, ACT_PER_SEQ, ACT_KEYS.index((n, kt)) + 1))

            def turn_p(b, n, kt, bank):
                if kt == 0:
                    pe.wait_ge(exp_done, count(b, 2 * NU, 2 * n + 2))
                for h in range(HG):
                    last = turn(ps[:, bank, h * P:(h + 1) * P], Pr[:, n % 2, h, kt * P:(kt + 1) * P], ident[:, :])
                last.then_inc(p_turned, 1)

            def values(b, n, kt):
                qt, g, _ = unit(n)
                wait_copied(b, n, kt)
                if kt == 0:
                    pe.wait_ge(attn_ready, count(b, NU, n - 1))
                if (n % NU, kt) == (0, 0):
                    pe.wait_ge(vb_ready, b + (1 + n // NU))
                for h in range(HG):
                    last = mm(ps[h * HD:(h + 1) * HD, 6 + n % 2, 0:P], Vb[:, kt, g * HD:(g + 1) * HD],
                              PT[:, KEYS.index((n, kt)) % 4, h * P:(h + 1) * P], start=(kt == 0), stop=end_of_unit(n, kt))
                last.then_inc(pv_done, 1)
                if end_of_unit(n, kt):
                    pe.wait_ge(rinv_ready, count(b, NU, n + 1))
                    turn(ps[:, 6 + n % 2, P:2 * P], rE[:, n % 4, :, :].rearrange("p h c -> p (h c)"), ident[:, :]).then_inc(o_done, 1)

            def project(b, qt, bank):
                pe.wait_ge(attn_low, count(b, TB, qt + 1))
                for g in range(NG):
                    last = three(ps[:, bank, :], aTh[:, qt % 2, g, :], aTl[:, qt % 2, g, :], woh[:, g, :], wol[:, g, :], g == 0, g == NG - 1)
                last.then_inc(proj_done, 1)

            def attend(b, steps):
                for i, (kind, n, k) in enumerate(steps):
                    if kind == "scores":
                        scores(b, n, k)
                    elif kind == "values":
                        values(b, n, k)
                    elif kind == "turn":
                        bank_free(b, steps, i)
                        turn_p(b, n, k, bank_of(steps, i))
                    elif kind == "project":
                        bank_free(b, steps, i)
                        project(b, n, bank_of(steps, i))

            pe.wait_ge(kt_loaded, 16 * 3)
            scores(0, 0, 0)
            scores(0, 0, 1)
            attend(0, FIRST)
            with pe.Fori(0, B - 1) as b:
                attend(b, BODY)
            attend(B - 1, LAST)
            end_phase(pe, 4)

            for b in range(2):
                turn_last_rows(range(TB * b, TB * b + TB))
                pe.wait_ge(xt_low, 2 * NT + TB * (b + 1))
                gate_up(2, 0, b)
            turn_last_rows(range(2 * TB, NT))
            pe.wait_ge(xt_low, 3 * NT)
            down(2, 0, 0)
            for j in range(1, 2 * B):
                gate_up(2, 0, j + 1)
                down(2, 0, j)
            ffn(2, True, 1)

        @block.scalar
        def _(act):
            func = nc.scalar.activation
            chained, roots = [0], [0]

            def link(ins):
                chained[0] += 1
                ins.then_inc(act_chain, 1)
                act.wait_ge(act_chain, chained[0])

            def root():
                roots[0] += 1
                act.wait_ge(root_asked, roots[0])
                func(sd[:, :], vv[:, :], ACT.Sqrt).then_inc(root_done, 1)

            def last_rows_high(tiles):
                for t in tiles:
                    act.wait_ge(xt_turned, 2 * NT + t + 1)
                    func(xTh[:, :, t * P:(t + 1) * P], ps[:, row_bank(t), :].rearrange("p (k n) -> p k n", k=KD), ACT.Copy).then_inc(xt_high, 1)

            def split_high(part, T, w, m, used=None):
                if m == 0 and used is not None:
                    act.wait_ge(out_done, used + CREDIT)
                if part < 2 and m < 2:
                    for d in range(KD):
                        dsl = slice(d * P, (d + 1) * P)
                        last = func(wh[:, w, m, dsl], raw[:, w, m, dsl], ACT.Copy, scale=rnp[:, part, d:d + 1])
                else:
                    last = func(wh[:, w, m, :], raw[:, w, m, :], ACT.Copy)
                last.then_inc(w_high, 1)

            def step(part, i, j, chain_end):
                s, q = step_no(part, i, j), j % 2
                act.wait_ge(gate_done, s + 1)
                act.wait_ge(hid_ready, s + (CREDIT - 1))
                func(act_o[:, q, :], ps[:, q, :], ACT.Silu if part == 2 else ACT.Gelu_apprx_tanh).then_inc(act_ready, 1)
                nxt = next_tile(part, i, j, chain_end)
                if nxt:
                    p2, T, w, used = nxt
                    if j % B == 1:
                        act.wait_ge(w_loaded[w], i * 16 + 16 * ((TILE0[part] + j // B + 1) // 2 + 1))
                    split_high(p2, T, w, j % B - 1, used)
                act.wait_ge(hid_ready, s + (CREDIT + 1))
                act.wait_ge(out_done, s + (CREDIT - 1))
                func(hidh[:, q, :], hid[:, q, :], ACT.Copy).then_inc(hid_high, 1)

            def ffn(part, chain_end, first=0):
                with act.Fori(first, HT // 2 - 1) as i:
                    for j in range(2 * B):
                        step(part, i, j, chain_end)
                for j in range(2 * B):
                    if j == 2 * B - 1 and not chain_end:
                        slots_high(-1, 0)
                    step(part, HT // 2 - 1, j, chain_end)
                if not chain_end:
                    slots_high(-1, 1)

            def slots_high(k, half):
                for i in (2 * half, 2 * half + 1):
                    act.wait_ge(xg_turned, k * TB + (TB + i + 1))
                    func(xTh[:, :, i * P:(i + 1) * P], ps[:, i % 2 * 2, :].rearrange("p (k n) -> p k n", k=KD), ACT.Copy).then_inc(xg_high, 1)

            def expert_gelu(k, h):
                act.wait_ge(gate_done, k * 2 + (STEPS + h + 1))
                func(act_o[:, h, :], ps[:, h, :], ACT.Gelu_apprx_tanh).then_inc(act_ready, 1)

            def expert_hidden_high(k, h):
                act.wait_ge(hid_ready, k * 2 + (STEPS + h + CREDIT + 1))
                act.wait_ge(out_done, k * 2 + (STEPS + h + CREDIT - 1))
                func(hidh[:, h, :], hid[:, h, :], ACT.Copy).then_inc(hid_high, 1)

            def expert_weights_high(k, h, ms):
                for m in ms:
                    if m == 0:
                        act.wait_ge(w_loaded[h], k * 16 + 16 * (HT // 2 + 2))
                        act.wait_ge(up_done, k * 2 + (STEPS + h + 1))
                    if m == 2:
                        act.wait_ge(out_done, k * 2 + (STEPS + h + 1 + CREDIT))
                    split_high(1, None, h, m)

            def experts():
                expert_weights_high(-1, 1, (0, 1, 2))
                with act.Fori(0, NB - 1) as k:
                    expert_gelu(k, 0)
                    expert_hidden_high(k, 0)
                    expert_weights_high(k, 0, (0, 1))
                    expert_gelu(k, 1)
                    slots_high(k, 0)
                    expert_hidden_high(k, 1)
                    slots_high(k, 1)
                    expert_weights_high(k, 0, (2,))
                    expert_weights_high(k, 1, (0, 1, 2))
                for h in range(2):
                    expert_gelu(NB - 1, h)
                    expert_hidden_high(NB - 1, h)

            def squares(k, a, t):
                link(func(sq[:, :], a[:, t, :], ACT.Square, accum_out=ssq[:, k, t:t + 1]))

            def first_split(m):
                if m < 2:
                    for d in range(KD):
                        dsl = slice(d * P, (d + 1) * P)
                        last = func(wh[:, 0, m, dsl], raw[:, 0, m, dsl], ACT.Copy, scale=rnp[:, 0, d:d + 1])
                else:
                    last = func(wh[:, 0, m, :], raw[:, 0, m, :], ACT.Copy)
                last.then_inc(w_high, 1)

            def a_root(kinds):
                roots[0] += 1
                act.wait_ge(root_asked, roots[0])
                func(a_sd[:, kinds, :], a_vv[:, kinds, :], ACT.Sqrt).then_inc(root_done, 1)
                act.wait_ge(scales_ready, roots[0])

            def g_root(b):
                kinds = closing_kinds(b)
                roots[0] += 1
                act.wait_ge(root_asked, roots[0])
                func(a_sd[:, kinds, :], a_vv[:, kinds, :], ACT.Sqrt).then_inc(root_done, 1)
                g_turns[0] += 1
                act.wait_ge(g_scaled, g_turns[0])

            g_turns = [0]

            def project_context(b):
                act.wait_ge(ctxT_loaded, 16 * (b + 1))
                if b:
                    act.wait_ge(kv_done, b)
                func(cTh[:, :], cT32[:, :], ACT.Copy).then_inc(ctx_high, 1)
                act.wait_ge(kv_done, b + 1)
                if b:
                    act.wait_ge(kv_turned, b)
                    act.wait_ge(kvT_low, b)
                func(kvf[:, :], ps[:, 2, :], ACT.Identity, bias=bk[:, 0:1]).then_inc(kv_biased, 1)
                act.wait_ge(kv_biased, b + 1)
                func(kvTh[:, b, :], kvf[:, :], ACT.Copy).then_inc(kvT_high, 1)
                act.wait_ge(kv_turned, b + 1)
                func(kvh[:, TB * b:TB * (b + 1), :], ps[:, 3, :].rearrange("p (j c) -> p j c", c=C), ACT.Copy).then_inc(kv_high, 1)

            def normed_row(k, b, i):
                m, t = row_no(k, b, i), TB * b + i
                if m >= 2:
                    act.wait_ge(xt_turned, m - 1)
                    if xhat_stores(m - 2):
                        act.wait_ge(xhat_stored[m % 2], 16 * xhat_stores(m - 2))
                func(xn[:, m % 2, :], x[:, t, :], ACT.Identity, bias=a_nmr[:, 2 * k, i:i + 1], scale=a_rs[:, 2 * k, i:i + 1]).then_inc(xn_ready, 1)

            def row_high(k, b, i):
                m, t = row_no(k, b, i), TB * b + i
                act.wait_ge(xt_turned, m + 1)
                if k:
                    act.wait_ge(pkv_done, b + 1)
                func(xTh[:, :, t * P:(t + 1) * P], ps[:, m % 2, :].rearrange("p (k n) -> p k n", k=KD), ACT.Copy).then_inc(xt_high, 1)

            def products_high(b):
                act.wait_ge(pkv_done, b + 1)
                if b:
                    act.wait_ge(sim_done, TB * b)
                func(oTh[:, :], ps[:, 2, :], ACT.Copy).then_inc(pkv_high, 1)

            def scaled(t):
                i = t % TB
                act.wait_ge(sim_done, t + 1)
                if t >= TB:
                    act.wait_ge(a_weighed, t - TB + 1)
                func(va[:, i, :], ps[:, 4 + i, :], ACT.Identity, bias=a_nmr[:, 1, i:i + 1], scale=a_rs[:, 1, i:i + 1]).then_inc(a_scaled, 1)

            def exponential(t):
                act.wait_ge(a_max, t + 1)
                if t >= TB:
                    act.wait_ge(a_added, t - TB + 1)
                func(vc[:, t % TB, :], vb[:, t % TB, :], ACT.Exp, bias=nma[:, t:t + 1], accum_out=sma[:, t:t + 1]).then_inc(a_exp, 1)

            def norm_rows(k, b, before=None):
                for i in range(TB):
                    if before:
                        before(i)
                    normed_row(k, b, i)
                    if i:
                        row_high(k, b, i - 1)
                row_high(k, b, TB - 1)

            act.wait_ge(wk_loaded, 32)
            func(wkh[:, :], wk32[:, :], ACT.Copy).then_inc(wk_high, 1)
            project_context(0)
            a_root(turn_kinds(-1))
            norm_rows(0, 0)
            products_high(0)
            for b in range(B):
                if b + 1 < B:
                    project_context(b + 1)
                a_root(turn_kinds(b))
                if b + 1 < B:
                    norm_rows(0, b + 1, lambda i: scaled(TB * b + i))
                else:
                    for i in range(TB):
                        scaled(TB * b + i)
                for i in range(TB):
                    exponential(TB * b + i)
                if b + 1 < B:
                    products_high(b + 1)
                if b == 1:
                    act.wait_ge(ctx_loaded, 16)
                    for t in range(NT):
                        link(func(ksq[:, :], ctx_rows[:, t, :], ACT.Square, accum_out=kss[:, t:t + 1]))
                    act.sem_inc(squares_ready, 1)
                if b:
                    norm_rows(1, b - 1)
            act.wait_ge(rw_scaled, 1)
            func(rwh[:, :, :], rws[:, :, :], ACT.Copy).then_inc(rw_high, 1)
            end_phase(act, 1)
            a_root(turn_kinds(B))
            norm_rows(1, B - 1)
            root()
            act.wait_ge(w_loaded[0], 16)
            for m in range(3):
                first_split(m)

            for b in range(B):
                act.wait_ge(lg_done, b + 1)
                func(lgT[:, b, :], ps[0:E, 4 + b, :], ACT.Copy).then_inc(lg_copied, 1)
            act.wait_ge(exp_asked, 1)
            func(key[:, :, :], lg2[:, :, :], ACT.Exp).then_inc(exp_taken, 1)
            ffn(0, False)
            experts()
            end_phase(act, 2)

            def part_squares(b):
                for t in range(b * TB, b * TB + TB):
                    act.wait_ge(y_summed, t + 1)
                    squares(1, accM, t)
                act.sem_inc(part_squared, 1)

            def part_root(b):
                ts = slice(b * TB, b * TB + TB)
                roots[0] += 1
                act.wait_ge(root_asked, roots[0])
                func(psd[:, :, ts], pv[:, :, ts], ACT.Sqrt).then_inc(root_done, 1)

            for t in range(NT):
                squares(0, accD, t)
            part_squares(0)
            part_root(0)
            part_squares(1)
            part_root(1)

            def sum_squares(t):
                act.wait_ge(g_sum, t + 1)
                if t:
                    act.wait_ge(sum_squared, t)
                func(sq[:, :], accD[:, t, :], ACT.Square, accum_out=ssq[:, 2, t:t + 1]).then_inc(sum_squared, 1)

            def query_row(t):
                if t >= TB:
                    act.wait_ge(qa_ready, t - TB + 1)
                    act.wait_ge(qb_ready, t - TB + 1)
                func(u[:, t % TB, :], x[:, t, :], ACT.Identity, bias=a_nmr[:, 1, t % TB:t % TB + 1],
                     scale=a_rs[:, 1, t % TB:t % TB + 1]).then_inc(u_ready, 1)

            def query_high(t):
                act.wait_ge(q_turned, t + 1)
                if t >= 2:
                    act.wait_ge(q_high_stored[t % 2], 16 * (t // 2))
                    act.wait_ge(q_low, t - 1)
                func(th[:, t % 2, :], ps[:, t % TB, :], ACT.Copy).then_inc(q_high, 1)

            for i in range(TB):
                sum_squares(i)

            def keys_high(b):
                if b == 0:
                    act.wait_ge(wo_loaded, 16)
                    func(woh[:, :, :], wo32[:, :, :], ACT.Copy).then_inc(wo_high, 1)
                if b < B:
                    act.wait_ge(k_turned, b + 1)
                    if b >= 2:
                        act.wait_ge(k_parts_stored, b - 1)
                    func(th[:, b % 2, :], ps[:, b % 2, :], ACT.Copy).then_inc(k_high, 1)

            for b in range(-1, B):
                if b == 0:
                    act.wait_ge(wo_low, 1)
                    act.wait_ge(k_parts_stored, B)
                g_root(b)
                for i in range(TB + 2):
                    if b >= 0 and i < TB:
                        query_row(b * TB + i)
                    if b >= 0 and i >= 2:
                        query_high(b * TB + i - 2)
                    if b + 2 < B and 1 <= i <= TB:
                        sum_squares((b + 2) * TB + i - 1)
                    if b == -1:
                        keys_high(i)
                if b == -1:
                    act.wait_ge(sum_squared, 2 * TB)
                    part_squares(2)
                    part_root(2)
                    part_squares(3)
                    part_root(3)
            for s_ in (exp_done, attn_high, p_copied_act, rt_copied):
                act.sem_inc(s_, LEAD)
            end_phase(act, 3)

            def exponential(b, n, hp):
                act.wait_ge(min_ready, count(b, 2 * NU, 2 * n + hp + 1))
                if hp == 0:
                    act.wait_ge(p_turned, count(b, PER_SEQ, KEYS.index((n - 1, 0)) if n else 0))
                    act.wait_ge(rinv_ready, count(b, NU, n - 3))
                for h in (2 * hp, 2 * hp + 1):
                    last = func(Pr[:, n % 2, h, 0:(unit(n)[0] + 1) * P], ps[:, h, 0:(unit(n)[0] + 1) * P], ACT.Exp,
                                bias=mnb[:, n % 2, h:h + 1], scale=-1.0, accum_out=smb[:, n % 4, h:h + 1])
                last.then_inc(exp_done, 1)

            def copy_p(b, n, kt, bank):
                act.wait_ge(p_turned, count(b, PER_SEQ, KEYS.index((n, kt)) + 1))
                act.wait_ge(pv_done, count(b, PER_SEQ, KEYS.index((n, kt)) - 3))
                func(PT[:, KEYS.index((n, kt)) % 4, :], ps[:, bank, :], ACT.Copy).then_inc(p_copied_act, 1)

            def copy_inverses(b, n):
                act.wait_ge(o_done, count(b, NU, n + 1))
                act.wait_ge(attn_ready, count(b, NU, n - 1))
                func(rT[:, n % 2, :], ps[:, 6 + n % 2, P:2 * P], ACT.Copy).then_inc(rt_copied, 1)

            def attend(b, steps):
                due, finished = [], []
                for i, (kind, n, k) in enumerate(steps):
                    if kind == "scores":
                        due.append((n, k))
                    elif kind == "turn":
                        if k % 2 == 0:
                            copy_p(b, n, k, bank_of(steps, i))
                            if due:
                                exponential(b, *due.pop(0))
                        if end_of_unit(n, k):
                            while due:
                                exponential(b, *due.pop(0))
                        while finished:
                            copy_inverses(b, finished.pop(0))
                    elif kind == "values":
                        if end_of_unit(n, k):
                            finished.append(n)
                    elif kind == "split":
                        while finished:
                            copy_inverses(b, finished.pop(0))
                        act.wait_ge(attn_ready, count(b, NU, NG * (n + 1)))
                        act.wait_ge(proj_done, count(b, TB, n - 1))
                        func(aTh[:, n % 2, :, :], aT[:, n % 2, :, :], ACT.Copy).then_inc(attn_high, 1)

            exponential(0, 0, 0)
            exponential(0, 0, 1)
            attend(0, FIRST)
            with act.Fori(0, B - 1) as b:
                attend(b, BODY)
            attend(B - 1, LAST)
            end_phase(act, 4)

            root()
            last_rows_high(range(TB))
            act.wait_ge(w_loaded[0], 16 * (TILE0[2] // 2 + 1))
            for m in range(3):
                split_high(2, None, 0, m)
            last_rows_high(range(TB, 2 * TB))
            step(2, 0, 0, True)
            last_rows_high(range(2 * TB, NT))
            for j in range(1, 2 * B):
                step(2, 0, j, True)
            ffn(2, True, 1)

        @block.vector
        def _(dve):
            V_ = nc.vector
            chained, roots = [0], [0]

            def link(ins):
                chained[0] += 1
                ins.then_inc(dve_chain, 1)
                dve.wait_ge(dve_chain, chained[0])

            def newton(dst, v, root, y, z):
                roots[0] += 1
                dve.sem_inc(root_asked, 1)
                dve.wait_ge(root_done, roots[0])
                link(V_.reciprocal(y, root))
                link(V_.tensor_tensor(out=z, in0=y, in1=y, op=ALU.mult))
                link(V_.tensor_tensor(out=z, in0=z, in1=v, op=ALU.mult))
                link(V_.tensor_scalar(z, z, -0.5, 1.5, ALU.mult, ALU.add))
                link(V_.tensor_tensor(out=dst, in0=y, in1=z, op=ALU.mult))

            def rsqrt(dst):
                newton(dst, vv[:, :], sd[:, :], r0[:, :], r1[:, :])

            def a_deviations(kinds):
                for k in range(kinds.start, kinds.stop):
                    for i in range(TB):
                        last = V_.bn_aggr(a_mv[:, k, i, :], a_bst[:, k, i, :])
                link(last)
                norms = ((1.0, LN_EPS), (SIM_SCALE * SIM_SCALE, 1e-6), (1.0 + RMS0_EPS, RMS0_EPS * LN_EPS))
                for k in range(kinds.start, kinds.stop):
                    last = V_.tensor_scalar(a_vv[:, k, :], a_mv[:, k, :, 1], *norms[k], ALU.mult, ALU.add)
                link(last)
                newton(a_rs[:, kinds, :], a_vv[:, kinds, :], a_sd[:, kinds, :], a_r0[:, kinds, :], a_r1[:, kinds, :])
                if kinds.start <= 1 < kinds.stop:
                    link(V_.tensor_scalar(a_rs[:, 1, :], a_rs[:, 1, :], SIM_SCALE, None, ALU.mult))
                V_.scalar_tensor_tensor(out=a_nmr[:, kinds, :], in0=a_mv[:, kinds, :, 0], scalar=-1.0, in1=a_rs[:, kinds, :],
                                        op0=ALU.mult, op1=ALU.mult).then_inc(scales_ready, 1)

            def deviations(mul, add, factor=None):
                for t in range(NT):
                    last = V_.bn_aggr(mv[:, t, :], bst[:, t, :])
                link(last)
                link(V_.tensor_scalar(vv[:, :], mv[:, :, 1], mul, add, ALU.mult, ALU.add))
                rsqrt(rs[:, :])
                if factor is not None:
                    link(V_.tensor_scalar(rs[:, :], rs[:, :], factor, None, ALU.mult))
                link(V_.scalar_tensor_tensor(out=nmr[:, :], in0=mv[:, :, 0], scalar=-1.0, in1=rs[:, :], op0=ALU.mult, op1=ALU.mult))

            def last_rows(tiles):
                def low(t):
                    dve.wait_ge(xt_high, 2 * NT + t + 1)
                    V_.tensor_tensor(out=xTl[:, :, t * P:(t + 1) * P], in0=ps[:, row_bank(t), :].rearrange("p (k n) -> p k n", k=KD),
                                     in1=xTh[:, :, t * P:(t + 1) * P].bitcast(F32), op=ALU.subtract).then_inc(xt_low, 1)
                for t in tiles:
                    dve.wait_ge(xt_turned, 2 * NT + t - 1)
                    V_.tensor_scalar(xn[:, t % 2, :], x[:, t, :], mv[:, t, 0:1], rs[:, t:t + 1], ALU.subtract, ALU.mult).then_inc(xn_ready, 1)
                    if t > tiles.start + 1:
                        low(t - 2)
                low(tiles.stop - 2)
                low(tiles.stop - 1)

            def split_low(part, T, w, m):
                dve.wait_ge(w_high, T * 3 + (m + 1))
                if part < 2 and m < 2:
                    for d in range(KD):
                        dsl = slice(d * P, (d + 1) * P)
                        last = V_.scalar_tensor_tensor(out=wl[:, w, m, dsl], in0=raw[:, w, m, dsl], scalar=rnp[:, part, d:d + 1],
                                                       in1=wh[:, w, m, dsl].bitcast(F32), op0=ALU.mult, op1=ALU.subtract)
                else:
                    last = V_.tensor_tensor(out=wl[:, w, m, :], in0=raw[:, w, m, :], in1=wh[:, w, m, :].bitcast(F32), op=ALU.subtract)
                last.then_inc(w_low, 1)

            def hidden(part, i, j, nxt):
                s, q, b = step_no(part, i, j), j % 2, j % B
                dve.wait_ge(act_ready, s + 1)
                dve.wait_ge(up_done, s + 1)
                dve.wait_ge(hid_low, s + (CREDIT - 1))
                V_.tensor_tensor(out=hid[:, q, :], in0=act_o[:, q, :], in1=ps[:, 2 + q, :], op=ALU.mult).then_inc(hid_ready, 1)
                if nxt:
                    split_low(nxt[0], nxt[1], nxt[2], j % B - 1)
                dve.wait_ge(hid_high, s + 1)
                V_.tensor_tensor(out=hidl[:, q, :], in0=hid[:, q, :], in1=hidh[:, q, :].bitcast(F32), op=ALU.subtract).then_inc(hid_low, 1)

            def add(part, i, j):
                s, b = step_no(part, i, j), j % B
                acc = (accD, None, x)[part][:, TB * b:TB * (b + 1), :]
                dve.wait_ge(out_done, s + (CREDIT + 1))
                dve.wait_ge(acc_added, s + (CREDIT - 1))
                V_.tensor_tensor(out=acc, in0=acc, in1=ps[:, 4:8, :], op=ALU.add).then_inc(acc_added, 1)

            def ffn(part, chain_end, first=0):
                with dve.Fori(first, HT // 2 - 1) as i:
                    for j in range(2 * B):
                        hidden(part, i, j + 1, next_tile(part, i, j + 1, chain_end))
                        add(part, i, j)
                i = HT // 2 - 1
                for j in range(2 * B):
                    if j == 2 * B - 2 and not chain_end:
                        slots_low(-1, 0)
                    if j < 2 * B - 1:
                        hidden(part, i, j + 1, next_tile(part, i, j + 1, chain_end))
                    elif not chain_end:
                        slots_low(-1, 1)
                    add(part, i, j)

            def slots_low(k, half):
                for i in (2 * half, 2 * half + 1):
                    dve.wait_ge(xg_high, k * TB + (TB + i + 1))
                    V_.tensor_tensor(out=xTl[:, :, i * P:(i + 1) * P], in0=ps[:, i % 2 * 2, :].rearrange("p (k n) -> p k n", k=KD),
                                     in1=xTh[:, :, i * P:(i + 1) * P].bitcast(F32), op=ALU.subtract).then_inc(xg_low, 1)

            def expert_hidden(k, h):
                s = k * 2 + (STEPS + h)
                dve.wait_ge(act_ready, s + 1)
                dve.wait_ge(up_done, s + 1)
                V_.tensor_tensor(out=hid[:, h, :], in0=act_o[:, h, :], in1=ps[:, 2 + h, :], op=ALU.mult).then_inc(hid_ready, 1)

            def expert_hidden_low(k, h):
                dve.wait_ge(hid_high, k * 2 + (STEPS + h + 1))
                V_.tensor_tensor(out=hidl[:, h, :], in0=hid[:, h, :], in1=hidh[:, h, :].bitcast(F32), op=ALU.subtract).then_inc(hid_low, 1)

            def expert_weights_low(k, h, ms):
                for m in ms:
                    split_low(1, k * 2 + (HT + 2 + h), h, m)

            def take_products(k):
                dve.wait_ge(out_done, k * 2 + (STEPS + 2 + CREDIT))
                dve.wait_ge(y_free, k + CREDIT)
                V_.tensor_copy(yo, ps[:, 4:8, :]).then_inc(y_ready, 1)
                dve.wait_ge(y_ready, k + 1)
                dve.sem_inc(acc_added, 2)

            def experts():
                expert_weights_low(-1, 1, (0, 1, 2))
                with dve.Fori(0, NB - 1) as k:
                    expert_hidden(k, 0)
                    expert_hidden_low(k, 0)
                    expert_weights_low(k, 0, (0, 1))
                    expert_hidden(k, 1)
                    slots_low(k, 0)
                    expert_hidden_low(k, 1)
                    slots_low(k, 1)
                    expert_weights_low(k, 0, (2,))
                    expert_weights_low(k, 1, (0, 1))
                    take_products(k)
                    expert_weights_low(k, 1, (2,))
                for h in range(2):
                    expert_hidden(NB - 1, h)
                    expert_hidden_low(NB - 1, h)
                take_products(NB - 1)

            for s_, k in ((hid_low, CREDIT), (y_free, CREDIT), (acc_added, CREDIT), (hid_ready, CREDIT),
                          *((s_, LEAD) for s_ in (min_ready, recip_done, rinv_ready, p_copied_dve, attn_ready, attn_low, proj_added))):
                dve.sem_inc(s_, k)

            dve.wait_ge(wk_high, 1)
            V_.tensor_tensor(out=wkl[:, :], in0=wk32[:, :], in1=wkh[:, :].bitcast(F32), op=ALU.subtract)
            def project_context(b):
                dve.wait_ge(ctx_high, b + 1)
                V_.tensor_tensor(out=cTl[:, :], in0=cT32[:, :], in1=cTh[:, :].bitcast(F32), op=ALU.subtract).then_inc(ctx_low, 1)
                dve.wait_ge(kvT_high, b + 1)
                V_.tensor_tensor(out=kvTl[:, b, :], in0=kvf[:, :], in1=kvTh[:, b, :].bitcast(F32), op=ALU.subtract).then_inc(kvT_low, 1)
                dve.wait_ge(kv_high, b + 1)
                V_.tensor_tensor(out=kvl[:, TB * b:TB * (b + 1), :], in0=ps[:, 3, :].rearrange("p (j c) -> p j c", c=C),
                                 in1=kvh[:, TB * b:TB * (b + 1), :].bitcast(F32), op=ALU.subtract).then_inc(kv_low, 1)

            def row_stats(k, b):
                for i in range(TB):
                    V_.bn_stats(a_bst[:, 2 * k, i, :], x[:, TB * b + i, :])

            def row_low(k, b, i):
                m, t = row_no(k, b, i), TB * b + i
                dve.wait_ge(xt_high, m + 1)
                V_.tensor_tensor(out=xTl[:, :, t * P:(t + 1) * P], in0=ps[:, m % 2, :].rearrange("p (k n) -> p k n", k=KD),
                                 in1=xTh[:, :, t * P:(t + 1) * P].bitcast(F32), op=ALU.subtract).then_inc(xt_low, 1)

            def products_low(b):
                dve.wait_ge(pkv_high, b + 1)
                V_.tensor_tensor(out=oTl[:, :], in0=ps[:, 2, :], in1=oTh[:, :].bitcast(F32), op=ALU.subtract).then_inc(pkv_low, 1)

            def weighed(t):
                i = t % TB
                dve.wait_ge(a_weighed, t + 1)
                link(V_.tensor_tensor_reduce(vb[:, i, :], vb[:, i, :], betaB[:, :], 1.0, -3.0e38, ALU.add, ALU.max, mxa[:, t:t + 1]))
                V_.tensor_scalar(nma[:, t:t + 1], mxa[:, t:t + 1], -1.0, None, ALU.mult).then_inc(a_max, 1)

            def residual(t):
                i = t % TB
                dve.wait_ge(a_exp, t + 1)
                link(V_.reciprocal(rca[:, t:t + 1], sma[:, t:t + 1]))
                V_.scalar_tensor_tensor(out=x[:, t, :], in0=vc[:, i, :], scalar=rca[:, t:t + 1], in1=x[:, t, :],
                                        op0=ALU.mult, op1=ALU.add).then_inc(a_added, 1)

            project_context(0)
            dve.wait_ge(x_loaded[0], 16)
            row_stats(0, 0)
            dve.drain()
            a_deviations(turn_kinds(-1))
            for i in range(TB):
                row_low(0, 0, i)
            products_low(0)
            for b in range(B):
                t = TB * b
                if b + 1 < B:
                    project_context(b + 1)
                    dve.wait_ge(x_loaded[b + 1], 16)
                    row_stats(0, b + 1)
                for i in range(TB):
                    dve.wait_ge(sim_done, t + i + 1)
                    last = V_.bn_stats(a_bst[:, 1, i, :], ps[:, 4 + i, :])
                link(last)
                a_deviations(turn_kinds(b))
                for i in range(TB):
                    if b + 1 < B:
                        row_low(0, b + 1, i)
                    weighed(t + i)
                residual(t)
                residual(t + 1)
                if b + 1 < B:
                    products_low(b + 1)
                residual(t + 2)
                residual(t + 3)
                dve.wait_ge(a_added, t + TB)
                row_stats(1, b)
                if b:
                    for i in range(TB):
                        row_low(1, b - 1, i)
            dve.wait_ge(small_loaded, 80)
            link(V_.tensor_scalar(rsc[:, :], rsc[:, :], float(D) ** -0.5, None, ALU.mult))
            for d in range(KD):
                last = V_.tensor_scalar(rws[:, d, :], rw32[:, d, :], rsc[:, d:d + 1], None, ALU.mult)
            last.then_inc(rw_scaled, 1)
            dve.wait_ge(rw_high, 1)
            V_.tensor_tensor(out=rwl[:, :, :], in0=rws[:, :, :], in1=rwh[:, :, :].bitcast(F32), op=ALU.subtract).then_inc(rw_low, 1)
            end_phase(dve, 1)
            a_deviations(turn_kinds(B))
            for i in range(TB):
                row_low(1, B - 1, i)

            dve.wait_ge(squares_ready, 1)
            link(V_.tensor_scalar(vv[:, :], kss[:, :], 1.0 / C, RMS1_EPS, ALU.mult, ALU.add))
            rsqrt(krs[:, :])
            dve.sem_inc(k_scaled, 1)
            for m in range(3):
                split_low(0, 0, 0, m)
            dve.wait_ge(lg_turned, 1)
            dve.wait_ge(consts_ready, 2)

            def over_e(a):
                return a.unsqueeze(2).broadcast_to((P, NT, E))

            descB = desc[:, :].unsqueeze(1).broadcast_to((P, NT, E))
            link(V_.tensor_copy(lg[:, :, :], ps[:, 3, 0:NT * E].rearrange("p (t e) -> p t e", e=E)))

            def largest(src, m, oh):
                link(V_.tensor_reduce(m[:, :], src[:, :, :], AX.X, ALU.max))
                link(V_.tensor_tensor(out=key[:, :, :], in0=src[:, :, :], in1=over_e(m[:, :]), op=ALU.is_equal))
                link(V_.tensor_tensor(out=key[:, :, :], in0=key[:, :, :], in1=descB, op=ALU.mult))
                link(V_.tensor_reduce(pk[:, :], key[:, :, :], AX.X, ALU.max))
                link(V_.tensor_tensor(out=oh[:, :, :], in0=key[:, :, :], in1=over_e(pk[:, :]), op=ALU.is_equal))

            largest(lg, m1, oh1)
            link(V_.scalar_tensor_tensor(out=lg2[:, :, :], in0=oh1[:, :, :], scalar=-3.0e38, in1=lg[:, :, :], op0=ALU.mult, op1=ALU.add))
            largest(lg2, m2, oh2)
            V_.tensor_tensor(out=lg2[:, :, :], in0=lg[:, :, :], in1=over_e(m1[:, :]), op=ALU.subtract).then_inc(exp_asked, 1)
            V_.tensor_tensor(out=both[:, :, :], in0=oh1[:, :, :], in1=oh2[:, :, :], op=ALU.add).then_inc(both_ready, 1)
            dve.wait_ge(both_ready, 1)
            dve.wait_ge(exp_taken, 1)
            link(V_.tensor_tensor(out=key[:, :, :], in0=key[:, :, :], in1=both[:, :, :], op=ALU.mult))
            link(V_.tensor_reduce(m1[:, :], key[:, :, :], AX.X, ALU.add))
            link(V_.reciprocal(m2[:, :], m1[:, :]))
            link(V_.tensor_tensor(out=key[:, :, :], in0=key[:, :, :], in1=over_e(m2[:, :]), op=ALU.mult))
            dve.wait_ge(small_loaded, 96)
            link(V_.tensor_tensor(out=lg[:, :, :], in0=key[:, :, :], in1=pesB[:, :].unsqueeze(1).broadcast_to((P, NT, E)), op=ALU.mult))
            dve.wait_ge(ranks_done, 1)
            V_.tensor_copy(pos[:, :, :], ps[:, 4, 0:NT * E].rearrange("p (t e) -> p t e", e=E))
            link(V_.tensor_copy(tot[:, :, :], ps[:, 4, NT * E:2 * NT * E].rearrange("p (t e) -> p t e", e=E)))
            V_.memset(before[:, 0, :], 0.0)
            V_.memset(first[:, :], 0.0)
            V_.memset(tile_f[:, :], 0.0)
            link(V_.memset(blocks[:, :], 1.0))
            dve.wait_ge(acc_zero, 1)
            hidden(0, 0, 0, None)

            def tokens_before(tiles):
                for t in tiles:
                    link(V_.tensor_tensor(out=before[:, t, :], in0=before[:, t - 1, :], in1=tot[:, t - 1, :], op=ALU.add))
                if tiles.stop == NT:
                    link(V_.tensor_tensor(out=tot[:, 0, :], in0=before[:, NT - 1, :], in1=tot[:, NT - 1, :], op=ALU.add))

            def expert_blocks():
                for k in range(1, NT * P // S):
                    link(V_.scalar_tensor_tensor(out=blocks[:, :], in0=tot[:, 0, :], scalar=float(S * k), in1=blocks[:, :], op0=ALU.is_gt, op1=ALU.add))
                for e in range(1, E):
                    link(V_.tensor_tensor(out=first[:, e:e + 1], in0=first[:, e - 1:e], in1=blocks[:, e - 1:e], op=ALU.add))

            def places():
                link(V_.tensor_tensor(out=pos[:, :, :], in0=pos[:, :, :], in1=before[:, :, :], op=ALU.add))
                link(V_.scalar_tensor_tensor(out=pos[:, :, :], in0=first[:, :].unsqueeze(1).broadcast_to((P, NT, E)), scalar=float(S), in1=pos[:, :, :],
                                             op0=ALU.mult, op1=ALU.add))

            def slots_and_weights(k, oh):
                for src, dst in ((pos, slot_f), (lg, wgt)):
                    link(V_.tensor_tensor(out=key[:, :, :], in0=src[:, :, :], in1=oh[:, :, :], op=ALU.mult))
                    link(V_.tensor_reduce(dst[:, k, :], key[:, :, :], AX.X, ALU.add))

            def block_tiles(experts_):
                for e in experts_:
                    link(V_.scalar_tensor_tensor(out=tile_f[:, :], in0=block_no[:, :], scalar=first[:, e:e + 1], in1=tile_f[:, :], op0=ALU.is_ge, op1=ALU.add))
                if experts_.stop == E:
                    link(V_.tensor_scalar(tile_f[:, :], tile_f[:, :], 2.0, float(HT), ALU.mult, ALU.add))
                    link(V_.tensor_copy(slot[:, :, :], slot_f[:, :, :]))
                    V_.tensor_copy(tile_no[:, :], tile_f[:, :]).then_inc(slots_ready, 1)

            for j in range(2 * B):
                hidden(0, 0, j + 1, next_tile(0, 0, j + 1, False))
                if j == 0:
                    tokens_before(range(1, NT // 2))
                elif j == 1:
                    tokens_before(range(NT // 2, NT))
                elif j == 2:
                    expert_blocks()
                elif j == 3:
                    places()
                    slots_and_weights(0, oh1)
                elif j == 4:
                    slots_and_weights(1, oh2)
                elif j == 5:
                    dve.wait_ge(consts_ready, 3)
                    block_tiles(range(1, E // 2))
                elif j == 6:
                    block_tiles(range(E // 2, E))
                add(0, 0, j)
            ffn(0, False, 1)
            experts()
            end_phase(dve, 2)

            def combine(b):
                for t in range(b * TB, b * TB + TB):
                    dve.wait_ge(y_fetched[t % TB], 32 * (t // TB + 1))
                    link(V_.tensor_scalar(accM[:, t, :], accM[:, t, :], wgt[:, 0, t:t + 1], None, ALU.mult))
                    V_.scalar_tensor_tensor(out=accM[:, t, :], in0=landing(t), scalar=wgt[:, 1, t:t + 1], in1=accM[:, t, :],
                                            op0=ALU.mult, op1=ALU.add).then_inc(y_summed, 1)

            def part_deviations(b):
                ts = slice(b * TB, b * TB + TB)
                dve.wait_ge(part_squared, b + 1)
                link(V_.tensor_scalar(pv[:, :, ts], ssq[:, 0:2, ts], 1.0 / D, RMS0_EPS, ALU.mult, ALU.add))
                newton(rr[:, :, ts], pv[:, :, ts], psd[:, :, ts], py[:, :, ts], pz[:, :, ts])

            combine(0)
            part_deviations(0)
            combine(1)
            dve.wait_ge(y_summed, 2 * TB)
            dve.wait_ge(post_loaded, 48)

            def parts(t):
                if t >= TB:
                    dve.wait_ge(g_sum, t - TB + 1)
                V_.scalar_tensor_tensor(out=ta[:, t % TB, :], in0=accD[:, t, :], scalar=rr[:, 0, t:t + 1], in1=postB[:, 0, :], op0=ALU.mult, op1=ALU.mult)
                V_.scalar_tensor_tensor(out=tb[:, t % TB, :], in0=accM[:, t, :], scalar=rr[:, 1, t:t + 1], in1=postB[:, 1, :],
                                        op0=ALU.mult, op1=ALU.mult).then_inc(g_parts, 1)

            def final(t):
                V_.scalar_tensor_tensor(out=accD[:, t, :], in0=accD[:, t, :], scalar=a_rs[:, 0, t % TB:t % TB + 1], in1=postB[:, 2, :],
                                        op0=ALU.mult, op1=ALU.mult).then_inc(g_final, 1)

            def add_residual(t):
                dve.wait_ge(xr_loaded[t % TB], 16 * (t // TB + 1))
                dve.wait_ge(g_final, t + 1)
                V_.tensor_tensor(out=x[:, t, :], in0=accD[:, t, :], in1=xr[:, t % TB, :], op=ALU.add).then_inc(g_added, 1)

            def new_stats(t):
                dve.wait_ge(g_added, t + 1)
                V_.bn_stats(a_bst[:, 1, t % TB, :], x[:, t, :])

            def query_cosine(t):
                dve.wait_ge(u_ready, t + 1)
                if t >= 2:
                    dve.wait_ge(q_turned, t - 1)
                V_.tensor_tensor(out=qa[:, t % 2, :], in0=u[:, t % TB, :], in1=wcos[:, t % TB, :], op=ALU.mult).then_inc(qa_ready, 1)

            def query_low(t):
                dve.wait_ge(q_high, t + 1)
                if t >= 2:
                    dve.wait_ge(q_low_stored[t % 2], 16 * (t // 2))
                V_.tensor_tensor(out=tl[:, t % 2, :], in0=ps[:, t % TB, :], in1=th[:, t % 2, :].bitcast(F32), op=ALU.subtract).then_inc(q_low, 1)

            def g_deviations(b):
                kinds = closing_kinds(b)
                if b + 1 < B:
                    dve.wait_ge(sum_squared, (b + 2) * TB)
                if b >= 0:
                    for i in range(TB):
                        last = V_.bn_aggr(a_mv[:, 1, i, :], a_bst[:, 1, i, :])
                    link(last)
                    last = V_.tensor_scalar(a_vv[:, 1, :], a_mv[:, 1, :, 1], 1.0 + RMS1_EPS, RMS1_EPS * LN_EPS, ALU.mult, ALU.add)
                if b + 1 < B:
                    last = V_.tensor_scalar(a_vv[:, 0, :], ssq[:, 2, (b + 1) * TB:(b + 2) * TB], 1.0 / D, RMS0_EPS, ALU.mult, ALU.add)
                link(last)
                newton(a_rs[:, kinds, :], a_vv[:, kinds, :], a_sd[:, kinds, :], a_r0[:, kinds, :], a_r1[:, kinds, :])
                if b >= 0:
                    link(V_.scalar_tensor_tensor(out=a_nmr[:, 1, :], in0=a_mv[:, 1, :, 0], scalar=-1.0, in1=a_rs[:, 1, :], op0=ALU.mult, op1=ALU.mult))
                dve.sem_inc(g_scaled, 1)

            for i in range(TB):
                parts(i)
            part_deviations(1)

            def keys_low(b):
                if b == 0:
                    dve.wait_ge(wo_high, 1)
                    V_.tensor_tensor(out=wol[:, :, :], in0=wo32[:, :, :], in1=woh[:, :, :].bitcast(F32), op=ALU.subtract).then_inc(wo_low, 1)
                dve.wait_ge(k_high, b + 1)
                if b >= 2:
                    dve.wait_ge(k_parts_stored, b - 1)
                V_.tensor_tensor(out=tl[:, b % 2, :], in0=ps[:, b % 2, :], in1=th[:, b % 2, :].bitcast(F32), op=ALU.subtract).then_inc(k_low, 1)

            for b in range(-1, B):
                g_deviations(b)
                if b == 0:
                    dve.wait_ge(b_loaded, 32)
                    dve.wait_ge(k_parts_stored, B)
                for i in range(TB + 2):
                    if b >= 0 and i < TB:
                        query_cosine(b * TB + i)
                    if b + 1 < B and i < TB:
                        final((b + 1) * TB + i)
                    if b >= 0 and i >= 2:
                        query_low(b * TB + i - 2)
                    if b + 2 < B and i < TB:
                        parts((b + 2) * TB + i)
                    if b + 1 < B and i < TB:
                        add_residual((b + 1) * TB + i)
                    if b == -1 and i < TB:
                        keys_low(i)
                    if b == -1 and i == 1:
                        combine(2)
                    if b + 1 < B and 1 <= i <= TB:
                        new_stats((b + 1) * TB + i - 1)
                if b == -1:
                    part_deviations(2)
                    combine(3)
                    part_deviations(3)
                dve.drain()
            end_phase(dve, 3)

            def last_stats(tiles):
                for t in tiles:
                    V_.bn_stats(bst[:, t, :], x[:, t, :])

            def minimum(b, n, hp):
                dve.wait_ge(s_done, count(b, 2 * NU, 2 * n + hp + 1))
                V_.tensor_reduce(mnb[:, n % 2, 2 * hp:2 * hp + 2], ps[:, 2 * hp:2 * hp + 2, 0:(unit(n)[0] + 1) * P], AX.X, ALU.min).then_inc(min_ready, 1)

            def inverse(b, n):
                dve.wait_ge(exp_done, count(b, 2 * NU, 2 * n + 2))
                dve.wait_ge(o_done, count(b, NU, n - 3))
                V_.reciprocal(rcb[:, n % 4, :], smb[:, n % 4, :]).then_inc(recip_done, 1)

            def spread_inverse(b, n):
                dve.wait_ge(recip_done, count(b, NU, n + 1))
                V_.tensor_copy(rE[:, n % 4, :, :], rcb[:, n % 4, :].unsqueeze(2).broadcast_to((P, HG, HD))).then_inc(rinv_ready, 1)

            def normed(b, n):
                qt, g, _ = unit(n)
                if g == 0:
                    dve.wait_ge(attn_low, count(b, TB, n // NG - 1))
                dve.wait_ge(rt_copied, count(b, NU, n + 1))
                V_.tensor_tensor(out=aT[:, qt % 2, g, :], in0=ps[:, 6 + n % 2, 0:P], in1=rT[:, n % 2, :], op=ALU.mult).then_inc(attn_ready, 1)

            def copy_p(b, n, kt, bank):
                dve.wait_ge(p_turned, count(b, PER_SEQ, KEYS.index((n, kt)) + 1))
                dve.wait_ge(pv_done, count(b, PER_SEQ, KEYS.index((n, kt)) - 3))
                V_.tensor_copy(PT[:, KEYS.index((n, kt)) % 4, :], ps[:, bank, :]).then_inc(p_copied_dve, 1)

            def attend(b, steps):
                finished = []
                for i, (kind, n, k) in enumerate(steps):
                    if kind == "scores":
                        minimum(b, n, k)
                        if k == 0:
                            inverse(b, n - 1)
                        else:
                            spread_inverse(b, n - 1)
                        if (n, k) == (NU + 2, 0):
                            dve.wait_ge(pv_done, count(b, PER_SEQ, PER_SEQ))
                            V_.tensor_copy(Vb[:, :, :], V[:, bass.ds(b * TB + TB, TB), :]).then_inc(vb_ready, 1)
                    elif kind == "values":
                        if end_of_unit(n, k):
                            finished.append(n)
                    elif kind == "turn":
                        if steps is LAST and (n, k) == (NU - 1, 0):
                            inverse(b, n)
                            spread_inverse(b, n)
                        if steps is LAST and k == 0 and n < LAG + NT - TB:
                            if n == LAG:
                                dve.wait_ge(proj_added, count(b, TB, 0))
                            last_stats([n - LAG])
                        if k % 2 == 1:
                            copy_p(b, n, k, bank_of(steps, i))
                        while finished:
                            normed(b, finished.pop(0))
                    elif kind == "split":
                        while finished:
                            normed(b, finished.pop(0))
                        dve.wait_ge(attn_high, count(b, TB, n + 1))
                        V_.tensor_tensor(out=aTl[:, n % 2, :, :], in0=aT[:, n % 2, :, :], in1=aTh[:, n % 2, :, :].bitcast(F32),
                                         op=ALU.subtract).then_inc(attn_low, 1)
                    elif kind == "project":
                        dve.wait_ge(proj_done, count(b, TB, n + 1))
                        row = x[:, bass.ds(b * TB + n, 1), :].rearrange("p o d -> p (o d)")
                        V_.tensor_tensor(out=row, in0=row, in1=ps[:, bank_of(steps, i), :], op=ALU.add).then_inc(proj_added, 1)
                        if steps is LAST:
                            dve.wait_ge(proj_added, count(b, TB, n + 1))
                            last_stats([b * TB + n])

            dve.wait_ge(rows_loaded, 16)
            V_.tensor_copy(Vb[:, :, :], V[:, 0:TB, :]).then_inc(vb_ready, 1)
            minimum(0, 0, 0)
            minimum(0, 0, 1)
            attend(0, FIRST)
            with dve.Fori(0, B - 1) as b:
                attend(b, BODY)
            attend(B - 1, LAST)
            end_phase(dve, 4)

            deviations(1.0, LN_EPS)
            last_rows(range(TB))
            for m in range(3):
                split_low(2, TILE0[2], 0, m)
            last_rows(range(TB, 2 * TB))
            hidden(2, 0, 0, None)
            last_rows(range(2 * TB, NT))
            for j in range(2 * B):
                hidden(2, 0, j + 1, next_tile(2, 0, j + 1, True))
                add(2, 0, j)
            ffn(2, True, 1)


def kernel(**inputs):
    import numpy as np
    import concourse.bacc as bacc
    from concourse.bass_utils import run_bass_kernel_spmd

    def a(name):
        return np.asarray(inputs[name])

    def tiles(gate, up, down):
        n = down.shape[0] // P
        cols = [w.reshape(-1, P, n, P).transpose(2, 1, 0, 3).reshape(n, P, 1, -1) for w in (gate, up)]
        return np.concatenate([*cols, down.reshape(n, P, 1, -1)], axis=2)

    we = [a("L0_ffn_we_" + n) for n in ("gate", "up", "down")]
    ffn_w = np.concatenate([
        tiles(a("L0_ffn_w_gate"), a("L0_ffn_w_up"), a("L0_ffn_w_down")),
        tiles(we[0].transpose(1, 0, 2).reshape(512, -1), we[1].transpose(1, 0, 2).reshape(512, -1), we[2].reshape(-1, 512)),
        tiles(a("L1_ffn_w_gate").T, a("L1_ffn_w_up").T, a("L1_ffn_w_down").T)])

    HD, T = 32, 512
    freq = (np.float32(1.0) / np.float32(10000.0) ** (np.arange(0, HD, 2, dtype=np.float32) / np.float32(HD))).astype(np.float32)
    angle = np.outer(np.arange(T, dtype=np.float32), freq).astype(np.float32)
    cos = np.cos(np.concatenate([angle, angle], -1)).astype(np.float32)
    sin = np.concatenate([-np.sin(angle), np.sin(angle)], -1).astype(np.float32)

    def with_halves_swapped(w):
        return np.stack([w, w.reshape(-1, 2, HD // 2)[:, ::-1].reshape(-1)])

    def columns(w):
        return w.reshape(-1, P).T

    arrays = {
        "x": a("x"), "ctx": a("ctx_512"), "ctxT": a("ctx_512").reshape(-1, 128).T, "wkT": a("L0_xattn_W_k").T,
        "bk": a("L0_xattn_b_k"), "gamma": a("L0_xattn_ln_gamma")[None], "beta": a("L0_xattn_ln_beta")[None],
        "ffn_w": ffn_w, "rn_pre": np.stack([columns(a("L0_ffn_rn_pre1")), columns(a("L0_ffn_rn_pre2"))], 1),
        "rn_post": np.stack([a("L0_ffn_rn_post1"), a("L0_ffn_rn_post2"), a("L0_ffn_rn_post")]),
        "router": a("L0_ffn_router_w"), "router_scale": columns(a("L0_ffn_router_scale")), "expert_scale": a("L0_ffn_per_expert_scale")[None],
        "q_w": with_halves_swapped(a("L1_xattn_q_norm_w")), "k_w": with_halves_swapped(a("L1_xattn_k_norm_w")),
        "woT": a("L1_xattn_w_out").T, "cos": cos, "sin": sin,
    }
    nc = bacc.Bacc("TRN2", target_bir_lowering=False, num_devices=1)
    args, given = [], {}
    for name, v in arrays.items():
        v = np.ascontiguousarray(v)
        given[f"in_{name}"] = v
        args.append(nc.dram_tensor(f"in_{name}", v.shape, mybir.dt.from_np(v.dtype), kind="ExternalInput").ap())
    shape = a("x").shape
    out = nc.dram_tensor("out_x", shape, F32, kind="ExternalOutput").ap()
    two_layers(nc, *args, out)
    r = run_bass_kernel_spmd(nc, [given], core_ids=[0])
    return r.results[0]["out_x"]
```
